# Optimizing a Trainium2 kernel written in Bass

```python
import numpy as np
import jax
import jax.numpy as jnp

def _softmax(x, axis=-1):
    return jax.nn.softmax(x, axis=axis)

def _gelu(x):
    return jax.nn.gelu(x, approximate=True)

def _silu(x):
    return jax.nn.silu(x)

def _sigmoid(x):
    return jax.nn.sigmoid(x)

def _layernorm(x, axis=-1, eps=1e-05):
    m = jnp.mean(x, axis=axis, keepdims=True)
    v = jnp.var(x, axis=axis, keepdims=True)
    return (x - m) / jnp.sqrt(v + eps)

def _scatter_add(tgt, idx, src, axis=0):
    return tgt.at[idx].add(src)

def _segment_sum(src, seg, n):
    return jax.ops.segment_sum(src, seg, n)
kernel_name = 'mk_xattn_ffn_d2_seqx_r8_7a3232'

def setup_inputs(seed: int=0):
    np.random.seed(seed)
    _w = jnp.asarray

    def _rec_inputs():
        import jax
        import jax.numpy as jnp
        _rk = jax.random.key(seed)
        x = -0.0002928 + 1 * jax.random.normal(jax.random.fold_in(_rk, 1), (8, 56, 128), jnp.float32)
        _lenS = 56 - jax.random.randint(jax.random.fold_in(_rk, 7), (8,), 0, max(1, 56 // 4) + 1, jnp.int32)
        _lenS2 = 1500 - jax.random.randint(jax.random.fold_in(_rk, 8), (8,), 0, max(1, 1500 // 4) + 1, jnp.int32)
        _ctx_512P = jax.random.normal(jax.random.fold_in(_rk, 11), (8, 16, 64), jnp.float32)
        _ctx_512c = jax.random.dirichlet(jax.random.fold_in(_rk, 511), 0.3 * jnp.ones((16,), jnp.float32), (8, 1500))
        _ctx_512t = jnp.einsum('bsk,bkd->bsd', _ctx_512c, _ctx_512P)
        _ctx_512t = _ctx_512t * jax.lax.rsqrt(jnp.mean(jnp.square(_ctx_512t)) + 1e-12) * 0.953939
        ctx_512 = 0.00222621 + 0.99962 * (_ctx_512t + 0.3 * jax.random.normal(jax.random.fold_in(_rk, 611), (8, 1500, 64), jnp.float32))
        return (x, ctx_512)
    x, ctx_512 = _rec_inputs()

    def _L0_xattn_setup():
        import jax, jax.numpy as jnp
        import numpy as np
        H, D, C1, C2, S, M, B, W = (16, 32, 128, 64, 256, 64, 2, 4)

        def _ln(x, g, b):
            m = jnp.mean(x, -1, keepdims=True)
            v = jnp.var(x, -1, keepdims=True)
            return (x - m) * jax.lax.rsqrt(v + 1e-05) * g + b

        def _mha(x, y, wq, wk, wv, li1_w, li1_b, lnx_g, lnx_b, lny_g, lny_b, ln3_g, ln3_b, li2_w, li2_b, li3_w, li3_b, causal):
            xn = _ln(x, lnx_g, lnx_b)
            yn = _ln(y, lny_g, lny_b)
            q = jnp.einsum('bsc,hcd->bhsd', xn, wq)
            k = jnp.einsum('btc,hcd->bhtd', yn, wk)
            v = jnp.einsum('btc,hcd->bhtd', yn, wv)
            a = jax.nn.softmax(jnp.einsum('bhsd,bhtd->bhst', q, k) * D ** (-0.5), axis=-1)
            if causal:
                s, t = (a.shape[-2], a.shape[-1])
                mask = (jnp.arange(t)[None, :] > jnp.arange(s)[:, None]).astype(a.dtype)
                a = a * mask
            o = jnp.einsum('bhst,bhtd->bhsd', a, v)
            o = o.transpose(0, 2, 1, 3).reshape(x.shape[0], x.shape[1], H * D)
            x_out = x + o @ li1_w + li1_b
            h = jax.nn.gelu(_ln(x_out, ln3_g, ln3_b) @ li2_w + li2_b, approximate=False)
            return x_out + h @ li3_w + li3_b
        key = jax.random.key(seed)
        ks = iter(jax.random.split(key, 64))

        def w(shape, scale=0.02):
            return jax.random.normal(next(ks), shape, jnp.float32) * scale
        inp = {'xx': jax.random.normal(next(ks), (B, S, C1), jnp.float32), 'ee': jax.random.normal(next(ks), (B, M, C2), jnp.float32), 'ln1_g': jnp.ones(C1, jnp.float32), 'ln1_b': jnp.zeros(C1, jnp.float32), 'ln2_g': jnp.ones(C1, jnp.float32), 'ln2_b': jnp.zeros(C1, jnp.float32)}
        for pfx, cy in (('a1', C1), ('a2', C2)):
            inp[pfx + '_wq'] = w((H, C1, D))
            inp[pfx + '_wk'] = w((H, cy, D))
            inp[pfx + '_wv'] = w((H, cy, D))
            inp[pfx + '_li1_w'] = w((H * D, C1))
            inp[pfx + '_li1_b'] = jnp.zeros(C1, jnp.float32)
            inp[pfx + '_lnx_g'] = jnp.ones(C1, jnp.float32)
            inp[pfx + '_lnx_b'] = jnp.zeros(C1, jnp.float32)
            inp[pfx + '_lny_g'] = jnp.ones(cy, jnp.float32)
            inp[pfx + '_lny_b'] = jnp.zeros(cy, jnp.float32)
            inp[pfx + '_ln3_g'] = jnp.ones(C1, jnp.float32)
            inp[pfx + '_ln3_b'] = jnp.zeros(C1, jnp.float32)
            inp[pfx + '_li2_w'] = w((C1, C1 * W))
            inp[pfx + '_li2_b'] = jnp.zeros(C1 * W, jnp.float32)
            inp[pfx + '_li3_w'] = w((C1 * W, C1))
            inp[pfx + '_li3_b'] = jnp.zeros(C1, jnp.float32)
        inp['training'] = 0
        return inp
    _L0_xattn_all = _L0_xattn_setup()
    _L0_xattn_in = {k: v for k, v in _L0_xattn_all.items() if k in ('ln1_g', 'ln1_b', 'ln2_g', 'ln2_b', 'a1_wq', 'a1_wk', 'a1_wv', 'a1_li1_w', 'a1_li1_b', 'a1_lnx_g', 'a1_lnx_b', 'a1_lny_g', 'a1_lny_b', 'a1_ln3_g', 'a1_ln3_b', 'a1_li2_w', 'a1_li2_b', 'a1_li3_w', 'a1_li3_b', 'a2_wq', 'a2_wk', 'a2_wv', 'a2_li1_w', 'a2_li1_b', 'a2_lnx_g', 'a2_lnx_b', 'a2_lny_g', 'a2_lny_b', 'a2_ln3_g', 'a2_ln3_b', 'a2_li2_w', 'a2_li2_b', 'a2_li3_w', 'a2_li3_b')}
    del _L0_xattn_all

    def _L0_ffn_setup():
        import jax, jax.numpy as jnp
        import numpy as np
        HIDDEN = 128
        INTER = 512
        NUM_EXPERTS = 8
        TOP_K = 2
        EPS = 1e-05

        def _layer_norm(x, g, b):
            m = jnp.mean(x, axis=-1, keepdims=True)
            v = jnp.mean(jnp.square(x - m), axis=-1, keepdims=True)
            return (x - m) * jax.lax.rsqrt(v + EPS) * g + b
        key = jax.random.key(seed)
        ks = jax.random.split(key, 8)
        s = 0.02
        return {'x': jax.random.normal(ks[0], (4, 256, HIDDEN), dtype=jnp.float32), 'ln1_g': jnp.ones((HIDDEN,), jnp.float32), 'ln1_b': jnp.zeros((HIDDEN,), jnp.float32), 'attn_w': jax.random.normal(ks[1], (HIDDEN, HIDDEN), jnp.float32) * s, 'ln2_g': jnp.ones((HIDDEN,), jnp.float32), 'ln2_b': jnp.zeros((HIDDEN,), jnp.float32), 'gate_w': jax.random.normal(ks[2], (NUM_EXPERTS, HIDDEN), jnp.float32) * s, 'gate_proj': jax.random.normal(ks[3], (NUM_EXPERTS, INTER, HIDDEN), jnp.float32) * s, 'up_proj': jax.random.normal(ks[4], (NUM_EXPERTS, INTER, HIDDEN), jnp.float32) * s, 'down_proj': jax.random.normal(ks[5], (NUM_EXPERTS, HIDDEN, INTER), jnp.float32) * s}
    _L0_ffn_all = _L0_ffn_setup()
    _L0_ffn_in = {k: v for k, v in _L0_ffn_all.items() if k in ('ln1_g', 'ln1_b', 'attn_w', 'ln2_g', 'ln2_b', 'gate_w', 'gate_proj', 'up_proj', 'down_proj')}
    del _L0_ffn_all

    def _L1_xattn_setup():
        import jax, jax.numpy as jnp
        import numpy as np
        NUM_HEADS = 16
        HEAD_DIM = 64
        Q_DIM = 128
        KV_DIM = 64
        INNER = NUM_HEADS * HEAD_DIM
        key = jax.random.key(seed)
        ks = jax.random.split(key, 7)
        B, N, M = (32, 128, 256)
        q = jax.random.normal(ks[0], (B, N, Q_DIM), dtype=jnp.float32)
        kv = jax.random.normal(ks[1], (B, M, KV_DIM), dtype=jnp.float32)
        Wq = jax.random.normal(ks[2], (Q_DIM, INNER), dtype=jnp.float32) / np.sqrt(Q_DIM)
        Wk = jax.random.normal(ks[3], (KV_DIM, INNER), dtype=jnp.float32) / np.sqrt(KV_DIM)
        Wv = jax.random.normal(ks[4], (KV_DIM, INNER), dtype=jnp.float32) / np.sqrt(KV_DIM)
        Wo = jax.random.normal(ks[5], (INNER, Q_DIM), dtype=jnp.float32) / np.sqrt(INNER)
        bo = jax.random.normal(ks[6], (Q_DIM,), dtype=jnp.float32) * 0.01
        return {'q': q, 'kv': kv, 'Wq': Wq, 'Wk': Wk, 'Wv': Wv, 'Wo': Wo, 'bo': bo}
    _L1_xattn_all = _L1_xattn_setup()
    _L1_xattn_in = {k: v for k, v in _L1_xattn_all.items() if k in ('Wq', 'Wk', 'Wv', 'Wo', 'bo')}
    del _L1_xattn_all

    def _L1_ffn_setup():
        import jax, jax.numpy as jnp
        import numpy as np
        B, T, D, H, E, K = (2, 128, 128, 16, 8, 2)
        HS = D // H
        FF = 4 * D

        def layernorm(x, g, b, eps=1e-05):
            m = jnp.mean(x, axis=-1, keepdims=True)
            v = jnp.mean((x - m) ** 2, axis=-1, keepdims=True)
            return (x - m) * jax.lax.rsqrt(v + eps) * g + b
        key = jax.random.key(seed)
        ks = jax.random.split(key, 10)
        s = 0.02
        return {'x': jax.random.normal(ks[0], (B, T, D), jnp.float32), 'Wq': jax.random.normal(ks[1], (H, D, HS), jnp.float32) * s, 'Wk': jax.random.normal(ks[2], (H, D, HS), jnp.float32) * s, 'Wv': jax.random.normal(ks[3], (H, D, HS), jnp.float32) * s, 'gate_W': jax.random.normal(ks[4], (D, E), jnp.float32) * s, 'W1': jax.random.normal(ks[5], (E, D, FF), jnp.float32) * s, 'b1': jnp.zeros((E, FF), jnp.float32), 'W2': jax.random.normal(ks[6], (E, FF, D), jnp.float32) * s, 'b2': jnp.zeros((E, D), jnp.float32), 'ln1_g': jnp.ones((D,), jnp.float32), 'ln1_b': jnp.zeros((D,), jnp.float32), 'ln2_g': jnp.ones((D,), jnp.float32), 'ln2_b': jnp.zeros((D,), jnp.float32)}
    _L1_ffn_all = _L1_ffn_setup()
    _L1_ffn_in = {k: v for k, v in _L1_ffn_all.items() if k in ('Wq', 'Wk', 'Wv', 'gate_W', 'W1', 'b1', 'W2', 'b2', 'ln1_g', 'ln1_b', 'ln2_g', 'ln2_b')}
    del _L1_ffn_all
    return {'x': x, 'ctx_512': ctx_512, 'L0_xattn_ln1_g': _L0_xattn_in['ln1_g'], 'L0_xattn_ln1_b': _L0_xattn_in['ln1_b'], 'L0_xattn_ln2_g': _L0_xattn_in['ln2_g'], 'L0_xattn_ln2_b': _L0_xattn_in['ln2_b'], 'L0_xattn_a1_wq': _L0_xattn_in['a1_wq'], 'L0_xattn_a1_wk': _L0_xattn_in['a1_wk'], 'L0_xattn_a1_wv': _L0_xattn_in['a1_wv'], 'L0_xattn_a1_li1_w': _L0_xattn_in['a1_li1_w'], 'L0_xattn_a1_li1_b': _L0_xattn_in['a1_li1_b'], 'L0_xattn_a1_lnx_g': _L0_xattn_in['a1_lnx_g'], 'L0_xattn_a1_lnx_b': _L0_xattn_in['a1_lnx_b'], 'L0_xattn_a1_lny_g': _L0_xattn_in['a1_lny_g'], 'L0_xattn_a1_lny_b': _L0_xattn_in['a1_lny_b'], 'L0_xattn_a1_ln3_g': _L0_xattn_in['a1_ln3_g'], 'L0_xattn_a1_ln3_b': _L0_xattn_in['a1_ln3_b'], 'L0_xattn_a1_li2_w': _L0_xattn_in['a1_li2_w'], 'L0_xattn_a1_li2_b': _L0_xattn_in['a1_li2_b'], 'L0_xattn_a1_li3_w': _L0_xattn_in['a1_li3_w'], 'L0_xattn_a1_li3_b': _L0_xattn_in['a1_li3_b'], 'L0_xattn_a2_wq': _L0_xattn_in['a2_wq'], 'L0_xattn_a2_wk': _L0_xattn_in['a2_wk'], 'L0_xattn_a2_wv': _L0_xattn_in['a2_wv'], 'L0_xattn_a2_li1_w': _L0_xattn_in['a2_li1_w'], 'L0_xattn_a2_li1_b': _L0_xattn_in['a2_li1_b'], 'L0_xattn_a2_lnx_g': _L0_xattn_in['a2_lnx_g'], 'L0_xattn_a2_lnx_b': _L0_xattn_in['a2_lnx_b'], 'L0_xattn_a2_lny_g': _L0_xattn_in['a2_lny_g'], 'L0_xattn_a2_lny_b': _L0_xattn_in['a2_lny_b'], 'L0_xattn_a2_ln3_g': _L0_xattn_in['a2_ln3_g'], 'L0_xattn_a2_ln3_b': _L0_xattn_in['a2_ln3_b'], 'L0_xattn_a2_li2_w': _L0_xattn_in['a2_li2_w'], 'L0_xattn_a2_li2_b': _L0_xattn_in['a2_li2_b'], 'L0_xattn_a2_li3_w': _L0_xattn_in['a2_li3_w'], 'L0_xattn_a2_li3_b': _L0_xattn_in['a2_li3_b'], 'L0_ffn_ln1_g': _L0_ffn_in['ln1_g'], 'L0_ffn_ln1_b': _L0_ffn_in['ln1_b'], 'L0_ffn_attn_w': _L0_ffn_in['attn_w'], 'L0_ffn_ln2_g': _L0_ffn_in['ln2_g'], 'L0_ffn_ln2_b': _L0_ffn_in['ln2_b'], 'L0_ffn_gate_w': _L0_ffn_in['gate_w'], 'L0_ffn_gate_proj': _L0_ffn_in['gate_proj'], 'L0_ffn_up_proj': _L0_ffn_in['up_proj'], 'L0_ffn_down_proj': _L0_ffn_in['down_proj'], 'L1_xattn_Wq': _L1_xattn_in['Wq'], 'L1_xattn_Wk': _L1_xattn_in['Wk'], 'L1_xattn_Wv': _L1_xattn_in['Wv'], 'L1_xattn_Wo': _L1_xattn_in['Wo'], 'L1_xattn_bo': _L1_xattn_in['bo'], 'L1_ffn_Wq': _L1_ffn_in['Wq'], 'L1_ffn_Wk': _L1_ffn_in['Wk'], 'L1_ffn_Wv': _L1_ffn_in['Wv'], 'L1_ffn_gate_W': _L1_ffn_in['gate_W'], 'L1_ffn_W1': _L1_ffn_in['W1'], 'L1_ffn_b1': _L1_ffn_in['b1'], 'L1_ffn_W2': _L1_ffn_in['W2'], 'L1_ffn_b2': _L1_ffn_in['b2'], 'L1_ffn_ln1_g': _L1_ffn_in['ln1_g'], 'L1_ffn_ln1_b': _L1_ffn_in['ln1_b'], 'L1_ffn_ln2_g': _L1_ffn_in['ln2_g'], 'L1_ffn_ln2_b': _L1_ffn_in['ln2_b']}

def reference(x, ctx_512, L0_xattn_ln1_g, L0_xattn_ln1_b, L0_xattn_ln2_g, L0_xattn_ln2_b, L0_xattn_a1_wq, L0_xattn_a1_wk, L0_xattn_a1_wv, L0_xattn_a1_li1_w, L0_xattn_a1_li1_b, L0_xattn_a1_lnx_g, L0_xattn_a1_lnx_b, L0_xattn_a1_lny_g, L0_xattn_a1_lny_b, L0_xattn_a1_ln3_g, L0_xattn_a1_ln3_b, L0_xattn_a1_li2_w, L0_xattn_a1_li2_b, L0_xattn_a1_li3_w, L0_xattn_a1_li3_b, L0_xattn_a2_wq, L0_xattn_a2_wk, L0_xattn_a2_wv, L0_xattn_a2_li1_w, L0_xattn_a2_li1_b, L0_xattn_a2_lnx_g, L0_xattn_a2_lnx_b, L0_xattn_a2_lny_g, L0_xattn_a2_lny_b, L0_xattn_a2_ln3_g, L0_xattn_a2_ln3_b, L0_xattn_a2_li2_w, L0_xattn_a2_li2_b, L0_xattn_a2_li3_w, L0_xattn_a2_li3_b, L0_ffn_ln1_g, L0_ffn_ln1_b, L0_ffn_attn_w, L0_ffn_ln2_g, L0_ffn_ln2_b, L0_ffn_gate_w, L0_ffn_gate_proj, L0_ffn_up_proj, L0_ffn_down_proj, L1_xattn_Wq, L1_xattn_Wk, L1_xattn_Wv, L1_xattn_Wo, L1_xattn_bo, L1_ffn_Wq, L1_ffn_Wk, L1_ffn_Wv, L1_ffn_gate_W, L1_ffn_W1, L1_ffn_b1, L1_ffn_W2, L1_ffn_b2, L1_ffn_ln1_g, L1_ffn_ln1_b, L1_ffn_ln2_g, L1_ffn_ln2_b):
    import jax
    import jax.numpy as jnp

    def _L0_xattn_ref(xx, ee, ln1_g, ln1_b, ln2_g, ln2_b, a1_wq, a1_wk, a1_wv, a1_li1_w, a1_li1_b, a1_lnx_g, a1_lnx_b, a1_lny_g, a1_lny_b, a1_ln3_g, a1_ln3_b, a1_li2_w, a1_li2_b, a1_li3_w, a1_li3_b, a2_wq, a2_wk, a2_wv, a2_li1_w, a2_li1_b, a2_lnx_g, a2_lnx_b, a2_lny_g, a2_lny_b, a2_ln3_g, a2_ln3_b, a2_li2_w, a2_li2_b, a2_li3_w, a2_li3_b, training):
        import jax, jax.numpy as jnp
        import numpy as np
        H, D, C1, C2, S, M, B, W = (16, 32, 128, 64, 256, 64, 2, 4)

        def _ln(x, g, b):
            m = jnp.mean(x, -1, keepdims=True)
            v = jnp.var(x, -1, keepdims=True)
            return (x - m) * jax.lax.rsqrt(v + 1e-05) * g + b

        def _mha(x, y, wq, wk, wv, li1_w, li1_b, lnx_g, lnx_b, lny_g, lny_b, ln3_g, ln3_b, li2_w, li2_b, li3_w, li3_b, causal):
            xn = _ln(x, lnx_g, lnx_b)
            yn = _ln(y, lny_g, lny_b)
            q = jnp.einsum('bsc,hcd->bhsd', xn, wq)
            k = jnp.einsum('btc,hcd->bhtd', yn, wk)
            v = jnp.einsum('btc,hcd->bhtd', yn, wv)
            a = jax.nn.softmax(jnp.einsum('bhsd,bhtd->bhst', q, k) * D ** (-0.5), axis=-1)
            if causal:
                s, t = (a.shape[-2], a.shape[-1])
                mask = (jnp.arange(t)[None, :] > jnp.arange(s)[:, None]).astype(a.dtype)
                a = a * mask
            o = jnp.einsum('bhst,bhtd->bhsd', a, v)
            o = o.transpose(0, 2, 1, 3).reshape(x.shape[0], x.shape[1], H * D)
            x_out = x + o @ li1_w + li1_b
            h = jax.nn.gelu(_ln(x_out, ln3_g, ln3_b) @ li2_w + li2_b, approximate=False)
            return x_out + h @ li3_w + li3_b
        x = _ln(xx, ln1_g, ln1_b)
        x = x + _mha(x, x, a1_wq, a1_wk, a1_wv, a1_li1_w, a1_li1_b, a1_lnx_g, a1_lnx_b, a1_lny_g, a1_lny_b, a1_ln3_g, a1_ln3_b, a1_li2_w, a1_li2_b, a1_li3_w, a1_li3_b, causal=True)
        x = _ln(x, ln2_g, ln2_b)
        return x + _mha(x, ee, a2_wq, a2_wk, a2_wv, a2_li1_w, a2_li1_b, a2_lnx_g, a2_lnx_b, a2_lny_g, a2_lny_b, a2_ln3_g, a2_ln3_b, a2_li2_w, a2_li2_b, a2_li3_w, a2_li3_b, causal=False)

    def _L0_ffn_ref(x, ln1_g, ln1_b, attn_w, ln2_g, ln2_b, gate_w, gate_proj, up_proj, down_proj):
        import jax, jax.numpy as jnp
        import numpy as np
        HIDDEN = 128
        INTER = 512
        NUM_EXPERTS = 8
        TOP_K = 2
        EPS = 1e-05

        def _layer_norm(x, g, b):
            m = jnp.mean(x, axis=-1, keepdims=True)
            v = jnp.mean(jnp.square(x - m), axis=-1, keepdims=True)
            return (x - m) * jax.lax.rsqrt(v + EPS) * g + b
        B, S, H = x.shape
        h = x + jnp.einsum('bsh,oh->bso', _layer_norm(x, ln1_g, ln1_b), attn_w)
        t = _layer_norm(h, ln2_g, ln2_b).reshape(-1, H)
        T = t.shape[0]
        logits = jnp.einsum('th,eh->te', t, gate_w)
        top_vals, top_idx = jax.lax.top_k(logits, TOP_K)
        rw = jax.nn.softmax(top_vals, axis=-1)
        comb = jnp.zeros((T, NUM_EXPERTS), dtype=t.dtype)
        comb = comb.at[jnp.arange(T)[:, None], top_idx].add(rw)
        out = jnp.zeros_like(t)
        for e in range(NUM_EXPERTS):
            g = jnp.einsum('th,ih->ti', t, gate_proj[e])
            u = jnp.einsum('th,ih->ti', t, up_proj[e])
            oe = jnp.einsum('ti,hi->th', jax.nn.silu(g) * u, down_proj[e])
            out = out + comb[:, e:e + 1] * oe
        return h + out.reshape(B, S, H)

    def _L1_xattn_ref(q, kv, Wq, Wk, Wv, Wo, bo):
        import jax, jax.numpy as jnp
        import numpy as np
        NUM_HEADS = 16
        HEAD_DIM = 64
        Q_DIM = 128
        KV_DIM = 64
        INNER = NUM_HEADS * HEAD_DIM
        B, N, _ = q.shape
        M = kv.shape[1]
        scale = HEAD_DIM ** (-0.5)
        qh = (q @ Wq).reshape(B, N, NUM_HEADS, HEAD_DIM).transpose(0, 2, 1, 3)
        kh = (kv @ Wk).reshape(B, M, NUM_HEADS, HEAD_DIM).transpose(0, 2, 1, 3)
        vh = (kv @ Wv).reshape(B, M, NUM_HEADS, HEAD_DIM).transpose(0, 2, 1, 3)
        scores = jnp.einsum('bhnd,bhmd->bhnm', qh, kh) * scale
        attn = jax.nn.softmax(scores, axis=-1)
        out = jnp.einsum('bhnm,bhmd->bhnd', attn, vh)
        out = out.transpose(0, 2, 1, 3).reshape(B, N, INNER)
        return out @ Wo + bo

    def _L1_ffn_ref(x, Wq, Wk, Wv, gate_W, W1, b1, W2, b2, ln1_g, ln1_b, ln2_g, ln2_b):
        import jax, jax.numpy as jnp
        import numpy as np
        B, T, D, H, E, K = (2, 128, 128, 16, 8, 2)
        HS = D // H
        FF = 4 * D

        def layernorm(x, g, b, eps=1e-05):
            m = jnp.mean(x, axis=-1, keepdims=True)
            v = jnp.mean((x - m) ** 2, axis=-1, keepdims=True)
            return (x - m) * jax.lax.rsqrt(v + eps) * g + b
        b, t, d = x.shape
        q = jnp.einsum('btd,hdf->bhtf', x, Wq)
        k = jnp.einsum('btd,hdf->bhtf', x, Wk)
        v = jnp.einsum('btd,hdf->bhtf', x, Wv)
        wei = jnp.einsum('bhtf,bhsf->bhts', q, k) * d ** (-0.5)
        mask = jnp.tril(jnp.ones((t, t), bool))
        wei = jnp.where(mask, wei, -jnp.inf)
        wei = jax.nn.softmax(wei, axis=-1)
        attn = jnp.einsum('bhts,bhsf->bhtf', wei, v)
        attn = attn.transpose(0, 2, 1, 3).reshape(b, t, d)
        y = x + layernorm(attn, ln1_g, ln1_b)
        flat = y.reshape(-1, d)
        logits = flat @ gate_W
        topv, topi = jax.lax.top_k(logits, K)
        w = jax.nn.softmax(topv, axis=-1)
        combine = jnp.sum(jax.nn.one_hot(topi, E, dtype=flat.dtype) * w[..., None], axis=1)
        h = jax.nn.relu(jnp.einsum('nd,edf->enf', flat, W1) + b1[:, None, :])
        eo = jnp.einsum('enf,efd->end', h, W2) + b2[:, None, :]
        moe = jnp.einsum('ne,end->nd', combine, eo)
        out = y + layernorm(moe.reshape(b, t, d), ln2_g, ln2_b)
        return out
    x = x + _L0_xattn_ref(_layernorm(x, axis=-1), ctx_512, L0_xattn_ln1_g, L0_xattn_ln1_b, L0_xattn_ln2_g, L0_xattn_ln2_b, L0_xattn_a1_wq, L0_xattn_a1_wk, L0_xattn_a1_wv, L0_xattn_a1_li1_w, L0_xattn_a1_li1_b, L0_xattn_a1_lnx_g, L0_xattn_a1_lnx_b, L0_xattn_a1_lny_g, L0_xattn_a1_lny_b, L0_xattn_a1_ln3_g, L0_xattn_a1_ln3_b, L0_xattn_a1_li2_w, L0_xattn_a1_li2_b, L0_xattn_a1_li3_w, L0_xattn_a1_li3_b, L0_xattn_a2_wq, L0_xattn_a2_wk, L0_xattn_a2_wv, L0_xattn_a2_li1_w, L0_xattn_a2_li1_b, L0_xattn_a2_lnx_g, L0_xattn_a2_lnx_b, L0_xattn_a2_lny_g, L0_xattn_a2_lny_b, L0_xattn_a2_ln3_g, L0_xattn_a2_ln3_b, L0_xattn_a2_li2_w, L0_xattn_a2_li2_b, L0_xattn_a2_li3_w, L0_xattn_a2_li3_b, 0)
    x = x + _L0_ffn_ref(_layernorm(x, axis=-1), L0_ffn_ln1_g, L0_ffn_ln1_b, L0_ffn_attn_w, L0_ffn_ln2_g, L0_ffn_ln2_b, L0_ffn_gate_w, L0_ffn_gate_proj, L0_ffn_up_proj, L0_ffn_down_proj)
    x = x + _L1_xattn_ref(_layernorm(x, axis=-1), ctx_512, L1_xattn_Wq, L1_xattn_Wk, L1_xattn_Wv, L1_xattn_Wo, L1_xattn_bo)
    x = x + _L1_ffn_ref(_layernorm(x, axis=-1), L1_ffn_Wq, L1_ffn_Wk, L1_ffn_Wv, L1_ffn_gate_W, L1_ffn_W1, L1_ffn_b1, L1_ffn_W2, L1_ffn_b2, L1_ffn_ln1_g, L1_ffn_ln1_b, L1_ffn_ln2_g, L1_ffn_ln2_b)
    return x

_drawn_inputs = setup_inputs


def setup_inputs(seed=0):
    import zlib

    import numpy as np

    out = dict(_drawn_inputs(seed))
    spreads = {'L0_xattn_ln1_g': (1.0, 0.2),
     'L0_xattn_ln1_b': (0.0, 0.1),
     'L0_xattn_ln2_g': (1.0, 0.2),
     'L0_xattn_ln2_b': (0.0, 0.1),
     'L0_xattn_a1_li1_b': (0.0, 0.1),
     'L0_xattn_a1_lnx_g': (1.0, 0.6),
     'L0_xattn_a1_lnx_b': (0.0, 0.8),
     'L0_xattn_a1_lny_g': (1.0, 0.6),
     'L0_xattn_a1_lny_b': (0.0, 0.627),
     'L0_xattn_a1_ln3_g': (1.0, 0.6),
     'L0_xattn_a1_ln3_b': (0.0, 0.8),
     'L0_xattn_a1_li2_b': (0.0, 0.344),
     'L0_xattn_a1_li3_b': (0.0, 0.1),
     'L0_xattn_a2_li1_b': (0.0, 0.1),
     'L0_xattn_a2_lnx_g': (1.0, 0.6),
     'L0_xattn_a2_lnx_b': (0.0, 0.8),
     'L0_xattn_a2_lny_g': (1.0, 0.6),
     'L0_xattn_a2_lny_b': (0.0, 2.0),
     'L0_xattn_a2_ln3_g': (1.0, 0.6),
     'L0_xattn_a2_ln3_b': (0.0, 0.698),
     'L0_xattn_a2_li2_b': (0.0, 0.31),
     'L0_xattn_a2_li3_b': (0.0, 0.1),
     'L0_ffn_ln1_g': (1.0, 0.535),
     'L0_ffn_ln1_b': (0.0, 0.1),
     'L0_ffn_ln2_g': (1.0, 0.6),
     'L0_ffn_ln2_b': (0.0, 0.8),
     'L1_ffn_b1': (0.0, 0.508),
     'L1_ffn_b2': (0.0, 0.1),
     'L1_ffn_ln1_g': (1.0, 0.2),
     'L1_ffn_ln1_b': (0.0, 0.405),
     'L1_ffn_ln2_g': (1.0, 0.6),
     'L1_ffn_ln2_b': (0.0, 0.392)}
    factors = {'L0_xattn_a1_wq': 8.0,
     'L0_xattn_a1_wk': 8.0,
     'L0_xattn_a1_wv': 3.963,
     'L0_xattn_a1_li1_w': 2.757,
     'L0_xattn_a2_wq': 8.0,
     'L0_xattn_a2_wk': 8.0,
     'L0_ffn_gate_w': 8.0,
     'L0_ffn_gate_proj': 6.069,
     'L0_ffn_up_proj': 8.0,
     'L0_ffn_down_proj': 8.0,
     'L1_xattn_bo': 33.496,
     'L1_ffn_Wq': 6.743,
     'L1_ffn_Wk': 7.46,
     'L1_xattn_Wq': 3.15,
     'L1_xattn_Wk': 2.999}
    for name, (base, spread) in spreads.items():
        noise = np.random.default_rng([zlib.crc32(name.encode()), seed]).standard_normal(out[name].shape)
        drawn = base * np.exp(spread * noise) if base else spread * noise
        out[name] = jnp.asarray(drawn.astype(out[name].dtype))
    for name, factor in factors.items():
        out[name] = (out[name] * factor).astype(out[name].dtype)
    return out
```

```python
import concourse.bass as bass
import concourse.mybir as mybir
from contextlib import ExitStack

BATCH, SEQ, C = 8, 56, 128
KEYS, CTX = 1500, 64
HEADS = 16
TILES = 4
TP = BATCH * SEQ // TILES
TOK = BATCH * SEQ
KT = 12
KP = KEYS // KT
HQ = HEADS * SEQ
HQ_TILES = HQ // 128
HALF = HQ // 2
FF = 512
FCH = FF // 128
EXPERTS = 8
EPS = 1e-5
NEG = -1e30
SPAN = 500
SPANS = KEYS // SPAN

ROWS = ["L0_xattn_ln1_g", "L0_xattn_ln1_b", "L0_xattn_a1_li1_b", "L0_xattn_a1_li3_b",
        "L0_xattn_ln2_g", "L0_xattn_ln2_b", "L0_xattn_a2_li1_b", "L0_xattn_a2_li3_b",
        "L1_xattn_bo", "L1_ffn_ln1_g", "L1_ffn_ln1_b", "L1_ffn_ln2_g", "L1_ffn_ln2_b"]
COLS = ["L0_xattn_a1_lnx_g", "L0_xattn_a1_lnx_b", "L0_xattn_a1_lny_g", "L0_xattn_a1_lny_b",
        "L0_xattn_a1_ln3_g", "L0_xattn_a1_ln3_b",
        "L0_xattn_a2_lnx_g", "L0_xattn_a2_lnx_b", "L0_xattn_a2_lny_g", "L0_xattn_a2_lny_b",
        "L0_xattn_a2_ln3_g", "L0_xattn_a2_ln3_b",
        "L0_ffn_ln1_g", "L0_ffn_ln1_b", "L0_ffn_ln2_g", "L0_ffn_ln2_b"]
COL_A1_LI2 = len(COLS)
COL_A2_LI2 = COL_A1_LI2 + FCH
COL_B1 = COL_A2_LI2 + FCH
NCOLS = COL_B1 + EXPERTS * FCH


class Count:

    def __init__(self):
        self.n = 0

    def up(self, k=1):
        self.n += k
        return self.n


def build_program(nc, d, out):
    f32, f32r, i32 = mybir.dt.float32, mybir.dt.float32r, mybir.dt.int32
    ALU, ACT, AX = mybir.AluOpType, mybir.ActivationFunctionType, mybir.AxisListType

    with ExitStack() as ctx:
        def sb(name, shape, dt=f32):
            return ctx.enter_context(nc.sbuf_tensor(name, shape, dt))

        def sem(name):
            return ctx.enter_context(nc.semaphore(name))

        PS = ctx.enter_context(nc.psum_tensor("PS", [128, 8, 512], f32))

        ident = sb("ident", [128, 128])
        ones = sb("ones", [128, 1])
        mask_blocks = sb("mask_blocks", [TP, TP])
        mask_later = sb("mask_later", [TP, TP])
        mask_causal = sb("mask_causal", [TP, TP])
        heads4 = sb("heads4", [128, 4])
        heads16 = sb("heads16", [128, 16])
        rows = sb("rows", [TP, len(ROWS), C])
        cols = sb("cols", [128, NCOLS])

        x_in = sb("x_in", [TP, TILES, C])
        hat = sb("hat", [TP, TILES, C])
        ta = sb("ta", [TP, TILES, C])
        tb = sb("tb", [TP, TILES, C])
        tc_ = sb("tc_", [TP, TILES, C])
        stats = sb("stats", [TP, TILES, 6])
        mv = sb("mv", [TP, TILES, 2])
        rs = sb("rs", [TP, 4, TILES])
        xn = sb("xn", [128, TOK])
        yn = sb("yn", [128, TOK])
        big1 = sb("big1", [128, 8, TOK])
        big2 = sb("big2", [128, 4, TOK])
        wA = sb("wA", [128, 6 * 512])
        wq2 = sb("wq2", [128, 512])
        li2x = sb("li2x", [128, 3 * 512])
        wkpad = sb("wkpad", [128, HEADS, 128])
        wvpad = sb("wvpad", [128, HEADS, 128])
        attn_w = sb("attn_w", [128, C])
        gate0 = sb("gate0", [128, EXPERTS])
        gate1 = sb("gate1", [128, EXPERTS])
        b2 = sb("b2", [EXPERTS, C])
        we = sb("we", [128, 2, 3 * 512])
        lg = sb("lg", [TP, TILES, EXPERTS])
        top = sb("top", [TP, TILES, 8])
        gt = sb("gt", [TP, 4, TILES, EXPERTS])
        comb = sb("comb", [TP, EXPERTS, TILES])
        cw = sb("cw", [TP, 2, TILES])
        gs = sb("gs", [TP, TILES])
        combT = sb("combT", [EXPERTS, TOK])
        qp = sb("qp", [128, BATCH, HEADS, SEQ])
        cmean = sb("cmean", [KP, BATCH * KT])
        crstd = sb("crstd", [KP, BATCH * KT])
        cst = sb("cst", [KP, KT, 6])
        ctmp = sb("ctmp", [KP, 2, BATCH * KT])
        CT = sb("CT", [KP, KT, CTX])
        kA = sb("kA", [128, 2, KEYS], f32r)
        kB = sb("kB", [128, 2, KEYS], f32r)
        qA = sb("qA", [128, 2, HQ], f32r)
        qB = sb("qB", [128, 2, HQ], f32r)
        mx = sb("mx", [128, HQ_TILES, SPANS])
        negm = sb("negm", [128, HQ_TILES])
        mhr = sb("mhr", [128, HQ_TILES], f32r)
        mhl = sb("mhl", [128, HQ_TILES, 2])
        rden = sb("rden", [64, HQ])
        arena = sb("arena", [128, 9344])

        def part(off, n):
            return arena[:, off:off + n]

        XX = part(0, KT * 128).rearrange("p (k n) -> p k n", k=KT)[0:KP]
        Y = part(1536, KEYS)
        V = part(3072, 2 * KT * 128).rearrange("p (b k n) -> p b k n", b=2, k=KT)[0:KP]
        P = part(6144, 3 * HQ).rearrange("p (b n) -> p b n", b=3)[0:KP]
        S = part(0, 2 * 16 * TP).rearrange("p (b h k) -> p b h k", b=2, h=16)[0:TP]
        Kblk = part(3584, 16 * TP).rearrange("p (c h k) -> p c h k", c=4, h=4)
        PT = part(5376, 2 * 4 * TP).rearrange("p (b h q) -> p b h q", b=2, h=4)[0:TP]
        VT = part(6272, TILES * 512).rearrange("p (t n) -> p t n", t=TILES)[0:TP]
        OT = part(8320, 2 * 512).rearrange("p (b n) -> p b n", b=2)[0:TP]
        rsum = sb("rsum", [TP, 2, 16])
        rneg = sb("rneg", [TP, 2, 16])
        act = part(0, 2 * FCH * TOK).rearrange("p (b c n) -> p b c n", b=2, c=FCH)
        sg = part(3584, 2 * TOK).rearrange("p (b n) -> p b n", b=2)

        craw = qp[:, :, :, :].rearrange("p b h q -> p (b h q)")[0:KP, 0:BATCH * KT * CTX] \
            .rearrange("p (t c) -> p t c", c=CTX)

        w_q1, w_k1, w_v1 = wA[:, 0:512], wA[:, 512:1024], wA[:, 1024:1536]
        w_a1 = [wA[:, 1536:2048], wA[:, 2048:2560], wA[:, 2560:3072]]
        w_a2 = [li2x[:, 0:512], li2x[:, 512:1024], li2x[:, 1024:1536]]
        w_qL1 = wA[:, 0:1024]
        w_oL1 = wA[:, 1024:2048].rearrange("p (c n) -> p c n", c=8)
        w_qkvL1 = wA[:, 2048:2048 + 3 * C].rearrange("p (j n) -> p j n", j=3)

        x_loaded = sem("x_loaded")
        params_loaded = sem("params_loaded")
        wA_loaded = sem("wA_loaded")
        wB_loaded = sem("wB_loaded")
        craw_loaded = sem("craw_loaded")
        wL1_loaded = sem("wL1_loaded")
        pads_loaded = sem("pads_loaded")
        expert_loaded = [sem("expert_loaded_0"), sem("expert_loaded_1")]
        ct_loaded = sem("ct_loaded")
        y_loaded = sem("y_loaded")
        v_loaded = [sem("v_loaded_0"), sem("v_loaded_1")]
        out_stored = sem("out_stored")
        consts_step = sem("consts_step")
        dve_step = sem("dve_step")
        act_step = sem("act_step")
        pads_zeroed = sem("pads_zeroed")
        stats_ready = sem("stats_ready")
        tm_ready = sem("tm_ready")
        fmT_ps = sem("fmT_ps")
        fm_ready = sem("fm_ready")
        lin_ps = sem("lin_ps")
        lin_moved = sem("lin_moved")
        proj_ps = sem("proj_ps")
        kblk_ready = sem("kblk_ready")
        s_ps = sem("s_ps")
        s_read = sem("s_read")
        s_shifted = sem("s_shifted")
        exp_done = sem("exp_done")
        sum_done = sem("sum_done")
        masked = sem("masked")
        pt_ps = sem("pt_ps")
        pt_moved = sem("pt_moved")
        o_sa_ps = sem("o_sa_ps")
        o_sa_ready = sem("o_sa_ready")
        oT_ps = sem("oT_ps")
        oT_moved = sem("oT_moved")
        gate_in = sem("gate_in")
        gate_exp = sem("gate_exp")
        comb_ready = sem("comb_ready")
        combT_ps = sem("combT_ps")
        combT_ready = sem("combT_ready")
        g_ps = sem("g_ps")
        g_moved = sem("g_moved")
        mul_done = sem("mul_done")
        dn_ps = sem("dn_ps")
        dn_added = sem("dn_added")
        xx_ready = sem("xx_ready")
        xxT_ps = sem("xxT_ps")
        y_ready = sem("y_ready")
        kab_ready = sem("kab_ready")
        v_ready = sem("v_ready")
        qs_ready = sem("qs_ready")
        sc_ps = sem("sc_ps")
        sc_max = sem("sc_max")
        negm_ready = sem("negm_ready")
        mrow_ps = sem("mrow_ps")
        mrow_moved = sem("mrow_moved")
        st_ps = sem("st_ps")
        p_ready = sem("p_ready")
        pv_done = sem("pv_done")
        o_moved = sem("o_moved")
        u_ready = sem("u_ready")

        block = ctx.enter_context(nc.Block())

        LIN_PREP0 = 12 + 4
        LIN_U0 = LIN_PREP0 + 4 + HEADS
        LIN_PREP1 = LIN_U0 + 4 + 4
        LIN_U1 = LIN_PREP1 + 8 + HEADS

        def row(name, t=TILES):
            v = rows[:, ROWS.index(name):ROWS.index(name) + 1, :]
            return v.broadcast_to([TP, t, C])

        def col(name):
            return cols[:, COLS.index(name):COLS.index(name) + 1]

        def static_and_loop(engine, step, last):
            step(0, 0, True)
            with engine.Fori(0, (last - 1) // 2) as i:
                step(2 * i + 1, 1, True)
                step(2 * i + 2, 0, True)
            step(last, last % 2, False)

        @block.sync
        def _(sp):
            sp.dma_start(x_in[:, :, :], d["x"].rearrange("(t p) c -> p t c", p=TP)).then_inc(x_loaded, 16)
            sp.dma_start(rows[:, :, :], d["rows"].partition_broadcast(TP)).then_inc(params_loaded, 16)
            sp.dma_start(cols[:, :], d["cols"]).then_inc(params_loaded, 16)
            for dst, name in ((w_q1, "a1_wq"), (w_k1, "a1_wk"), (w_v1, "a1_wv"), (w_a1[1], "a1_li2")):
                sp.dma_start(dst, d[name]).then_inc(wA_loaded, 16)
            for dst, name in ((w_a1[0], "a1_li1"), (w_a1[2], "a1_li3")):
                sp.dma_start(dst.rearrange("p (c n) -> p c n", c=4),
                             d[name].rearrange("(c p) n -> p c n", p=128)).then_inc(wA_loaded, 16)
            sp.dma_start(craw, d["ctx"].rearrange("b (p k) c -> p b k c", p=KP)).then_inc(craw_loaded, 16)
            sp.dma_start(wq2[:, :], d["a2_wq"]).then_inc(wB_loaded, 16)
            sp.dma_start(w_a2[1], d["a2_li2"]).then_inc(wB_loaded, 16)
            for dst, name in ((w_a2[0], "a2_li1"), (w_a2[2], "a2_li3")):
                sp.dma_start(dst.rearrange("p (c n) -> p c n", c=4),
                             d[name].rearrange("(c p) n -> p c n", p=128)).then_inc(wB_loaded, 16)
            sp.dma_start(attn_w[:, :], d["attn_w"]).then_inc(wB_loaded, 16)
            sp.dma_start(gate0[:, :], d["gate0"]).then_inc(wB_loaded, 16)
            sp.dma_start(gate1[:, :], d["gate1"]).then_inc(wB_loaded, 16)
            sp.dma_start(b2[:, :], d["b2"]).then_inc(wB_loaded, 16)

            def load_pads(call, D, wk, wv):
                per = 128 // D
                sp.wait_ge(pads_zeroed, 2 * (call + 1))
                for r in range(per):
                    src = wk[r:HEADS:per].rearrange("g d c -> d g c")
                    dst = wkpad[r * D:(r + 1) * D, r:HEADS:per, :]
                    for j in range(2):
                        sp.dma_start(dst[:, :, j * CTX:(j + 1) * CTX], src).then_inc(pads_loaded, 16)
                    src = wv[r:HEADS:per].rearrange("g c d -> c g d")
                    dst = wvpad[0:CTX, r:HEADS:per, :]
                    sp.dma_start(dst[:, :, r * D:(r + 1) * D], src).then_inc(pads_loaded, 16)

            load_pads(0, 32, d["a2_wk"], d["a2_wv"])

            def load_ct(n, par, has_next):
                sp.wait_ge(xx_ready, n + 1)
                sp.dma_start(CT[:, :, :], d["ctx"][bass.ds(n + 1, 1)].rearrange("b (p k) c -> p (b k) c", p=KP)) \
                    .then_inc(ct_loaded, 16)

            sp.dma_start(CT[:, :, :], d["ctx"][0:1].rearrange("b (p k) c -> p (b k) c", p=KP)).then_inc(ct_loaded, 16)
            with sp.Fori(0, BATCH - 1) as i:
                load_ct(i, 0, True)

            sp.wait_ge(proj_ps, 2)
            sp.dma_start(w_qL1, d["L1_Wq"]).then_inc(wL1_loaded, 16)
            sp.dma_start(w_oL1, d["L1_Wo"].rearrange("(c p) n -> p c n", p=128)).then_inc(wL1_loaded, 16)
            for j, name in enumerate(("L1f_Wq", "L1f_Wk", "L1f_Wv")):
                sp.dma_start(w_qkvL1[:, j, :], d[name]).then_inc(wL1_loaded, 16)

            def load_expert0(e, par):
                for j, name in enumerate(("gp", "up", "dp")):
                    sp.dma_start(we[:, par, j * 512:(j + 1) * 512], d[name][bass.ds(e, 1)].rearrange("a p n -> (a p) n")) \
                        .then_inc(expert_loaded[par], 16)

            def load_expert1(e, par):
                for j, name in enumerate(("W1", "W2")):
                    sp.dma_start(we[:, par, j * 512:(j + 1) * 512], d[name][bass.ds(e, 1)].rearrange("a p n -> (a p) n")) \
                        .then_inc(expert_loaded[par], 16)

            def load_experts(call, load):
                load(0, 0)
                load(1, 1)
                with sp.Fori(0, EXPERTS // 2 - 1) as i:
                    for par in range(2):
                        sp.wait_ge(dn_ps, 2 * i + EXPERTS * call + par + 1)
                        load(2 * i + 2 + par, par)

            load_experts(0, load_expert0)
            load_pads(1, 64, d["L1_Wk"], d["L1_Wv"])

            def load_kv(n, par, first):
                g = n + BATCH
                sp.wait_ge(kab_ready, g)
                for j in range(2):
                    sp.dma_start(Y[j * CTX:(j + 1) * CTX, :], d["ctxT"][bass.ds(n, 1)].rearrange("a c k -> (a c) k")) \
                        .then_inc(y_loaded, 16)
                sp.wait_ge(pv_done, (g - 1) * KT)
                sp.dma_start(V[:, par, :, 0:CTX], d["ctx"][bass.ds(n, 1)].rearrange("b (p k) c -> p (b k) c", p=KP)) \
                    .then_inc(v_loaded[par], 16)

            sp.wait_ge(dn_ps, EXPERTS)
            with sp.Fori(0, BATCH // 2) as i:
                load_kv(2 * i, 0, True)
                load_kv(2 * i + 1, 1, True)
            load_experts(1, load_expert1)
            sp.wait_ge(tm_ready, 10)
            sp.dma_start(out.rearrange("(t p) c -> p t c", p=TP), x_in[:, :, :]).then_inc(out_stored, 16)
            sp.wait_ge(out_stored, 16)

        @block.gpsimd
        def _(pool):
            n = Count()

            def seq(ins):
                ins.then_inc(consts_step, 1)
                pool.wait_ge(consts_step, n.up())

            def zero_pads(call):
                pool.memset(wkpad[:, :, :], 0.0).then_inc(pads_zeroed, 1)
                pool.wait_ge(pads_zeroed, 2 * call + 1)
                pool.memset(wvpad[:, :, :], 0.0).then_inc(pads_zeroed, 1)
                pool.wait_ge(pads_zeroed, 2 * call + 2)

            seq(pool.memset(ones[:, :], 1.0))
            seq(pool.memset(ident[:, :], 0.0))
            seq(pool.affine_select(out=ident[:, :], in_=ident[:, :], compare_op=ALU.not_equal, fill=1.0,
                                   base=0, pattern=[[-1, 128]], channel_multiplier=1))
            seq(pool.memset(mask_blocks[:, :], 0.0))
            seq(pool.affine_select(out=mask_blocks[:, 0:SEQ], in_=mask_blocks[:, 0:SEQ], compare_op=ALU.is_ge,
                                   fill=NEG, base=SEQ - 1, pattern=[[0, SEQ]], channel_multiplier=-1))
            seq(pool.affine_select(out=mask_blocks[:, SEQ:TP], in_=mask_blocks[:, SEQ:TP], compare_op=ALU.is_ge,
                                   fill=NEG, base=-SEQ, pattern=[[0, SEQ]], channel_multiplier=1))
            seq(pool.memset(mask_later[:, :], 1.0))
            seq(pool.affine_select(out=mask_later[:, :], in_=mask_later[:, :], compare_op=ALU.is_gt, fill=0.0,
                                   base=0, pattern=[[1, TP]], channel_multiplier=-1))
            seq(pool.affine_select(out=mask_causal[:, :], in_=mask_blocks[:, :], compare_op=ALU.is_ge, fill=NEG,
                                   base=0, pattern=[[-1, TP]], channel_multiplier=1))
            for m, w, k in ((heads4, 32, 4), (heads16, 8, 16)):
                seq(pool.memset(m[:, :], 1.0))
                seq(pool.affine_select(out=m[:, :], in_=m[:, :], compare_op=ALU.is_ge, fill=0.0,
                                       base=0, pattern=[[-w, k]], channel_multiplier=1))
                seq(pool.affine_select(out=m[:, :], in_=m[:, :], compare_op=ALU.is_ge, fill=0.0,
                                       base=w - 1, pattern=[[w, k]], channel_multiplier=-1))
            zero_pads(0)
            seq(pool.memset(kB[64:128, :, :].bitcast(f32), 0.0))
            seq(pool.memset(kB[64:66, :, :].bitcast(f32), 1.0))
            seq(pool.memset(qB[64:128, :, :].bitcast(f32), 0.0))

            def self_attention(call, heads, chunk_of):
                pool.wait_ge(lin_moved, 12 if call == 0 else LIN_U1 + 8 + 3)
                for p in range(TILES):
                    for c in range(4):
                        if p >= 1:
                            pool.wait_ge(s_ps, 16 * call + 4 * (p - 1) + c + 1)
                        k = big2[:, chunk_of(c), p * TP:(p + 1) * TP].unsqueeze(1).broadcast_to([128, 4, TP])
                        m = heads[:, :] if call == 0 else heads[:, 4 * c:4 * c + 4]
                        pool.tensor_tensor(Kblk[:, c, :, :], k, m.unsqueeze(2).broadcast_to([128, 4, TP]), ALU.mult) \
                            .then_inc(kblk_ready, 1)
                    if call == 0 and p >= 1:
                        mask_pair(p - 1)
                if call == 0:
                    mask_pair(TILES - 1)

            def mask_pair(p):
                pool.wait_ge(sum_done, p + 1)
                pool.tensor_tensor(S[:, p % 2], S[:, p % 2], mask_later[:, :].unsqueeze(1).broadcast_to([TP, 16, TP]),
                                   ALU.mult).then_inc(masked, 1)

            self_attention(0, heads4, lambda c: c)

            def normalise(nb):
                pool.wait_ge(xxT_ps, SPANS * nb) if not isinstance(nb, int) or nb > 0 else None
                pool.wait_ge(ct_loaded, 16 * nb + 16)
                mean = cmean[:, bass.ds(nb * KT, KT)].unsqueeze(2).broadcast_to([KP, KT, CTX])
                rstd = crstd[:, bass.ds(nb * KT, KT)]
                pool.tensor_tensor(CT[:, :, :], CT[:, :, :], mean, ALU.subtract).then_inc(consts_step, 1)
                pool.wait_ge(consts_step, 2 * nb + (n.n + 1))
                for j in range(2):
                    ins = pool.tensor_tensor(XX[:, :, j * CTX:(j + 1) * CTX], CT[:, :, :],
                                             rstd.unsqueeze(2).broadcast_to([KP, KT, CTX]), ALU.mult)
                ins.then_inc(xx_ready, 1)
                pool.memset(gsp[:, :], 0.0).then_inc(consts_step, 1)

            def split_keys(g, par, src_sem, src_val):
                pool.wait_ge(src_sem, src_val)
                pool.tensor_tensor(kA[:, par, :], Y[:, :], ones[:, :].broadcast_to([128, KEYS]), ALU.mult) \
                    .then_inc(kstep, 1)
                pool.wait_ge(kstep, 2 * g + 1)
                pool.tensor_tensor(kA[64:128, par, :], Y[64:128, :], kA[64:128, par, :], ALU.subtract) \
                    .then_inc(kstep, 1)
                pool.wait_ge(kstep, 2 * g + 2)
                pool.tensor_tensor(kB[0:64, par, :], kA[0:64, par, :], ones[0:64, :].broadcast_to([64, KEYS]), ALU.mult) \
                    .then_inc(kab_ready, 1)

            def prep0(nb, par, has_next):
                if not isinstance(nb, int) or nb >= 2:
                    pool.wait_ge(pv_done, KT * (nb - 1))
                split_keys(nb, par, y_ready, SPANS * nb + SPANS)
                pool.tensor_copy(V[:, par, :, 0:CTX], XX[:, :, 0:CTX]).then_inc(v_ready, 1)
                if has_next:
                    pool.wait_ge(v_ready, nb + 1)
                    normalise(nb + 1)

            gsp = sb("gsp", [1, 1])
            kstep = sem("kstep")
            pool.wait_ge(stats_ready, 1)
            pool.wait_ge(proj_ps, 1)
            pool.memset(V[:, :, :, CTX:128], 1.0)
            normalise(0)
            prep0(0, 0, True)
            prep0(1, 1, True)
            with pool.Fori(0, BATCH // 2 - 2) as i:
                prep0(2 * i + 2, 0, True)
                prep0(2 * i + 3, 1, True)
            prep0(BATCH - 2, 0, True)
            prep0(BATCH - 1, 1, False)
            n.up(2 * BATCH)

            pool.wait_ge(lin_ps, LIN_U0 + 4)
            zero_pads(1)

            def prep1(nb, par):
                g = nb + BATCH
                pool.wait_ge(pv_done, KT * (g - 1))
                split_keys(g, par, y_loaded, 32 * nb + 32)

            pool.wait_ge(dn_ps, EXPERTS)
            pool.memset(V[:, :, :, CTX:128], 1.0).then_inc(v_ready, 1)
            with pool.Fori(0, BATCH // 2) as i:
                prep1(2 * i, 0)
                prep1(2 * i + 1, 1)

            self_attention(1, heads16, lambda c: 0)

        @block.scalar
        def _(sc):
            fmT, lin, pts = Count(), Count(), Count()

            def move_fm(outs):
                sc.wait_ge(fmT_ps, fmT.up())
                for dst, g, b in outs:
                    if g is None:
                        ins = sc.activation(dst, PS[:, 7, 0:TOK], ACT.Identity)
                    else:
                        ins = sc.activation(dst, PS[:, 7, 0:TOK], ACT.Identity, bias=col(b), scale=col(g))
                ins.then_inc(fm_ready, 1)

            def move_lin(dst, n, func=ACT.Identity, bias=0.0, parts=128, view=None):
                sc.wait_ge(lin_ps, lin.up())
                src = PS[0:parts, (lin.n - 1) % 7, 0:n]
                sc.activation(dst, view(src) if view else src, func, bias=bias).then_inc(lin_moved, 1)

            def self_attention(call):
                def exp(p):
                    sc.wait_ge(s_shifted, TILES * call + p + 1)
                    sc.activation(S[:, p % 2], S[:, p % 2], ACT.Exp).then_inc(exp_done, 1)

                def values(p):
                    for c in range(4):
                        sc.wait_ge(pt_ps, pts.up())
                        sc.activation(PT[:, c % 2], PS[0:TP, 4 + c % 2, 0:4 * TP].rearrange("p (h q) -> p h q", h=4),
                                      ACT.Identity).then_inc(pt_moved, 1)
                    if call == 0:
                        sc.wait_ge(oT_ps, p + 1)
                        sc.activation(big1[:, 0:4, p * TP:(p + 1) * TP],
                                      PS[:, 7, 0:4 * TP].rearrange("p (c q) -> p c q", c=4), ACT.Identity) \
                            .then_inc(oT_moved, 1)

                exp(0)
                for p in range(TILES):
                    if p + 1 < TILES:
                        exp(p + 1)
                    values(p)

            def mlp(pre, c0):
                move_fm([(xn[:, :], pre + "ln3_g", pre + "ln3_b")])
                for c in range(FCH):
                    move_lin(big2[:, c, :], TOK, ACT.Gelu, cols[:, c0 + c:c0 + c + 1])

            def queries(nq):
                for c in range(nq):
                    move_lin(big1[:, c, :], TOK)
                for h in range(HEADS):
                    move_lin(qp[:, :, h, :], TOK, view=lambda s: s.rearrange("p (b q) -> p b q", b=BATCH))

            def cross(call, scale):
                def fills(nb):
                    for f in range(SPANS):
                        sc.wait_ge(xxT_ps, SPANS * nb + f + 1)
                        sc.activation(Y[:, f * SPAN:(f + 1) * SPAN], PS[:, f % 2, 0:SPAN], ACT.Identity,
                                      bias=col("L0_xattn_a2_lny_b"), scale=col("L0_xattn_a2_lny_g")) \
                            .then_inc(y_ready, 1)

                def step(b, par, has_next):
                    g0 = (b + BATCH * call) * KT
                    for kt in range(KT):
                        sc.wait_ge(st_ps, g0 + kt + 1)
                        if call or not isinstance(b, int) or b or kt >= 3:
                            sc.wait_ge(pv_done, g0 + kt - 2)
                        bank = 2 + 2 * (kt % 2)
                        sc.activation(P[:, kt % 3, :].rearrange("p (j n) -> p j n", j=2),
                                      PS[0:KP, bank:bank + 2, 0:HALF], ACT.Exp, scale=scale).then_inc(p_ready, 1)
                        if kt == 1 and has_next and call == 0:
                            sc.wait_ge(kab_ready, b + 1)
                            fills(b + 1)

                if call == 0:
                    fills(0)
                static_and_loop(sc, step, BATCH - 1)

            sc.wait_ge(params_loaded, 32)
            move_fm([(xn[:, :], "L0_xattn_a1_lnx_g", "L0_xattn_a1_lnx_b"),
                     (yn[:, :], "L0_xattn_a1_lny_g", "L0_xattn_a1_lny_b")])
            for c in range(4):
                move_lin(big1[:, c, :], TOK)
            for c in range(4):
                move_lin(big2[:, c, :], TOK)
            for p in range(TILES):
                move_lin(VT[:, p, :], 512, parts=TP)
            self_attention(0)
            mlp("L0_xattn_a1_", COL_A1_LI2)

            move_fm([(xn[:, :], "L0_xattn_a2_lnx_g", "L0_xattn_a2_lnx_b")])
            sc.wait_ge(stats_ready, 1)
            queries(4)
            cross(0, 32 ** -0.5)
            for c in range(4):
                move_lin(big1[:, c, :], TOK)
            mlp("L0_xattn_a2_", COL_A2_LI2)

            def gate(call):
                sc.wait_ge(gate_in, call + 1)
                sc.activation(gt[:, 0], gt[:, 0], ACT.Exp).then_inc(gate_exp, 1)

            move_fm([(xn[:, :], "L0_ffn_ln1_g", "L0_ffn_ln1_b")])
            move_fm([(xn[:, :], "L0_ffn_ln2_g", "L0_ffn_ln2_b")])
            gate(0)

            def silu(e, par, has_next):
                for c in range(FCH):
                    m = e * FCH + c
                    sc.wait_ge(g_ps, m + 1)
                    if not isinstance(e, int) or m >= 2:
                        sc.wait_ge(mul_done, m - 1)
                    sc.activation(sg[:, c % 2, :], PS[:, 2 + c % 2, 0:TOK], ACT.Silu).then_inc(g_moved, 1)

            static_and_loop(sc, silu, EXPERTS - 1)

            move_fm([(xn[:, :], None, None)])
            queries(8)
            cross(1, 64 ** -0.5)
            for c in range(8):
                move_lin(big1[:, c, :], TOK)

            move_fm([(xn[:, :], None, None)])
            move_lin(big1[:, 0, :], TOK)
            move_lin(big2[:, 0, :], TOK)
            move_lin(VT[:, :, 0:C], 512, parts=TP, view=lambda s: s.rearrange("p (t n) -> p t n", t=TILES))
            self_attention(1)

            move_fm([(xn[:, :], None, None)])
            gate(1)

            def relu(e, par, has_next):
                for c in range(FCH):
                    m = e * FCH + c
                    sc.wait_ge(g_ps, m + 1 + EXPERTS * FCH)
                    if not isinstance(e, int) or e >= 2:
                        sc.wait_ge(dn_ps, e - 1 + EXPERTS)
                    sc.activation(act[:, par, c, :], PS[:, 2 + c % 2, 0:TOK], ACT.Relu,
                                  bias=cols[:, bass.ds(COL_B1 + m, 1)]).then_inc(g_moved, 1)

            static_and_loop(sc, relu, EXPERTS - 1)

        @block.vector
        def _(v):
            n, proj = Count(), Count()

            def seq(ins):
                ins.then_inc(dve_step, 1)
                v.wait_ge(dve_step, n.up())

            def rsqrt(y, var, tmp):
                seq(v.tensor_scalar(y.bitcast(i32), var.bitcast(i32), -0.5, 1597463007.0, ALU.mult, ALU.add))
                for _ in range(4):
                    seq(v.tensor_tensor(tmp, y, y, ALU.mult))
                    seq(v.scalar_tensor_tensor(tmp, tmp, -0.5, var, ALU.mult, ALU.mult))
                    seq(v.scalar_tensor_tensor(y, tmp, 1.5, y, ALU.add, ALU.mult))

            def layernorm(src, dst):
                for t in range(TILES):
                    ins = v.bn_stats(stats[:, t, :], src[:, t, :])
                seq(ins)
                for t in range(TILES):
                    ins = v.bn_aggr(mv[:, t, :], stats[:, t, :])
                seq(ins)
                seq(v.tensor_scalar(rs[:, 0, :], mv[:, :, 1], EPS, None, ALU.add))
                rsqrt(rs[:, 1, :], rs[:, 0, :], rs[:, 2, :])
                for t in range(TILES):
                    ins = v.tensor_scalar(dst[:, t, :], src[:, t, :], mv[:, t, 0:1], rs[:, 1, t:t + 1],
                                          ALU.subtract, ALU.mult)
                seq(ins)

            def tt(dst, a, b, op):
                seq(v.tensor_tensor(dst, a, b, op))

            def affine(dst, src, g, b):
                tt(dst, src, row(g), ALU.mult)
                tt(dst, dst, row(b), ALU.add)

            def proj_in():
                v.wait_ge(proj_ps, proj.up())
                return PS[0:TP, 0, :].rearrange("p (t c) -> p t c", t=TILES)

            def ready():
                v.engine_nop().then_inc(tm_ready, 1)

            def self_attention(call, scale, mask, D):
                def shift(p):
                    if p >= 2 and call == 0:
                        v.wait_ge(pt_ps, 16 * call + 4 * (p - 1))
                    elif p >= 2:
                        v.wait_ge(pt_ps, 16 * call + 4 * (p - 1))
                    for c in range(4):
                        v.wait_ge(s_ps, 16 * call + 4 * p + c + 1)
                        ins = v.scalar_tensor_tensor(
                            S[:, p % 2, 4 * c:4 * c + 4, :],
                            PS[0:TP, c, 0:4 * TP].rearrange("p (h k) -> p h k", h=4), scale,
                            mask[:, :].unsqueeze(1).broadcast_to([TP, 4, TP]), ALU.mult, ALU.add)
                        ins.then_inc(s_read, 1)
                    v.wait_ge(s_read, 16 * call + 4 * p + 4)
                    seq(v.tensor_reduce(rneg[:, p % 2, :], S[:, p % 2], AX.X, ALU.max))
                    v.tensor_tensor(S[:, p % 2], S[:, p % 2],
                                    rneg[:, p % 2, :].unsqueeze(2).broadcast_to([TP, 16, TP]),
                                    ALU.subtract).then_inc(s_shifted, 1)

                def sums(p):
                    v.wait_ge(exp_done, TILES * call + p + 1)
                    v.tensor_reduce(rsum[:, p % 2, :], S[:, p % 2], AX.X, ALU.add).then_inc(sum_done, 1)
                    v.wait_ge(sum_done, TILES * call + p + 1)
                    seq(v.reciprocal(rsum[:, p % 2, :], rsum[:, p % 2, :]))

                def output(p):
                    v.wait_ge(o_sa_ps, TILES * call + p + 1)
                    if call == 0 and p >= 2:
                        v.wait_ge(oT_ps, p - 1)
                    dst = OT[:, p % 2, :] if call == 0 else tb[:, p, :]
                    v.tensor_tensor(dst.rearrange("p (h e) -> p h e", e=D),
                                    PS[0:TP, 6, 0:16 * D].rearrange("p (h e) -> p h e", e=D),
                                    rsum[:, p % 2, :].unsqueeze(2).broadcast_to([TP, 16, D]),
                                    ALU.mult).then_inc(o_sa_ready, 1)

                shift(0)
                for p in range(TILES):
                    if p + 1 < TILES:
                        shift(p + 1)
                    sums(p)
                    output(p)

            def mlp(b1, b3, skip):
                tt(tb[:, :, :], proj_in(), tb[:, :, :], ALU.add)
                layernorm(tb, hat)
                ready()
                tt(tc_[:, :, :], tb[:, :, :], row(b3), ALU.add)
                tt(tc_[:, :, :], tc_[:, :, :], skip[:, :, :], ALU.add)
                tt(tc_[:, :, :], proj_in(), tc_[:, :, :], ALU.add)

            def cross(call):
                def split_queries(nb, par):
                    if call or not isinstance(nb, int) or nb >= 2:
                        v.wait_ge(pv_done, KT * (nb + BATCH * call - 1))
                    q = qp[:, bass.ds(nb, 1)].rearrange("p a h q -> p (a h q)")
                    v.tensor_copy(qA[:, par, :], q).then_inc(qs_ready, 1)
                    v.wait_ge(qs_ready, 2 * (nb + BATCH * call) + 1)
                    v.tensor_tensor(qB[0:64, par, :], q[0:64], qA[0:64, par, :], ALU.subtract).then_inc(qs_ready, 1)

                def maxima(nb, par):
                    g = nb + BATCH * call
                    for j in range(HQ_TILES * SPANS):
                        v.wait_ge(sc_ps, g * HQ_TILES * SPANS + j + 1)
                        v.tensor_reduce(mx[:, j // SPANS, j % SPANS:j % SPANS + 1], PS[:, j % 2, 0:SPAN],
                                        AX.X, ALU.max).then_inc(sc_max, 1)
                    v.wait_ge(sc_max, (g + 1) * HQ_TILES * SPANS)
                    v.tensor_reduce(negm[:, :], mx[:, :, :], AX.X, ALU.max, negate=True).then_inc(negm_ready, 1)
                    v.wait_ge(negm_ready, 4 * g + 1)
                    v.tensor_copy(mhr[:, :], negm[:, :]).then_inc(negm_ready, 1)
                    v.wait_ge(negm_ready, 4 * g + 2)
                    v.tensor_copy(mhl[:, :, 0], mhr[:, :].bitcast(f32)).then_inc(negm_ready, 1)
                    v.tensor_tensor(mhl[:, :, 1], negm[:, :], mhr[:, :].bitcast(f32), ALU.subtract) \
                        .then_inc(negm_ready, 1)
                    v.wait_ge(mrow_ps, g + 1)
                    v.tensor_copy(qB[64:66, par, 0:512], PS[64:66, 0, 0:512])
                    v.tensor_copy(qB[64:66, par, 512:HQ], PS[64:66, 1, 0:HQ - 512]).then_inc(mrow_moved, 1)

                def output(b):
                    g = b + BATCH * call
                    v.wait_ge(pv_done, KT * (g + 1))
                    den = PS[64:128, 6:8, 0:HALF]
                    v.reciprocal(rden[:, :].rearrange("p (j n) -> p j n", j=2), den).then_inc(o_step, 1)
                    v.wait_ge(o_step, g + 1)
                    v.tensor_tensor(qp[0:64, bass.ds(b, 1)].rearrange("p a h q -> p (a h q)")
                                    .rearrange("p (j n) -> p j n", j=2),
                                    PS[0:64, 6:8, 0:HALF], rden[:, :].rearrange("p (j n) -> p j n", j=2),
                                    ALU.mult).then_inc(o_moved, 1)

                def step(b, par, has_next):
                    if has_next:
                        split_queries(b + 1, 1 - par)
                        maxima(b + 1, 1 - par)
                    output(b)

                v.wait_ge(lin_moved, (LIN_U0, LIN_U1)[call])
                split_queries(0, 0)
                maxima(0, 0)
                static_and_loop(v, step, BATCH - 1)
                v.wait_ge(o_moved, BATCH * (call + 1))

            def gate(call):
                src = proj_in()
                seq(v.tensor_copy(lg[:, :, :], PS[0:TP, 0, 0:TILES * EXPERTS].rearrange("p (t e) -> p t e", t=TILES)))
                for t in range(TILES):
                    ins = v.max(top[:, t, :], lg[:, t, :])
                seq(ins)
                bc = lambda a: a.broadcast_to([TP, TILES, EXPERTS])
                v.tensor_tensor(gt[:, 0], lg[:, :, :], bc(top[:, :, 0:1]), ALU.subtract).then_inc(gate_in, 1)
                tt(gt[:, 1], lg[:, :, :], bc(top[:, :, 1:2]), ALU.is_gt)
                tt(gt[:, 2], lg[:, :, :], bc(top[:, :, 1:2]), ALU.is_equal)
                seq(v.tensor_reduce(gs[:, :], gt[:, 1], AX.X, ALU.add))
                tt(gt[:, 3, :, 0], gt[:, 2, :, 0], gs[:, :], ALU.add)
                for e in range(1, EXPERTS):
                    tt(gt[:, 3, :, e], gt[:, 3, :, e - 1], gt[:, 2, :, e], ALU.add)
                seq(v.scalar_tensor_tensor(gt[:, 2], gt[:, 3], 2.0, gt[:, 2], ALU.is_le, ALU.mult))
                tt(gt[:, 1], gt[:, 1], gt[:, 2], ALU.add)
                v.wait_ge(gate_exp, call + 1)
                tt(gt[:, 1], gt[:, 1], gt[:, 0], ALU.mult)
                seq(v.tensor_reduce(gs[:, :], gt[:, 1], AX.X, ALU.add))
                seq(v.reciprocal(gs[:, :], gs[:, :]))
                seq(v.tensor_tensor(comb[:, :, :].rearrange("p e t -> p t e"), gt[:, 1],
                                    gs[:, :].unsqueeze(2).broadcast_to([TP, TILES, EXPERTS]), ALU.mult))
                v.engine_nop().then_inc(comb_ready, 1)

            def add_expert(e, par, call):
                g = e + EXPERTS * call
                v.tensor_copy(cw[:, par, :], comb[:, bass.ds(e, 1), :].rearrange("p a t -> p (a t)")) \
                    .then_inc(cw_ready, 1)
                v.wait_ge(cw_ready, g + 1)
                v.wait_ge(dn_ps, g + 1)
                v.wait_ge(dn_added, g + call + 1)
                for t in range(TILES):
                    ins = v.scalar_tensor_tensor(tc_[:, t, :], PS[0:TP, 4 + par, t * C:(t + 1) * C],
                                                 cw[:, par, t:t + 1], tc_[:, t, :], ALU.mult, ALU.add)
                ins.then_inc(dn_added, 1)

            cw_ready = sem("cw_ready")
            o_step = sem("o_step")

            v.wait_ge(x_loaded, 16)
            layernorm(x_in, hat)
            layernorm(hat, hat)
            v.wait_ge(params_loaded, 32)
            affine(ta[:, :, :], hat[:, :, :], "L0_xattn_ln1_g", "L0_xattn_ln1_b")
            layernorm(ta, hat)
            ready()
            tt(tb[:, :, :], ta[:, :, :], row("L0_xattn_a1_li1_b"), ALU.add)

            v.wait_ge(craw_loaded, 16)
            for b in range(BATCH):
                for k in range(KT):
                    ins = v.bn_stats(cst[:, k, :], craw[:, b * KT + k, :])
                seq(ins)
                w = slice(b * KT, (b + 1) * KT)
                tt(cmean[:, w], cst[:, :, 1], cst[:, :, 4], ALU.add)
                tt(ctmp[:, 0, w], cst[:, :, 1], cst[:, :, 4], ALU.subtract)
                tt(ctmp[:, 1, w], cst[:, :, 2], cst[:, :, 5], ALU.add)
            seq(v.tensor_scalar(cmean[:, :], cmean[:, :], 0.5, None, ALU.mult))
            seq(v.tensor_scalar(ctmp[:, 0, :], ctmp[:, 0, :], 0.5, None, ALU.mult))
            tt(ctmp[:, 0, :], ctmp[:, 0, :], ctmp[:, 0, :], ALU.mult)
            seq(v.scalar_tensor_tensor(ctmp[:, 0, :], ctmp[:, 1, :], 1.0 / CTX, ctmp[:, 0, :], ALU.mult, ALU.add))
            seq(v.tensor_scalar(ctmp[:, 0, :], ctmp[:, 0, :], EPS, None, ALU.add))
            rsqrt(crstd[:, :], ctmp[:, 0, :], ctmp[:, 1, :])
            v.engine_nop().then_inc(stats_ready, 1)

            self_attention(0, 32 ** -0.5, mask_blocks, 32)
            mlp("L0_xattn_a1_li1_b", "L0_xattn_a1_li3_b", ta)
            layernorm(tc_, hat)
            affine(ta[:, :, :], hat[:, :, :], "L0_xattn_ln2_g", "L0_xattn_ln2_b")
            layernorm(ta, hat)
            ready()
            tt(tb[:, :, :], ta[:, :, :], row("L0_xattn_a2_li1_b"), ALU.add)
            cross(0)
            seq(v.tensor_scalar(qp[0:64, :, :, :].rearrange("p b h q -> p (b h q)"),
                                qp[0:64, :, :, :].rearrange("p b h q -> p (b h q)"),
                                col("L0_xattn_a2_lny_g")[0:64], col("L0_xattn_a2_lny_b")[0:64],
                                ALU.mult, ALU.add))
            v.engine_nop().then_inc(u_ready, 1)
            mlp("L0_xattn_a2_li1_b", "L0_xattn_a2_li3_b", ta)
            tt(x_in[:, :, :], x_in[:, :, :], tc_[:, :, :], ALU.add)
            layernorm(x_in, ta)
            layernorm(ta, hat)
            ready()
            tt(tb[:, :, :], proj_in(), ta[:, :, :], ALU.add)
            layernorm(tb, hat)
            ready()
            v.tensor_tensor(tc_[:, :, :], x_in[:, :, :], tb[:, :, :], ALU.add).then_inc(dn_added, 1)
            gate(0)

            def expert0(e, par, has_next):
                for c in range(FCH):
                    m = e * FCH + c
                    v.wait_ge(g_moved, m + 1)
                    v.tensor_tensor(act[:, par, c, :], sg[:, c % 2, :], PS[:, 6 + c % 2, 0:TOK], ALU.mult) \
                        .then_inc(mul_done, 1)
                if not isinstance(e, int) or e:
                    add_expert(e - 1, 1 - par, 0)

            static_and_loop(v, expert0, EXPERTS - 1)
            add_expert(EXPERTS - 1, 1, 0)
            v.wait_ge(dn_added, EXPERTS + 1)
            layernorm(tc_, hat)
            ready()
            tt(x_in[:, :, :], tc_[:, :, :], row("L1_xattn_bo"), ALU.add)
            cross(1)
            v.engine_nop().then_inc(u_ready, 1)
            tt(x_in[:, :, :], proj_in(), x_in[:, :, :], ALU.add)
            layernorm(x_in, ta)
            ready()
            self_attention(1, 128 ** -0.5, mask_causal, 8)
            v.wait_ge(o_sa_ready, 2 * TILES)
            layernorm(tb, hat)
            affine(tb[:, :, :], hat[:, :, :], "L1_ffn_ln1_g", "L1_ffn_ln1_b")
            tt(tb[:, :, :], tb[:, :, :], ta[:, :, :], ALU.add)
            ready()
            tt(x_in[:, :, :], x_in[:, :, :], tb[:, :, :], ALU.add)
            gate(1)
            v.wait_ge(combT_ps, 1)
            seq(v.tensor_copy(combT[:, :], PS[0:EXPERTS, 7, 0:TOK]))
            v.engine_nop().then_inc(combT_ready, 1)
            v.tensor_copy(tc_[:, :, :], proj_in()).then_inc(dn_added, 1)

            def expert1(e, par, has_next):
                if not isinstance(e, int) or e:
                    add_expert(e - 1, 1 - par, 1)

            static_and_loop(v, expert1, EXPERTS - 1)
            add_expert(EXPERTS - 1, 1, 1)
            v.wait_ge(dn_added, 2 * EXPERTS + 2)
            layernorm(tc_, hat)
            affine(hat[:, :, :], hat[:, :, :], "L1_ffn_ln2_g", "L1_ffn_ln2_b")
            tt(x_in[:, :, :], x_in[:, :, :], hat[:, :, :], ALU.add)
            ready()

        @block.tensor
        def _(pe):
            tm, fm, lin, pts = Count(), Count(), Count(), Count()

            def to_fm(src):
                pe.wait_ge(tm_ready, tm.up())
                for t in range(TILES):
                    ins = pe.transpose(PS[:, 7, t * TP:(t + 1) * TP], src[:, t, :], ident[0:TP, 0:TP])
                ins.then_inc(fmT_ps, 1)

            def linear(products, nout, parts=128, offs=None):
                j = lin.n
                if j >= 7:
                    pe.wait_ge(lin_moved, j - 6)
                for i, (l, r) in enumerate(products):
                    if offs is None:
                        ins = pe.matmul(PS[0:parts, j % 7, 0:nout], l, r,
                                        start=i == 0, stop=i == len(products) - 1)
                    else:
                        ins = pe.matmul(PS[0:parts, j % 7, i * nout:(i + 1) * nout], l, r, start=True, stop=True)
                lin.up()
                ins.then_inc(lin_ps, 1)

            def project(lhs, w, chunks, width=C):
                for t in range(TILES):
                    for c in range(chunks):
                        ins = pe.matmul(PS[0:TP, 0, t * width:(t + 1) * width], lhs(c, t), w(c),
                                        start=c == 0, stop=c == chunks - 1)
                ins.then_inc(proj_ps, 1)

            def tok(tile, t):
                return tile[:, t * TP:(t + 1) * TP]

            def self_attention(call, q, D):
                last = lin.n
                pe.wait_ge(lin_moved, last)

                def scores(p):
                    for c in range(4):
                        pe.wait_ge(kblk_ready, 16 * call + 4 * p + c + 1)
                        if p >= 1:
                            pe.wait_ge(s_read, 16 * call + 4 * (p - 1) + c + 1)
                        pe.matmul(PS[0:TP, c, 0:4 * TP], q(c, p), Kblk[:, c, :, :].rearrange("p h k -> p (h k)"),
                                  start=True, stop=True).then_inc(s_ps, 1)

                def values(p):
                    if call == 0:
                        pe.wait_ge(masked, p + 1)
                    else:
                        pe.wait_ge(exp_done, TILES * call + p + 1)
                    if p >= 1:
                        pe.wait_ge(o_sa_ready, TILES * call + p)

                    def transposes(c):
                        if p * 4 + c >= 2:
                            pe.wait_ge(pt_moved, 16 * call + 4 * p + c - 1)
                        for h in range(4):
                            ins = pe.transpose(PS[0:TP, 4 + c % 2, h * TP:(h + 1) * TP], S[:, p % 2, 4 * c + h, :],
                                               ident[0:TP, 0:TP])
                        ins.then_inc(pt_ps, 1)

                    def weigh(c):
                        pe.wait_ge(pt_moved, 16 * call + 4 * p + c + 1)
                        for h in range(4):
                            hh = 4 * c + h
                            ins = pe.matmul(PS[0:TP, 6, hh * D:(hh + 1) * D], PT[:, c % 2, h, :],
                                            VT[:, p, hh * D:(hh + 1) * D], start=True, stop=True)
                        return ins

                    transposes(0)
                    for c in range(4):
                        if c + 1 < 4:
                            transposes(c + 1)
                        ins = weigh(c)
                    ins.then_inc(o_sa_ps, 1)

                def out_t(p):
                    pe.wait_ge(o_sa_ready, p + 1)
                    if p >= 1:
                        pe.wait_ge(oT_moved, p)
                    for c in range(4):
                        ins = pe.transpose(PS[:, 7, c * TP:(c + 1) * TP], OT[:, p % 2, c * 128:(c + 1) * 128],
                                           ident[0:TP, 0:TP])
                    ins.then_inc(oT_ps, 1)

                scores(0)
                for p in range(TILES):
                    if p + 1 < TILES:
                        scores(p + 1)
                    values(p)
                    if call == 0:
                        out_t(p)

            def mlp(w):
                project(lambda c, t: tok(big1[:, c, :], t), lambda c: w[0][:, c * C:(c + 1) * C], 4)
                to_fm(hat)
                pe.wait_ge(fm_ready, fm.up())
                for c in range(FCH):
                    linear([(w[1][:, c * 128:(c + 1) * 128], xn[:, :])], TOK)
                pe.wait_ge(lin_moved, lin.n)
                project(lambda c, t: tok(big2[:, c, :], t), lambda c: w[2][:, c * C:(c + 1) * C], FCH)

            def queries(wq, nq, loaded, per):
                pe.wait_ge(fm_ready, fm.up())
                for c in range(nq):
                    linear([(wq[:, c * 128:(c + 1) * 128], xn[:, :])], TOK)
                pe.wait_ge(pads_loaded, loaded)
                pe.wait_ge(lin_moved, lin.n)
                for h in range(HEADS):
                    linear([(wkpad[:, h, :], big1[:, h // per, :])], TOK)

            def cross(call):
                def fill(nb, f):
                    if f == 0:
                        pe.wait_ge(xx_ready, nb + 1)
                    if f == 0 and (not isinstance(nb, int) or nb >= 1):
                        pe.wait_ge(mrow_moved, nb)
                    if f == 2:
                        pe.wait_ge(y_ready, SPANS * nb + 1)
                    for j in range(SPAN // KP):
                        kt = f * (SPAN // KP) + j
                        ins = pe.transpose(PS[:, f % 2, j * KP:(j + 1) * KP], XX[:, kt, :], ident[0:KP, 0:KP])
                    ins.then_inc(xxT_ps, 1)

                def score(nb, par, j):
                    g = nb + BATCH * call
                    if j == 0:
                        pe.wait_ge(kab_ready, g + 1)
                        pe.wait_ge(qs_ready, 2 * g + 2)
                        if call or not isinstance(nb, int) or nb >= 1:
                            pe.wait_ge(mrow_moved, g)
                    if j >= 2:
                        pe.wait_ge(sc_max, g * HQ_TILES * SPANS + j - 1)
                    r, s = j // SPANS, j % SPANS
                    pe.matmul(PS[:, j % 2, 0:SPAN], qA[:, par, r * 128:(r + 1) * 128],
                              kA[:, par, s * SPAN:(s + 1) * SPAN], start=True, stop=True).then_inc(sc_ps, 1)

                def max_rows(nb):
                    g = nb + BATCH * call
                    pe.wait_ge(negm_ready, 4 * g + 4)
                    for j in range(HQ_TILES):
                        ins = pe.matmul(PS[64:66, j // 4, (j % 4) * 128:(j % 4 + 1) * 128], mhl[:, j, :], ident[:, :],
                                        start=True, stop=True)
                    ins.then_inc(mrow_ps, 1)

                def score_t(b, par, kt):
                    g0 = KT * (b + BATCH * call)
                    if kt == 0:
                        pe.wait_ge(mrow_moved, b + BATCH * call + 1)
                    if call or not isinstance(b, int) or b or kt >= 2:
                        pe.wait_ge(p_ready, g0 + kt - 1)
                    keys = slice(kt * KP, (kt + 1) * KP)
                    for j in range(2):
                        bank = PS[0:KP, 2 + 2 * (kt % 2) + j, 0:HALF]
                        pe.matmul(bank, kA[:, par, keys], qA[:, par, j * HALF:(j + 1) * HALF], start=True, stop=False)
                        ins = pe.matmul(bank, kB[:, par, keys], qB[:, par, j * HALF:(j + 1) * HALF],
                                        start=False, stop=True)
                    ins.then_inc(st_ps, 1)

                def weigh(b, par, kt):
                    g0 = KT * (b + BATCH * call)
                    if kt == 0:
                        if call == 0:
                            pe.wait_ge(v_ready, b + 1)
                        else:
                            pe.wait_ge(v_loaded[par], (b - par) * 8 + 16)
                        if call or not isinstance(b, int) or b:
                            pe.wait_ge(o_moved, b + BATCH * call)
                    pe.wait_ge(p_ready, g0 + kt + 1)
                    for j in range(2):
                        ins = pe.matmul(PS[:, 6 + j, 0:HALF], V[:, par, kt, :], P[:, kt % 3, j * HALF:(j + 1) * HALF],
                                        start=kt == 0, stop=kt == KT - 1)
                    ins.then_inc(pv_done, 1)

                def step(b, par, has_next):
                    score_t(b, par, 0)
                    for kt in range(KT):
                        if kt + 1 < KT:
                            score_t(b, par, kt + 1)
                        weigh(b, par, kt)
                        if has_next:
                            if kt == 0 and call == 0:
                                for f in range(SPANS):
                                    fill(b + 1, f)
                            if 3 <= kt < 10:
                                for j in range(SPANS):
                                    score(b + 1, 1 - par, (kt - 3) * SPANS + j)
                            if kt == 10:
                                max_rows(b + 1)

                if call == 0:
                    pe.wait_ge(xx_ready, 1)
                else:
                    pe.wait_ge(v_ready, BATCH + 1)
                pe.wait_ge(lin_moved, lin.n)
                if call == 0:
                    for f in range(SPANS):
                        fill(0, f)
                for j in range(HQ_TILES * SPANS):
                    score(0, 0, j)
                max_rows(0)
                static_and_loop(pe, step, BATCH - 1)

            def outputs(call, nq, per):
                pe.wait_ge(u_ready, call + 1)
                for c in range(nq):
                    linear([(wvpad[:, h, :], qp[:, :, h, :]) for h in range(c * per, (c + 1) * per)], TOK)
                pe.wait_ge(lin_moved, lin.n)

            def moe(call, gate_w):
                w = we[:, :, :].rearrange("p b (j n) -> p b j n", j=3)
                loads = 3 - call
                before = 0 if call == 0 else 4 * 3 * 16

                pe.wait_ge(fm_ready, fm.up())
                project(lambda c, t: tok(xn, t), lambda c: gate_w[:, :], 1, EXPERTS)

                def up(e, par, has_next):
                    pe.wait_ge(expert_loaded[par], (e - par) * (loads * 8) + (before + loads * 16))
                    for c in range(FCH):
                        m = e * FCH + c
                        if isinstance(m, int) and m < 2:
                            pass
                        elif call == 0:
                            pe.wait_ge(mul_done, m - 1)
                        else:
                            pe.wait_ge(g_moved, m - 1 + EXPERTS * FCH)
                        mm = pe.matmul(PS[:, 2 + c % 2, 0:TOK], w[:, par, 0, c * 128:(c + 1) * 128], xn[:, :],
                                       start=True, stop=True)
                        if call == 0:
                            mm = pe.matmul(PS[:, 6 + c % 2, 0:TOK], w[:, par, 1, c * 128:(c + 1) * 128], xn[:, :],
                                           start=True, stop=True)
                        mm.then_inc(g_ps, 1)

                def down(e, par):
                    if call == 0:
                        pe.wait_ge(mul_done, (e + 1) * FCH)
                    else:
                        pe.wait_ge(g_moved, (e + 1 + EXPERTS) * FCH)
                    if not isinstance(e, int) or e >= 2:
                        pe.wait_ge(dn_added, e + EXPERTS * call + call + 1)
                    for t in range(TILES):
                        for c in range(FCH):
                            mm = pe.matmul(PS[0:TP, 4 + par, t * C:(t + 1) * C], tok(act[:, par, c, :], t),
                                           w[:, par, 2 - call, c * C:(c + 1) * C], start=c == 0, stop=c == FCH - 1)
                    mm.then_inc(dn_ps, 1)

                def step(e, par, has_next):
                    up(e, par, has_next)
                    if not isinstance(e, int) or e:
                        down(e - 1, 1 - par)
                    if call == 1 and isinstance(e, int) and e == 0:
                        pe.wait_ge(comb_ready, 2)
                        for t in range(TILES):
                            mm = pe.transpose(PS[0:EXPERTS, 7, t * TP:(t + 1) * TP], comb[:, :, t],
                                              ident[0:TP, 0:TP])
                        mm.then_inc(combT_ps, 1)
                        pe.wait_ge(combT_ready, 1)
                        project(lambda c, t: combT[:, t * TP:(t + 1) * TP], lambda c: b2[:, :], 1)

                static_and_loop(pe, step, EXPERTS - 1)
                down(EXPERTS - 1, 1)

            pe.wait_ge(consts_step, 18)
            to_fm(hat)
            pe.wait_ge(fm_ready, fm.up())
            pe.wait_ge(wA_loaded, 6 * 16)
            for c in range(4):
                linear([(w_q1[:, c * 128:(c + 1) * 128], xn[:, :])], TOK)
            for c in range(4):
                linear([(w_k1[:, c * 128:(c + 1) * 128], yn[:, :])], TOK)
            for p in range(TILES):
                linear([(tok(yn, p), w_v1)], 512, TP)
            self_attention(0, lambda c, p: tok(big1[:, c, :], p), 32)
            pe.wait_ge(oT_moved, TILES)
            mlp(w_a1)
            to_fm(hat)
            pe.wait_ge(wB_loaded, 8 * 16)
            queries(wq2, 4, 12 * 16, 4)
            cross(0)
            outputs(0, 4, 4)
            mlp(w_a2)
            to_fm(hat)
            pe.wait_ge(fm_ready, fm.up())
            project(lambda c, t: tok(xn, t), lambda c: attn_w[:, :], 1)
            to_fm(hat)
            moe(0, gate0)
            to_fm(hat)
            pe.wait_ge(wL1_loaded, 5 * 16)
            queries(w_qL1, 8, 18 * 16, 2)
            cross(1)
            outputs(1, 8, 2)
            project(lambda c, t: tok(big1[:, c, :], t), lambda c: w_oL1[:, c, :], 8)
            to_fm(ta)
            pe.wait_ge(fm_ready, fm.up())
            linear([(w_qkvL1[:, 0, :], xn[:, :])], TOK)
            linear([(w_qkvL1[:, 1, :], xn[:, :])], TOK)
            linear([(tok(xn, p), w_qkvL1[:, 2, :]) for p in range(TILES)], C, TP, offs=True)
            self_attention(1, lambda c, p: tok(big1[:, 0, :], p), 8)
            to_fm(tb)
            moe(1, gate1)


def kernel(**inputs):
    import numpy as np
    import concourse.bacc as bacc
    from concourse.bass_utils import run_bass_kernel_spmd

    a = {k: np.asarray(v) for k, v in inputs.items()}
    L0, F0, X1, F1 = "L0_xattn_", "L0_ffn_", "L1_xattn_", "L1_ffn_"
    heads_side = lambda w: w.transpose(1, 0, 2).reshape(w.shape[1], -1)
    chunk_cols = lambda v: v.reshape(-1, 128).T
    both = lambda v: np.concatenate([v, v]) if v.shape[0] == CTX else v
    ctx = a["ctx_512"]
    arrays = {
        "x": a["x"].reshape(TOK, C),
        "ctx": ctx,
        "ctxT": ctx.reshape(BATCH, KP, KT, CTX).transpose(0, 3, 2, 1).reshape(BATCH, CTX, KEYS),
        "rows": np.stack([a[n] for n in ROWS]),
        "cols": np.concatenate([np.stack([both(a[n]) for n in COLS], axis=1),
                                chunk_cols(a[L0 + "a1_li2_b"]), chunk_cols(a[L0 + "a2_li2_b"]),
                                chunk_cols(a[F1 + "b1"])], axis=1),
        "a1_wq": heads_side(a[L0 + "a1_wq"]), "a1_wk": heads_side(a[L0 + "a1_wk"]),
        "a1_wv": heads_side(a[L0 + "a1_wv"]),
        "a1_li1": a[L0 + "a1_li1_w"], "a1_li2": a[L0 + "a1_li2_w"], "a1_li3": a[L0 + "a1_li3_w"],
        "a2_wq": heads_side(a[L0 + "a2_wq"]),
        "a2_wk": a[L0 + "a2_wk"].transpose(0, 2, 1), "a2_wv": a[L0 + "a2_wv"],
        "a2_li1": a[L0 + "a2_li1_w"], "a2_li2": a[L0 + "a2_li2_w"], "a2_li3": a[L0 + "a2_li3_w"],
        "attn_w": a[F0 + "attn_w"].T, "gate0": a[F0 + "gate_w"].T,
        "gp": a[F0 + "gate_proj"].transpose(0, 2, 1), "up": a[F0 + "up_proj"].transpose(0, 2, 1),
        "dp": a[F0 + "down_proj"].transpose(0, 2, 1).reshape(EXPERTS, FCH, 128, C).transpose(0, 2, 1, 3)
        .reshape(EXPERTS, 128, FF),
        "L1_Wq": a[X1 + "Wq"], "L1_Wo": a[X1 + "Wo"],
        "L1_Wk": a[X1 + "Wk"].T.reshape(HEADS, 64, CTX),
        "L1_Wv": a[X1 + "Wv"].reshape(CTX, HEADS, 64).transpose(1, 0, 2),
        "L1f_Wq": heads_side(a[F1 + "Wq"]), "L1f_Wk": heads_side(a[F1 + "Wk"]), "L1f_Wv": heads_side(a[F1 + "Wv"]),
        "gate1": a[F1 + "gate_W"], "W1": a[F1 + "W1"], "b2": a[F1 + "b2"],
        "W2": a[F1 + "W2"].reshape(EXPERTS, FCH, 128, C).transpose(0, 2, 1, 3).reshape(EXPERTS, 128, FF),
    }
    arrays = {k: np.ascontiguousarray(v) for k, v in arrays.items()}

    nc = bacc.Bacc("TRN2", target_bir_lowering=False, num_devices=1)
    f32 = mybir.dt.float32
    d = {k: nc.dram_tensor("in_" + k, v.shape, f32, kind="ExternalInput").ap() for k, v in arrays.items()}
    out = nc.dram_tensor("out", (TOK, C), f32, kind="ExternalOutput").ap()
    build_program(nc, d, out)
    r = run_bass_kernel_spmd(nc, [{"in_" + k: v for k, v in arrays.items()}], core_ids=[0])
    return r.results[0]["out"].reshape(BATCH, SEQ, C)
```

```python
import concourse.bass as bass
import concourse.mybir as mybir
from contextlib import ExitStack

BATCH, SEQ, C = 8, 56, 128
KEYS, CTX = 1500, 64
HEADS = 16
TILES = 4
TP = BATCH * SEQ // TILES
TOK = BATCH * SEQ
KT = 12
KP = KEYS // KT
HQ = HEADS * SEQ
HQ_TILES = HQ // 128
HALF = HQ // 2
FF = 512
FCH = FF // 128
EXPERTS = 8
EPS = 1e-5
NEG = -1e30
SPAN = 500
SPANS = KEYS // SPAN

ROWS = ["L0_xattn_ln1_g", "L0_xattn_ln1_b", "L0_xattn_a1_li1_b", "L0_xattn_a1_li3_b",
        "L0_xattn_ln2_g", "L0_xattn_ln2_b", "L0_xattn_a2_li1_b", "L0_xattn_a2_li3_b",
        "L1_xattn_bo", "L1_ffn_ln1_g", "L1_ffn_ln1_b", "L1_ffn_ln2_g", "L1_ffn_ln2_b"]
COLS = ["L0_xattn_a1_lnx_g", "L0_xattn_a1_lnx_b", "L0_xattn_a1_lny_g", "L0_xattn_a1_lny_b",
        "L0_xattn_a1_ln3_g", "L0_xattn_a1_ln3_b",
        "L0_xattn_a2_lnx_g", "L0_xattn_a2_lnx_b", "L0_xattn_a2_lny_g", "L0_xattn_a2_lny_b",
        "L0_xattn_a2_ln3_g", "L0_xattn_a2_ln3_b",
        "L0_ffn_ln1_g", "L0_ffn_ln1_b", "L0_ffn_ln2_g", "L0_ffn_ln2_b"]
COL_A1_LI2 = len(COLS)
COL_A2_LI2 = COL_A1_LI2 + FCH
COL_B1 = COL_A2_LI2 + FCH
NCOLS = COL_B1 + EXPERTS * FCH


class Count:

    def __init__(self):
        self.n = 0

    def up(self, k=1):
        self.n += k
        return self.n


def build_program(nc, d, out):
    f32, f32r, i32 = mybir.dt.float32, mybir.dt.float32r, mybir.dt.int32
    ALU, ACT, AX = mybir.AluOpType, mybir.ActivationFunctionType, mybir.AxisListType

    with ExitStack() as ctx:
        def sb(name, shape, dt=f32):
            return ctx.enter_context(nc.sbuf_tensor(name, shape, dt))

        def sem(name):
            return ctx.enter_context(nc.semaphore(name))

        PS = ctx.enter_context(nc.psum_tensor("PS", [128, 8, 512], f32))

        ident = sb("ident", [128, 128])
        ones = sb("ones", [128, 1])
        mask_blocks = sb("mask_blocks", [TP, TP])
        mask_later = sb("mask_later", [TP, TP])
        mask_causal = sb("mask_causal", [TP, TP])
        heads4 = sb("heads4", [128, 4])
        heads16 = sb("heads16", [128, 16])
        rows = sb("rows", [TP, len(ROWS), C])
        cols = sb("cols", [128, NCOLS])

        x_in = sb("x_in", [TP, TILES, C])
        hat = sb("hat", [TP, TILES, C])
        ta = sb("ta", [TP, TILES, C])
        tb = sb("tb", [TP, TILES, C])
        tc_ = sb("tc_", [TP, TILES, C])
        stats = sb("stats", [TP, TILES, 6])
        mv = sb("mv", [TP, TILES, 2])
        rs = sb("rs", [TP, 4, TILES])
        xn = sb("xn", [128, TOK])
        yn = sb("yn", [128, TOK])
        wA = sb("wA", [128, 6 * 512])
        wq2 = sb("wq2", [128, 512])
        li2x = sb("li2x", [128, 3 * 512])
        wkpad = sb("wkpad", [128, HEADS, 128])
        wvpad = sb("wvpad", [128, HEADS, 128])
        attn_w = sb("attn_w", [128, C])
        gate0 = sb("gate0", [128, EXPERTS])
        gate1 = sb("gate1", [128, EXPERTS])
        b2 = sb("b2", [EXPERTS, C])
        lg = sb("lg", [TP, TILES, EXPERTS])
        top = sb("top", [TP, TILES, 8])
        gt = sb("gt", [TP, 4, TILES, EXPERTS])
        comb = sb("comb", [TP, EXPERTS, TILES])
        cw = sb("cw", [TP, 2, TILES])
        gs = sb("gs", [TP, TILES])
        combT = sb("combT", [EXPERTS, TOK])
        qp = sb("qp", [128, BATCH, HEADS, SEQ])
        cmean = sb("cmean", [KP, BATCH * KT])
        crstd = sb("crstd", [KP, BATCH * KT])
        cst = sb("cst", [KP, KT, 6])
        ctmp = sb("ctmp", [KP, 2, BATCH * KT])
        kA = sb("kA", [128, 2, KEYS], f32r)
        kB = sb("kB", [128, 2, KEYS], f32r)
        qA = sb("qA", [128, 2, HQ], f32r)
        qB = sb("qB", [128, 2, HQ], f32r)
        mx = sb("mx", [128, HQ_TILES, SPANS])
        negm = sb("negm", [128, HQ_TILES])
        mhr = sb("mhr", [128, HQ_TILES], f32r)
        mhl = sb("mhl", [128, HQ_TILES, 2])
        rsum = sb("rsum", [TP, 2, 16])
        rneg = sb("rneg", [TP, 2, 16])
        with ExitStack() as first:
            def sb1(name, shape, dt=f32):
                return first.enter_context(nc.sbuf_tensor(name, shape, dt))

            we = sb1("we", [128, 2, 3 * 512])
            big1 = sb1("big1", [128, 8, TOK])
            big2 = sb1("big2", [128, 4, TOK])
            arena = sb1("arena", [128, 9344])

        CT = sb("CT", [KP, KT, CTX])
        ostage = sb("ostage", [128, HQ])
        rden = sb("rden", [64, HQ])
        sb("unused", [128, 512])
        P = sb("P", [KP, 2, HQ])
        Ph = sb("Ph", [KP, 2, HQ], f32r)
        Pl = sb("Pl", [KP, 2, HQ], f32r)
        XX = sb("XX", [KP, KT, 128])
        Y = sb("Y", [128, KEYS])
        Wh = sb("Wh", [KP, 2, KT, 128], f32r)
        Wl = sb("Wl", [KP, 2, KT, 128], f32r)

        def part(off, n):
            return arena[:, off:off + n]

        S = part(0, 2 * 16 * TP).rearrange("p (b h k) -> p b h k", b=2, h=16)[0:TP]
        Kblk = part(3584, 16 * TP).rearrange("p (c h k) -> p c h k", c=4, h=4)
        PT = part(5376, 2 * 4 * TP).rearrange("p (b h q) -> p b h q", b=2, h=4)[0:TP]
        VT = part(6272, TILES * 512).rearrange("p (t n) -> p t n", t=TILES)[0:TP]
        OT = part(8320, 2 * 512).rearrange("p (b n) -> p b n", b=2)[0:TP]
        act = part(0, 2 * FCH * TOK).rearrange("p (b c n) -> p b c n", b=2, c=FCH)
        sg = part(3584, 2 * TOK).rearrange("p (b n) -> p b n", b=2)

        craw = qp[:, :, :, :].rearrange("p b h q -> p (b h q)")[0:KP, 0:BATCH * KT * CTX] \
            .rearrange("p (t c) -> p t c", c=CTX)

        w_q1, w_k1, w_v1 = wA[:, 0:512], wA[:, 512:1024], wA[:, 1024:1536]
        w_a1 = [wA[:, 1536:2048], wA[:, 2048:2560], wA[:, 2560:3072]]
        w_a2 = [li2x[:, 0:512], li2x[:, 512:1024], li2x[:, 1024:1536]]
        w_qL1 = wA[:, 0:1024]
        w_oL1 = wA[:, 1024:2048].rearrange("p (c n) -> p c n", c=8)
        w_qkvL1 = wA[:, 2048:2048 + 3 * C].rearrange("p (j n) -> p j n", j=3)

        x_loaded = sem("x_loaded")
        params_loaded = sem("params_loaded")
        wA_loaded = sem("wA_loaded")
        wB_loaded = sem("wB_loaded")
        craw_loaded = sem("craw_loaded")
        wL1_loaded = sem("wL1_loaded")
        pads_loaded = sem("pads_loaded")
        expert_loaded = [sem("expert_loaded_0"), sem("expert_loaded_1")]
        ct_loaded = sem("ct_loaded")
        y_loaded = sem("y_loaded")
        v_loaded = sem("v_loaded")
        out_stored = sem("out_stored")
        consts_step = sem("consts_step")
        dve_step = sem("dve_step")
        act_step = sem("act_step")
        pads_zeroed = sem("pads_zeroed")
        stats_ready = sem("stats_ready")
        tm_ready = sem("tm_ready")
        fmT_ps = sem("fmT_ps")
        fm_ready = sem("fm_ready")
        lin_ps = sem("lin_ps")
        lin_moved = sem("lin_moved")
        proj_ps = sem("proj_ps")
        kblk_ready = sem("kblk_ready")
        s_ps = sem("s_ps")
        s_read = sem("s_read")
        s_shifted = sem("s_shifted")
        exp_done = sem("exp_done")
        sum_done = sem("sum_done")
        masked = sem("masked")
        pt_ps = sem("pt_ps")
        pt_moved = sem("pt_moved")
        o_sa_ps = sem("o_sa_ps")
        o_sa_ready = sem("o_sa_ready")
        oT_ps = sem("oT_ps")
        oT_moved = sem("oT_moved")
        gate_in = sem("gate_in")
        gate_exp = sem("gate_exp")
        comb_ready = sem("comb_ready")
        combT_ps = sem("combT_ps")
        combT_ready = sem("combT_ready")
        g_ps = sem("g_ps")
        g_moved = sem("g_moved")
        mul_done = sem("mul_done")
        dn_ps = sem("dn_ps")
        dn_added = sem("dn_added")
        xx_ready = sem("xx_ready")
        xxT_ps = sem("xxT_ps")
        xx_half = sem("xx_half")
        centred = sem("centred")
        w_filled = sem("w_filled")
        vh_ready = sem("vh_ready")
        y_ready = sem("y_ready")
        kab_ready = sem("kab_ready")
        v_ready = sem("v_ready")
        qs_ready = sem("qs_ready")
        sc_ps = sem("sc_ps")
        sc_max = sem("sc_max")
        negm_ready = sem("negm_ready")
        mrow_ps = sem("mrow_ps")
        mrow_moved = sem("mrow_moved")
        st_ps = sem("st_ps")
        p_ready = sem("p_ready")
        pf_ready = sem("pf_ready")
        pl_ready = sem("pl_ready")
        ph_used = sem("ph_used")
        pl_used = sem("pl_used")
        o_moved = sem("o_moved")
        o_out = sem("o_out")
        u_ready = sem("u_ready")

        block = ctx.enter_context(nc.Block())

        LIN_PREP0 = 12 + 4
        LIN_U0 = LIN_PREP0 + 4 + HEADS
        LIN_PREP1 = LIN_U0 + 4 + 4
        LIN_U1 = LIN_PREP1 + 8 + HEADS

        def row(name, t=TILES):
            v = rows[:, ROWS.index(name):ROWS.index(name) + 1, :]
            return v.broadcast_to([TP, t, C])

        def col(name):
            return cols[:, COLS.index(name):COLS.index(name) + 1]

        def static_and_loop(engine, step, last):
            step(0, 0, True)
            with engine.Fori(0, (last - 1) // 2) as i:
                step(2 * i + 1, 1, True)
                step(2 * i + 2, 0, True)
            step(last, last % 2, False)

        @block.sync
        def _(sp):
            sp.dma_start(x_in[:, :, :], d["x"].rearrange("(t p) c -> p t c", p=TP)).then_inc(x_loaded, 16)
            sp.dma_start(rows[:, :, :], d["rows"].partition_broadcast(TP)).then_inc(params_loaded, 16)
            sp.dma_start(cols[:, :], d["cols"]).then_inc(params_loaded, 16)
            for dst, name in ((w_q1, "a1_wq"), (w_k1, "a1_wk"), (w_v1, "a1_wv"), (w_a1[1], "a1_li2")):
                sp.dma_start(dst, d[name]).then_inc(wA_loaded, 16)
            for dst, name in ((w_a1[0], "a1_li1"), (w_a1[2], "a1_li3")):
                sp.dma_start(dst.rearrange("p (c n) -> p c n", c=4),
                             d[name].rearrange("(c p) n -> p c n", p=128)).then_inc(wA_loaded, 16)
            sp.dma_start(craw, d["ctx"].rearrange("b (p k) c -> p b k c", p=KP)).then_inc(craw_loaded, 16)
            sp.dma_start(wq2[:, :], d["a2_wq"]).then_inc(wB_loaded, 16)
            sp.dma_start(w_a2[1], d["a2_li2"]).then_inc(wB_loaded, 16)
            for dst, name in ((w_a2[0], "a2_li1"), (w_a2[2], "a2_li3")):
                sp.dma_start(dst.rearrange("p (c n) -> p c n", c=4),
                             d[name].rearrange("(c p) n -> p c n", p=128)).then_inc(wB_loaded, 16)
            sp.dma_start(attn_w[:, :], d["attn_w"]).then_inc(wB_loaded, 16)
            sp.dma_start(gate0[:, :], d["gate0"]).then_inc(wB_loaded, 16)
            sp.dma_start(gate1[:, :], d["gate1"]).then_inc(wB_loaded, 16)
            sp.dma_start(b2[:, :], d["b2"]).then_inc(wB_loaded, 16)

            def load_pads(call, D, wk, wv):
                per = 128 // D
                sp.wait_ge(pads_zeroed, 2 * (call + 1))
                for r in range(per):
                    src = wk[r:HEADS:per].rearrange("g d c -> d g c")
                    dst = wkpad[r * D:(r + 1) * D, r:HEADS:per, :]
                    for j in range(2):
                        sp.dma_start(dst[:, :, j * CTX:(j + 1) * CTX], src).then_inc(pads_loaded, 16)
                    src = wv[r:HEADS:per].rearrange("g c d -> c g d")
                    dst = wvpad[0:CTX, r:HEADS:per, :]
                    sp.dma_start(dst[:, :, r * D:(r + 1) * D], src).then_inc(pads_loaded, 16)

            load_pads(0, 32, d["a2_wk"], d["a2_wv"])

            def load_ct(n, par, has_next):
                sp.wait_ge(xx_ready, n + 1)
                sp.dma_start(CT[:, :, :], d["ctx"][bass.ds(n + 1, 1)].rearrange("b (p k) c -> p (b k) c", p=KP)) \
                    .then_inc(ct_loaded, 16)

            sp.dma_start(CT[:, :, :], d["ctx"][0:1].rearrange("b (p k) c -> p (b k) c", p=KP)).then_inc(ct_loaded, 16)
            with sp.Fori(0, BATCH - 1) as i:
                load_ct(i, 0, True)

            sp.wait_ge(proj_ps, 2)
            sp.dma_start(w_qL1, d["L1_Wq"]).then_inc(wL1_loaded, 16)
            sp.dma_start(w_oL1, d["L1_Wo"].rearrange("(c p) n -> p c n", p=128)).then_inc(wL1_loaded, 16)
            for j, name in enumerate(("L1f_Wq", "L1f_Wk", "L1f_Wv")):
                sp.dma_start(w_qkvL1[:, j, :], d[name]).then_inc(wL1_loaded, 16)

            def load_expert0(e, par):
                for j, name in enumerate(("gp", "up", "dp")):
                    sp.dma_start(we[:, par, j * 512:(j + 1) * 512], d[name][bass.ds(e, 1)].rearrange("a p n -> (a p) n")) \
                        .then_inc(expert_loaded[par], 16)

            def load_expert1(e, par):
                for j, name in enumerate(("W1", "W2")):
                    sp.dma_start(we[:, par, j * 512:(j + 1) * 512], d[name][bass.ds(e, 1)].rearrange("a p n -> (a p) n")) \
                        .then_inc(expert_loaded[par], 16)

            def load_experts(call, load):
                sp.wait_ge(u_ready, call + 1)
                load(0, 0)
                load(1, 1)
                with sp.Fori(0, EXPERTS // 2 - 1) as i:
                    for par in range(2):
                        sp.wait_ge(dn_ps, 2 * i + EXPERTS * call + par + 1)
                        load(2 * i + 2 + par, par)

            load_experts(0, load_expert0)
            load_pads(1, 64, d["L1_Wk"], d["L1_Wv"])

            def load_kv(n):
                sp.wait_ge(kab_ready, n + BATCH)
                for j in range(2):
                    sp.dma_start(Y[j * CTX:(j + 1) * CTX, :], d["ctxT"][bass.ds(n, 1)].rearrange("a c k -> (a c) k")) \
                        .then_inc(y_loaded, 16)
                sp.wait_ge(v_ready, n + BATCH)
                sp.dma_start(XX[:, :, 0:CTX], d["ctx"][bass.ds(n, 1)].rearrange("b (p k) c -> p (b k) c", p=KP)) \
                    .then_inc(v_loaded, 16)

            sp.wait_ge(dn_ps, EXPERTS)
            with sp.Fori(0, BATCH) as i:
                load_kv(i)
            load_experts(1, load_expert1)
            sp.wait_ge(tm_ready, 10)
            sp.dma_start(out.rearrange("(t p) c -> p t c", p=TP), x_in[:, :, :]).then_inc(out_stored, 16)
            sp.wait_ge(out_stored, 16)

        @block.gpsimd
        def _(pool):
            n = Count()

            def seq(ins):
                ins.then_inc(consts_step, 1)
                pool.wait_ge(consts_step, n.up())

            def zero_pads(call):
                pool.memset(wkpad[:, :, :], 0.0).then_inc(pads_zeroed, 1)
                pool.wait_ge(pads_zeroed, 2 * call + 1)
                pool.memset(wvpad[:, :, :], 0.0).then_inc(pads_zeroed, 1)
                pool.wait_ge(pads_zeroed, 2 * call + 2)

            seq(pool.memset(ones[:, :], 1.0))
            seq(pool.memset(ident[:, :], 0.0))
            seq(pool.affine_select(out=ident[:, :], in_=ident[:, :], compare_op=ALU.not_equal, fill=1.0,
                                   base=0, pattern=[[-1, 128]], channel_multiplier=1))
            seq(pool.memset(mask_blocks[:, :], 0.0))
            seq(pool.affine_select(out=mask_blocks[:, 0:SEQ], in_=mask_blocks[:, 0:SEQ], compare_op=ALU.is_ge,
                                   fill=NEG, base=SEQ - 1, pattern=[[0, SEQ]], channel_multiplier=-1))
            seq(pool.affine_select(out=mask_blocks[:, SEQ:TP], in_=mask_blocks[:, SEQ:TP], compare_op=ALU.is_ge,
                                   fill=NEG, base=-SEQ, pattern=[[0, SEQ]], channel_multiplier=1))
            seq(pool.memset(mask_later[:, :], 1.0))
            seq(pool.affine_select(out=mask_later[:, :], in_=mask_later[:, :], compare_op=ALU.is_gt, fill=0.0,
                                   base=0, pattern=[[1, TP]], channel_multiplier=-1))
            seq(pool.affine_select(out=mask_causal[:, :], in_=mask_blocks[:, :], compare_op=ALU.is_ge, fill=NEG,
                                   base=0, pattern=[[-1, TP]], channel_multiplier=1))
            for m, w, k in ((heads4, 32, 4), (heads16, 8, 16)):
                seq(pool.memset(m[:, :], 1.0))
                seq(pool.affine_select(out=m[:, :], in_=m[:, :], compare_op=ALU.is_ge, fill=0.0,
                                       base=0, pattern=[[-w, k]], channel_multiplier=1))
                seq(pool.affine_select(out=m[:, :], in_=m[:, :], compare_op=ALU.is_ge, fill=0.0,
                                       base=w - 1, pattern=[[w, k]], channel_multiplier=-1))
            zero_pads(0)
            seq(pool.memset(kB[64:128, :, :].bitcast(f32), 0.0))
            seq(pool.memset(kB[64:66, :, :].bitcast(f32), 1.0))
            seq(pool.memset(qB[64:128, :, :].bitcast(f32), 0.0))

            def self_attention(call, heads, chunk_of):
                pool.wait_ge(lin_moved, 12 if call == 0 else LIN_U1 + 8 + 3)
                for p in range(TILES):
                    for c in range(4):
                        if p >= 1:
                            pool.wait_ge(s_ps, 16 * call + 4 * (p - 1) + c + 1)
                        k = big2[:, chunk_of(c), p * TP:(p + 1) * TP].unsqueeze(1).broadcast_to([128, 4, TP])
                        m = heads[:, :] if call == 0 else heads[:, 4 * c:4 * c + 4]
                        pool.tensor_tensor(Kblk[:, c, :, :], k, m.unsqueeze(2).broadcast_to([128, 4, TP]), ALU.mult) \
                            .then_inc(kblk_ready, 1)
                    if call == 0 and p >= 1:
                        mask_pair(p - 1)
                if call == 0:
                    mask_pair(TILES - 1)

            def mask_pair(p):
                pool.wait_ge(sum_done, p + 1)
                pool.tensor_tensor(S[:, p % 2], S[:, p % 2], mask_later[:, :].unsqueeze(1).broadcast_to([TP, 16, TP]),
                                   ALU.mult).then_inc(masked, 1)

            self_attention(0, heads4, lambda c: c)

            def normalise(nb, parts=(0, 1)):
                for part_ in parts:
                    if part_ == 0:
                        pool.wait_ge(ct_loaded, 16 * nb + 16)
                        mean = cmean[:, bass.ds(nb * KT, KT)].unsqueeze(2).broadcast_to([KP, KT, CTX])
                        pool.tensor_tensor(CT[:, :, :], CT[:, :, :], mean, ALU.subtract).then_inc(centred, 1)
                    else:
                        pool.wait_ge(centred, nb + 1)
                        if not isinstance(nb, int) or nb > 0:
                            pool.wait_ge(xxT_ps, SPANS * nb)
                            pool.wait_ge(v_ready, nb)
                        rstd = crstd[:, bass.ds(nb * KT, KT)].unsqueeze(2).broadcast_to([KP, KT, CTX])
                        pool.tensor_tensor(XX[:, :, 0:CTX], CT[:, :, :], rstd, ALU.mult).then_inc(xx_half, 1)

            def low_part(b, call, kt):
                g0 = (b + BATCH * call) * KT
                pool.wait_ge(pf_ready, g0 + kt + 1)
                if call or not isinstance(b, int) or b or kt >= 2:
                    pool.wait_ge(pl_used, g0 + kt - 1)
                pool.tensor_tensor(Pl[:, kt % 2, :], P[:, kt % 2, :], Ph[:, kt % 2, :], ALU.subtract) \
                    .then_inc(pl_ready, 1)

            def cross(call):
                def step(b, par, has_next, has_third=False):
                    for kt in range(KT):
                        low_part(b, call, kt)
                        if has_third and kt in (5, 6):
                            normalise(b + 2, parts=(kt - 5,))

                fill_value = pool.memset(Wh[:, :, :, CTX:128].bitcast(f32), 1.0)
                fill_value.then_inc(w_filled, 1)
                pool.wait_ge(w_filled, 2 * call + 1)
                pool.memset(Wl[:, :, :, CTX:128].bitcast(f32), 0.0).then_inc(w_filled, 1)
                pool.wait_ge(w_filled, 2 * call + 2)
                if call == 0:
                    normalise(0)
                    normalise(1)
                    step(0, 0, True, True)
                    with pool.Fori(0, BATCH // 2 - 2) as i:
                        step(2 * i + 1, 1, True, True)
                        step(2 * i + 2, 0, True, True)
                    for b in range(BATCH - 3, BATCH):
                        step(b, b % 2, b + 1 < BATCH, b + 2 < BATCH)
                else:
                    static_and_loop(pool, step, BATCH - 1)

            pool.wait_ge(stats_ready, 1)
            pool.wait_ge(proj_ps, 1)
            cross(0)

            pool.wait_ge(lin_ps, LIN_U0 + 4)
            zero_pads(1)

            pool.wait_ge(dn_ps, EXPERTS)
            cross(1)

            self_attention(1, heads16, lambda c: 0)

        @block.scalar
        def _(sc):
            fmT, lin, pts = Count(), Count(), Count()

            def move_fm(outs):
                sc.wait_ge(fmT_ps, fmT.up())
                for dst, g, b in outs:
                    if g is None:
                        ins = sc.activation(dst, PS[:, 7, 0:TOK], ACT.Identity)
                    else:
                        ins = sc.activation(dst, PS[:, 7, 0:TOK], ACT.Identity, bias=col(b), scale=col(g))
                ins.then_inc(fm_ready, 1)

            def move_lin(dst, n, func=ACT.Identity, bias=0.0, parts=128, view=None):
                sc.wait_ge(lin_ps, lin.up())
                src = PS[0:parts, (lin.n - 1) % 7, 0:n]
                sc.activation(dst, view(src) if view else src, func, bias=bias).then_inc(lin_moved, 1)

            def self_attention(call):
                def exp(p):
                    sc.wait_ge(s_shifted, TILES * call + p + 1)
                    sc.activation(S[:, p % 2], S[:, p % 2], ACT.Exp).then_inc(exp_done, 1)

                def values(p):
                    for c in range(4):
                        sc.wait_ge(pt_ps, pts.up())
                        sc.activation(PT[:, c % 2], PS[0:TP, 4 + c % 2, 0:4 * TP].rearrange("p (h q) -> p h q", h=4),
                                      ACT.Identity).then_inc(pt_moved, 1)
                    if call == 0:
                        sc.wait_ge(oT_ps, p + 1)
                        sc.activation(big1[:, 0:4, p * TP:(p + 1) * TP],
                                      PS[:, 7, 0:4 * TP].rearrange("p (c q) -> p c q", c=4), ACT.Identity) \
                            .then_inc(oT_moved, 1)

                exp(0)
                for p in range(TILES):
                    if p + 1 < TILES:
                        exp(p + 1)
                    values(p)

            def mlp(pre, c0):
                move_fm([(xn[:, :], pre + "ln3_g", pre + "ln3_b")])
                for c in range(FCH):
                    move_lin(big2[:, c, :], TOK, ACT.Gelu, cols[:, c0 + c:c0 + c + 1])

            def queries(nq):
                for c in range(nq):
                    move_lin(big1[:, c, :], TOK)
                for h in range(HEADS):
                    move_lin(qp[:, :, h, :], TOK, view=lambda s: s.rearrange("p (b q) -> p b q", b=BATCH))

            def cross(call, scale):
                def fills(nb, which=range(SPANS)):
                    for f in which:
                        sc.wait_ge(xxT_ps, SPANS * nb + f + 1)
                        sc.activation(Y[:, f * SPAN:(f + 1) * SPAN], PS[:, f % 2, 0:SPAN], ACT.Identity,
                                      bias=col("L0_xattn_a2_lny_b"), scale=col("L0_xattn_a2_lny_g")) \
                            .then_inc(y_ready, 1)

                def double(nb):
                    sc.wait_ge(xx_half, nb + 1)
                    sc.activation(XX[:, :, CTX:128], XX[:, :, 0:CTX], ACT.Identity).then_inc(xx_ready, 1)

                def values_high(nb, par):
                    g = nb + BATCH * call
                    if not isinstance(nb, int) or nb >= 2 or call:
                        sc.wait_ge(pl_used, KT * (g - 1))
                    if call:
                        sc.wait_ge(v_loaded, 16 * nb + 16)
                    else:
                        sc.wait_ge(xx_half, nb + 1)
                    sc.activation(Wh[:, par, :, 0:CTX], XX[:, :, 0:CTX], ACT.Identity).then_inc(vh_ready, 1)

                def move_output(b):
                    g = b + BATCH * call
                    sc.wait_ge(pl_used, KT * (g + 1))
                    if call or not isinstance(b, int) or b:
                        sc.wait_ge(o_out, g)
                    sc.activation(ostage[:, :].rearrange("p (j n) -> p j n", j=2), PS[:, 6:8, 0:HALF],
                                  ACT.Identity).then_inc(o_moved, 1)

                def step(b, par, has_next, has_third=False):
                    g0 = (b + BATCH * call) * KT
                    for kt in range(KT):
                        sc.wait_ge(st_ps, g0 + kt + 1)
                        if call or not isinstance(b, int) or b or kt >= 2:
                            sc.wait_ge(pl_ready, g0 + kt - 1)
                            sc.wait_ge(ph_used, g0 + kt - 1)
                        bank = 2 + 2 * (kt % 2)
                        for dst, signal in ((Ph, p_ready), (P, pf_ready)):
                            sc.activation(dst[:, kt % 2, :].rearrange("p (j n) -> p j n", j=2),
                                          PS[0:KP, bank:bank + 2, 0:HALF], ACT.Exp, scale=scale).then_inc(signal, 1)
                        if kt == 0 and (not isinstance(b, int) or b):
                            move_output(b - 1)
                        if kt == 0 and has_next and call == 0:
                            sc.wait_ge(kab_ready, b + 1)
                            fills(b + 1, (0, 1))
                        if kt == 1 and has_next and call == 0:
                            fills(b + 1, (2,))
                        if kt == 2 and has_next:
                            values_high(b + 1, 1 - par)
                        if kt == 9 and has_third and call == 0:
                            double(b + 2)

                sc.wait_ge(w_filled, 2 * call + 2)
                if call == 0:
                    double(0)
                    values_high(0, 0)
                    fills(0)
                    double(1)
                    step(0, 0, True, True)
                    with sc.Fori(0, BATCH // 2 - 2) as i:
                        step(2 * i + 1, 1, True, True)
                        step(2 * i + 2, 0, True, True)
                    for b in range(BATCH - 3, BATCH):
                        step(b, b % 2, b + 1 < BATCH, b + 2 < BATCH)
                else:
                    values_high(0, 0)
                    static_and_loop(sc, step, BATCH - 1)
                move_output(BATCH - 1)

            sc.wait_ge(params_loaded, 32)
            move_fm([(xn[:, :], "L0_xattn_a1_lnx_g", "L0_xattn_a1_lnx_b"),
                     (yn[:, :], "L0_xattn_a1_lny_g", "L0_xattn_a1_lny_b")])
            for c in range(4):
                move_lin(big1[:, c, :], TOK)
            for c in range(4):
                move_lin(big2[:, c, :], TOK)
            for p in range(TILES):
                move_lin(VT[:, p, :], 512, parts=TP)
            self_attention(0)
            mlp("L0_xattn_a1_", COL_A1_LI2)

            move_fm([(xn[:, :], "L0_xattn_a2_lnx_g", "L0_xattn_a2_lnx_b")])
            sc.wait_ge(stats_ready, 1)
            queries(4)
            cross(0, 32 ** -0.5)
            for c in range(4):
                move_lin(big1[:, c, :], TOK)
            mlp("L0_xattn_a2_", COL_A2_LI2)

            def gate(call):
                sc.wait_ge(gate_in, call + 1)
                sc.activation(gt[:, 0], gt[:, 0], ACT.Exp).then_inc(gate_exp, 1)

            move_fm([(xn[:, :], "L0_ffn_ln1_g", "L0_ffn_ln1_b")])
            move_fm([(xn[:, :], "L0_ffn_ln2_g", "L0_ffn_ln2_b")])
            gate(0)

            def silu(e, par, has_next):
                for c in range(FCH):
                    m = e * FCH + c
                    sc.wait_ge(g_ps, m + 1)
                    if not isinstance(e, int) or m >= 2:
                        sc.wait_ge(mul_done, m - 1)
                    sc.activation(sg[:, c % 2, :], PS[:, 2 + c % 2, 0:TOK], ACT.Silu).then_inc(g_moved, 1)

            static_and_loop(sc, silu, EXPERTS - 1)

            move_fm([(xn[:, :], None, None)])
            queries(8)
            cross(1, 64 ** -0.5)
            for c in range(8):
                move_lin(big1[:, c, :], TOK)

            move_fm([(xn[:, :], None, None)])
            move_lin(big1[:, 0, :], TOK)
            move_lin(big2[:, 0, :], TOK)
            move_lin(VT[:, :, 0:C], 512, parts=TP, view=lambda s: s.rearrange("p (t n) -> p t n", t=TILES))
            self_attention(1)

            move_fm([(xn[:, :], None, None)])
            gate(1)

            def relu(e, par, has_next):
                for c in range(FCH):
                    m = e * FCH + c
                    sc.wait_ge(g_ps, m + 1 + EXPERTS * FCH)
                    if not isinstance(e, int) or e >= 2:
                        sc.wait_ge(dn_ps, e - 1 + EXPERTS)
                    sc.activation(act[:, par, c, :], PS[:, 2 + c % 2, 0:TOK], ACT.Relu,
                                  bias=cols[:, bass.ds(COL_B1 + m, 1)]).then_inc(g_moved, 1)

            static_and_loop(sc, relu, EXPERTS - 1)

        @block.vector
        def _(v):
            n, proj = Count(), Count()

            def seq(ins):
                ins.then_inc(dve_step, 1)
                v.wait_ge(dve_step, n.up())

            def rsqrt(y, var, tmp):
                seq(v.tensor_scalar(y.bitcast(i32), var.bitcast(i32), -0.5, 1597463007.0, ALU.mult, ALU.add))
                for _ in range(4):
                    seq(v.tensor_tensor(tmp, y, y, ALU.mult))
                    seq(v.scalar_tensor_tensor(tmp, tmp, -0.5, var, ALU.mult, ALU.mult))
                    seq(v.scalar_tensor_tensor(y, tmp, 1.5, y, ALU.add, ALU.mult))

            def layernorm(src, dst):
                for t in range(TILES):
                    ins = v.bn_stats(stats[:, t, :], src[:, t, :])
                seq(ins)
                for t in range(TILES):
                    ins = v.bn_aggr(mv[:, t, :], stats[:, t, :])
                seq(ins)
                seq(v.tensor_scalar(rs[:, 0, :], mv[:, :, 1], EPS, None, ALU.add))
                rsqrt(rs[:, 1, :], rs[:, 0, :], rs[:, 2, :])
                for t in range(TILES):
                    ins = v.tensor_scalar(dst[:, t, :], src[:, t, :], mv[:, t, 0:1], rs[:, 1, t:t + 1],
                                          ALU.subtract, ALU.mult)
                seq(ins)

            def tt(dst, a, b, op):
                seq(v.tensor_tensor(dst, a, b, op))

            def affine(dst, src, g, b):
                tt(dst, src, row(g), ALU.mult)
                tt(dst, dst, row(b), ALU.add)

            def proj_in():
                v.wait_ge(proj_ps, proj.up())
                return PS[0:TP, 0, :].rearrange("p (t c) -> p t c", t=TILES)

            def ready():
                v.engine_nop().then_inc(tm_ready, 1)

            def self_attention(call, scale, mask, D):
                def shift(p):
                    if p >= 2 and call == 0:
                        v.wait_ge(pt_ps, 16 * call + 4 * (p - 1))
                    elif p >= 2:
                        v.wait_ge(pt_ps, 16 * call + 4 * (p - 1))
                    for c in range(4):
                        v.wait_ge(s_ps, 16 * call + 4 * p + c + 1)
                        ins = v.scalar_tensor_tensor(
                            S[:, p % 2, 4 * c:4 * c + 4, :],
                            PS[0:TP, c, 0:4 * TP].rearrange("p (h k) -> p h k", h=4), scale,
                            mask[:, :].unsqueeze(1).broadcast_to([TP, 4, TP]), ALU.mult, ALU.add)
                        ins.then_inc(s_read, 1)
                    v.wait_ge(s_read, 16 * call + 4 * p + 4)
                    seq(v.tensor_reduce(rneg[:, p % 2, :], S[:, p % 2], AX.X, ALU.max))
                    v.tensor_tensor(S[:, p % 2], S[:, p % 2],
                                    rneg[:, p % 2, :].unsqueeze(2).broadcast_to([TP, 16, TP]),
                                    ALU.subtract).then_inc(s_shifted, 1)

                def sums(p):
                    v.wait_ge(exp_done, TILES * call + p + 1)
                    v.tensor_reduce(rsum[:, p % 2, :], S[:, p % 2], AX.X, ALU.add).then_inc(sum_done, 1)
                    v.wait_ge(sum_done, TILES * call + p + 1)
                    seq(v.reciprocal(rsum[:, p % 2, :], rsum[:, p % 2, :]))

                def output(p):
                    v.wait_ge(o_sa_ps, TILES * call + p + 1)
                    if call == 0 and p >= 2:
                        v.wait_ge(oT_ps, p - 1)
                    dst = OT[:, p % 2, :] if call == 0 else tb[:, p, :]
                    v.tensor_tensor(dst.rearrange("p (h e) -> p h e", e=D),
                                    PS[0:TP, 6, 0:16 * D].rearrange("p (h e) -> p h e", e=D),
                                    rsum[:, p % 2, :].unsqueeze(2).broadcast_to([TP, 16, D]),
                                    ALU.mult).then_inc(o_sa_ready, 1)

                shift(0)
                for p in range(TILES):
                    if p + 1 < TILES:
                        shift(p + 1)
                    sums(p)
                    output(p)

            def mlp(b1, b3, skip):
                tt(tb[:, :, :], proj_in(), tb[:, :, :], ALU.add)
                layernorm(tb, hat)
                ready()
                tt(tc_[:, :, :], tb[:, :, :], row(b3), ALU.add)
                tt(tc_[:, :, :], tc_[:, :, :], skip[:, :, :], ALU.add)
                tt(tc_[:, :, :], proj_in(), tc_[:, :, :], ALU.add)

            def cross(call):
                def split_queries(nb, par):
                    if call or not isinstance(nb, int) or nb >= 2:
                        v.wait_ge(st_ps, KT * (nb + BATCH * call - 1))
                    q = qp[:, bass.ds(nb, 1)].rearrange("p a h q -> p (a h q)")
                    v.tensor_copy(qA[:, par, :], q).then_inc(qs_ready, 1)
                    v.wait_ge(qs_ready, 2 * (nb + BATCH * call) + 1)
                    v.tensor_tensor(qB[0:64, par, :], q[0:64], qA[0:64, par, :], ALU.subtract).then_inc(qs_ready, 1)

                def split_keys(nb, par):
                    g = nb + BATCH * call
                    if call == 0:
                        v.wait_ge(y_ready, SPANS * nb + SPANS)
                    else:
                        v.wait_ge(y_loaded, 32 * nb + 32)
                    v.tensor_copy(kA[:, par, :], Y[:, :]).then_inc(kstep, 1)
                    v.wait_ge(kstep, g + 1)
                    v.tensor_copy(kB[0:64, par, :], kA[0:64, par, :])
                    v.tensor_tensor(kA[64:128, par, :], Y[64:128, :], kA[64:128, par, :], ALU.subtract) \
                        .then_inc(kab_ready, 1)

                def values_low(nb, par):
                    v.wait_ge(vh_ready, nb + BATCH * call + 1)
                    v.tensor_tensor(Wl[:, par, :, 0:CTX], XX[:, :, 0:CTX], Wh[:, par, :, 0:CTX], ALU.subtract) \
                        .then_inc(v_ready, 1)

                def invert(b, j):
                    if j == 0:
                        v.wait_ge(o_moved, b + BATCH * call + 1)
                    v.reciprocal(rden[:, j * 128:(j + 1) * 128], ostage[64:128, j * 128:(j + 1) * 128]) \
                        .then_inc(o_step, 1)

                def divide(b):
                    g = b + BATCH * call
                    v.wait_ge(o_step, HQ_TILES * (g + 1))
                    v.tensor_tensor(qp[0:64, bass.ds(b, 1)].rearrange("p a h q -> p (a h q)"),
                                    ostage[0:64, :], rden[:, :], ALU.mult).then_inc(o_out, 1)

                def maxima(nb, par, out_b=None):
                    g = nb + BATCH * call
                    for j in range(HQ_TILES * SPANS):
                        v.wait_ge(sc_ps, g * HQ_TILES * SPANS + j + 1)
                        v.tensor_reduce(mx[:, j // SPANS, j % SPANS:j % SPANS + 1], PS[:, j % 2, 0:SPAN],
                                        AX.X, ALU.max).then_inc(sc_max, 1)
                        if out_b is not None and j % SPANS == 1:
                            invert(out_b, j // SPANS)
                    v.wait_ge(sc_max, (g + 1) * HQ_TILES * SPANS)
                    v.tensor_reduce(negm[:, :], mx[:, :, :], AX.X, ALU.max, negate=True).then_inc(negm_ready, 1)
                    v.wait_ge(negm_ready, 4 * g + 1)
                    v.tensor_copy(mhr[:, :], negm[:, :]).then_inc(negm_ready, 1)
                    v.wait_ge(negm_ready, 4 * g + 2)
                    v.tensor_copy(mhl[:, :, 0], mhr[:, :].bitcast(f32)).then_inc(negm_ready, 1)
                    v.tensor_tensor(mhl[:, :, 1], negm[:, :], mhr[:, :].bitcast(f32), ALU.subtract) \
                        .then_inc(negm_ready, 1)
                    v.wait_ge(mrow_ps, g + 1)
                    v.tensor_copy(qB[64:66, par, 0:512], PS[64:66, 0, 0:512])
                    v.tensor_copy(qB[64:66, par, 512:HQ], PS[64:66, 1, 0:HQ - 512]).then_inc(mrow_moved, 1)

                def step(b, par, has_next):
                    out_b = b - 1 if not isinstance(b, int) or b else None
                    if has_next:
                        split_queries(b + 1, 1 - par)
                        split_keys(b + 1, 1 - par)
                        values_low(b + 1, 1 - par)
                        maxima(b + 1, 1 - par, out_b)
                    elif out_b is not None:
                        for j in range(HQ_TILES):
                            invert(out_b, j)
                    if out_b is not None:
                        divide(out_b)

                v.wait_ge(lin_moved, (LIN_U0, LIN_U1)[call])
                split_queries(0, 0)
                split_keys(0, 0)
                values_low(0, 0)
                maxima(0, 0)
                static_and_loop(v, step, BATCH - 1)
                for j in range(HQ_TILES):
                    invert(BATCH - 1, j)
                divide(BATCH - 1)
                v.wait_ge(o_out, BATCH * (call + 1))

            kstep = sem("kstep")

            def gate(call):
                src = proj_in()
                seq(v.tensor_copy(lg[:, :, :], PS[0:TP, 0, 0:TILES * EXPERTS].rearrange("p (t e) -> p t e", t=TILES)))
                for t in range(TILES):
                    ins = v.max(top[:, t, :], lg[:, t, :])
                seq(ins)
                bc = lambda a: a.broadcast_to([TP, TILES, EXPERTS])
                v.tensor_tensor(gt[:, 0], lg[:, :, :], bc(top[:, :, 0:1]), ALU.subtract).then_inc(gate_in, 1)
                tt(gt[:, 1], lg[:, :, :], bc(top[:, :, 1:2]), ALU.is_gt)
                tt(gt[:, 2], lg[:, :, :], bc(top[:, :, 1:2]), ALU.is_equal)
                seq(v.tensor_reduce(gs[:, :], gt[:, 1], AX.X, ALU.add))
                tt(gt[:, 3, :, 0], gt[:, 2, :, 0], gs[:, :], ALU.add)
                for e in range(1, EXPERTS):
                    tt(gt[:, 3, :, e], gt[:, 3, :, e - 1], gt[:, 2, :, e], ALU.add)
                seq(v.scalar_tensor_tensor(gt[:, 2], gt[:, 3], 2.0, gt[:, 2], ALU.is_le, ALU.mult))
                tt(gt[:, 1], gt[:, 1], gt[:, 2], ALU.add)
                v.wait_ge(gate_exp, call + 1)
                tt(gt[:, 1], gt[:, 1], gt[:, 0], ALU.mult)
                seq(v.tensor_reduce(gs[:, :], gt[:, 1], AX.X, ALU.add))
                seq(v.reciprocal(gs[:, :], gs[:, :]))
                seq(v.tensor_tensor(comb[:, :, :].rearrange("p e t -> p t e"), gt[:, 1],
                                    gs[:, :].unsqueeze(2).broadcast_to([TP, TILES, EXPERTS]), ALU.mult))
                v.engine_nop().then_inc(comb_ready, 1)

            def add_expert(e, par, call):
                g = e + EXPERTS * call
                v.tensor_copy(cw[:, par, :], comb[:, bass.ds(e, 1), :].rearrange("p a t -> p (a t)")) \
                    .then_inc(cw_ready, 1)
                v.wait_ge(cw_ready, g + 1)
                v.wait_ge(dn_ps, g + 1)
                v.wait_ge(dn_added, g + call + 1)
                for t in range(TILES):
                    ins = v.scalar_tensor_tensor(tc_[:, t, :], PS[0:TP, 4 + par, t * C:(t + 1) * C],
                                                 cw[:, par, t:t + 1], tc_[:, t, :], ALU.mult, ALU.add)
                ins.then_inc(dn_added, 1)

            cw_ready = sem("cw_ready")
            o_step = sem("o_step")

            v.wait_ge(x_loaded, 16)
            layernorm(x_in, hat)
            layernorm(hat, hat)
            v.wait_ge(params_loaded, 32)
            affine(ta[:, :, :], hat[:, :, :], "L0_xattn_ln1_g", "L0_xattn_ln1_b")
            layernorm(ta, hat)
            ready()
            tt(tb[:, :, :], ta[:, :, :], row("L0_xattn_a1_li1_b"), ALU.add)

            v.wait_ge(craw_loaded, 16)
            for b in range(BATCH):
                for k in range(KT):
                    ins = v.bn_stats(cst[:, k, :], craw[:, b * KT + k, :])
                seq(ins)
                w = slice(b * KT, (b + 1) * KT)
                tt(cmean[:, w], cst[:, :, 1], cst[:, :, 4], ALU.add)
                tt(ctmp[:, 0, w], cst[:, :, 1], cst[:, :, 4], ALU.subtract)
                tt(ctmp[:, 1, w], cst[:, :, 2], cst[:, :, 5], ALU.add)
            seq(v.tensor_scalar(cmean[:, :], cmean[:, :], 0.5, None, ALU.mult))
            seq(v.tensor_scalar(ctmp[:, 0, :], ctmp[:, 0, :], 0.5, None, ALU.mult))
            tt(ctmp[:, 0, :], ctmp[:, 0, :], ctmp[:, 0, :], ALU.mult)
            seq(v.scalar_tensor_tensor(ctmp[:, 0, :], ctmp[:, 1, :], 1.0 / CTX, ctmp[:, 0, :], ALU.mult, ALU.add))
            seq(v.tensor_scalar(ctmp[:, 0, :], ctmp[:, 0, :], EPS, None, ALU.add))
            rsqrt(crstd[:, :], ctmp[:, 0, :], ctmp[:, 1, :])
            v.engine_nop().then_inc(stats_ready, 1)

            self_attention(0, 32 ** -0.5, mask_blocks, 32)
            mlp("L0_xattn_a1_li1_b", "L0_xattn_a1_li3_b", ta)
            layernorm(tc_, hat)
            affine(ta[:, :, :], hat[:, :, :], "L0_xattn_ln2_g", "L0_xattn_ln2_b")
            layernorm(ta, hat)
            ready()
            tt(tb[:, :, :], ta[:, :, :], row("L0_xattn_a2_li1_b"), ALU.add)
            cross(0)
            seq(v.tensor_scalar(qp[0:64, :, :, :].rearrange("p b h q -> p (b h q)"),
                                qp[0:64, :, :, :].rearrange("p b h q -> p (b h q)"),
                                col("L0_xattn_a2_lny_g")[0:64], col("L0_xattn_a2_lny_b")[0:64],
                                ALU.mult, ALU.add))
            v.engine_nop().then_inc(u_ready, 1)
            mlp("L0_xattn_a2_li1_b", "L0_xattn_a2_li3_b", ta)
            tt(x_in[:, :, :], x_in[:, :, :], tc_[:, :, :], ALU.add)
            layernorm(x_in, ta)
            layernorm(ta, hat)
            ready()
            tt(tb[:, :, :], proj_in(), ta[:, :, :], ALU.add)
            layernorm(tb, hat)
            ready()
            v.tensor_tensor(tc_[:, :, :], x_in[:, :, :], tb[:, :, :], ALU.add).then_inc(dn_added, 1)
            gate(0)

            def expert0(e, par, has_next):
                for c in range(FCH):
                    m = e * FCH + c
                    v.wait_ge(g_moved, m + 1)
                    v.tensor_tensor(act[:, par, c, :], sg[:, c % 2, :], PS[:, 6 + c % 2, 0:TOK], ALU.mult) \
                        .then_inc(mul_done, 1)
                if not isinstance(e, int) or e:
                    add_expert(e - 1, 1 - par, 0)

            static_and_loop(v, expert0, EXPERTS - 1)
            add_expert(EXPERTS - 1, 1, 0)
            v.wait_ge(dn_added, EXPERTS + 1)
            layernorm(tc_, hat)
            ready()
            tt(x_in[:, :, :], tc_[:, :, :], row("L1_xattn_bo"), ALU.add)
            cross(1)
            v.engine_nop().then_inc(u_ready, 1)
            tt(x_in[:, :, :], proj_in(), x_in[:, :, :], ALU.add)
            layernorm(x_in, ta)
            ready()
            self_attention(1, 128 ** -0.5, mask_causal, 8)
            v.wait_ge(o_sa_ready, 2 * TILES)
            layernorm(tb, hat)
            affine(tb[:, :, :], hat[:, :, :], "L1_ffn_ln1_g", "L1_ffn_ln1_b")
            tt(tb[:, :, :], tb[:, :, :], ta[:, :, :], ALU.add)
            ready()
            tt(x_in[:, :, :], x_in[:, :, :], tb[:, :, :], ALU.add)
            gate(1)
            v.wait_ge(combT_ps, 1)
            seq(v.tensor_copy(combT[:, :], PS[0:EXPERTS, 7, 0:TOK]))
            v.engine_nop().then_inc(combT_ready, 1)
            v.tensor_copy(tc_[:, :, :], proj_in()).then_inc(dn_added, 1)

            def expert1(e, par, has_next):
                if not isinstance(e, int) or e:
                    add_expert(e - 1, 1 - par, 1)

            static_and_loop(v, expert1, EXPERTS - 1)
            add_expert(EXPERTS - 1, 1, 1)
            v.wait_ge(dn_added, 2 * EXPERTS + 2)
            layernorm(tc_, hat)
            affine(hat[:, :, :], hat[:, :, :], "L1_ffn_ln2_g", "L1_ffn_ln2_b")
            tt(x_in[:, :, :], x_in[:, :, :], hat[:, :, :], ALU.add)
            ready()

        @block.tensor
        def _(pe):
            tm, fm, lin, pts = Count(), Count(), Count(), Count()

            def to_fm(src):
                pe.wait_ge(tm_ready, tm.up())
                for t in range(TILES):
                    ins = pe.transpose(PS[:, 7, t * TP:(t + 1) * TP], src[:, t, :], ident[0:TP, 0:TP])
                ins.then_inc(fmT_ps, 1)

            def linear(products, nout, parts=128, offs=None):
                j = lin.n
                if j >= 7:
                    pe.wait_ge(lin_moved, j - 6)
                for i, (l, r) in enumerate(products):
                    if offs is None:
                        ins = pe.matmul(PS[0:parts, j % 7, 0:nout], l, r,
                                        start=i == 0, stop=i == len(products) - 1)
                    else:
                        ins = pe.matmul(PS[0:parts, j % 7, i * nout:(i + 1) * nout], l, r, start=True, stop=True)
                lin.up()
                ins.then_inc(lin_ps, 1)

            def project(lhs, w, chunks, width=C):
                for t in range(TILES):
                    for c in range(chunks):
                        ins = pe.matmul(PS[0:TP, 0, t * width:(t + 1) * width], lhs(c, t), w(c),
                                        start=c == 0, stop=c == chunks - 1)
                ins.then_inc(proj_ps, 1)

            def tok(tile, t):
                return tile[:, t * TP:(t + 1) * TP]

            def self_attention(call, q, D):
                last = lin.n
                pe.wait_ge(lin_moved, last)

                def scores(p):
                    for c in range(4):
                        pe.wait_ge(kblk_ready, 16 * call + 4 * p + c + 1)
                        if p >= 1:
                            pe.wait_ge(s_read, 16 * call + 4 * (p - 1) + c + 1)
                        pe.matmul(PS[0:TP, c, 0:4 * TP], q(c, p), Kblk[:, c, :, :].rearrange("p h k -> p (h k)"),
                                  start=True, stop=True).then_inc(s_ps, 1)

                def values(p):
                    if call == 0:
                        pe.wait_ge(masked, p + 1)
                    else:
                        pe.wait_ge(exp_done, TILES * call + p + 1)
                    if p >= 1:
                        pe.wait_ge(o_sa_ready, TILES * call + p)

                    def transposes(c):
                        if p * 4 + c >= 2:
                            pe.wait_ge(pt_moved, 16 * call + 4 * p + c - 1)
                        for h in range(4):
                            ins = pe.transpose(PS[0:TP, 4 + c % 2, h * TP:(h + 1) * TP], S[:, p % 2, 4 * c + h, :],
                                               ident[0:TP, 0:TP])
                        ins.then_inc(pt_ps, 1)

                    def weigh(c):
                        pe.wait_ge(pt_moved, 16 * call + 4 * p + c + 1)
                        for h in range(4):
                            hh = 4 * c + h
                            ins = pe.matmul(PS[0:TP, 6, hh * D:(hh + 1) * D], PT[:, c % 2, h, :],
                                            VT[:, p, hh * D:(hh + 1) * D], start=True, stop=True)
                        return ins

                    transposes(0)
                    for c in range(4):
                        if c + 1 < 4:
                            transposes(c + 1)
                        ins = weigh(c)
                    ins.then_inc(o_sa_ps, 1)

                def out_t(p):
                    pe.wait_ge(o_sa_ready, p + 1)
                    if p >= 1:
                        pe.wait_ge(oT_moved, p)
                    for c in range(4):
                        ins = pe.transpose(PS[:, 7, c * TP:(c + 1) * TP], OT[:, p % 2, c * 128:(c + 1) * 128],
                                           ident[0:TP, 0:TP])
                    ins.then_inc(oT_ps, 1)

                scores(0)
                for p in range(TILES):
                    if p + 1 < TILES:
                        scores(p + 1)
                    values(p)
                    if call == 0:
                        out_t(p)

            def mlp(w):
                project(lambda c, t: tok(big1[:, c, :], t), lambda c: w[0][:, c * C:(c + 1) * C], 4)
                to_fm(hat)
                pe.wait_ge(fm_ready, fm.up())
                for c in range(FCH):
                    linear([(w[1][:, c * 128:(c + 1) * 128], xn[:, :])], TOK)
                pe.wait_ge(lin_moved, lin.n)
                project(lambda c, t: tok(big2[:, c, :], t), lambda c: w[2][:, c * C:(c + 1) * C], FCH)

            def queries(wq, nq, loaded, per):
                pe.wait_ge(fm_ready, fm.up())
                for c in range(nq):
                    linear([(wq[:, c * 128:(c + 1) * 128], xn[:, :])], TOK)
                pe.wait_ge(pads_loaded, loaded)
                pe.wait_ge(lin_moved, lin.n)
                for h in range(HEADS):
                    linear([(wkpad[:, h, :], big1[:, h // per, :])], TOK)

            def cross(call):
                def fill(nb, f):
                    if f == 0:
                        pe.wait_ge(xx_ready, nb + 1)
                    if f == 0 and (not isinstance(nb, int) or nb >= 1):
                        pe.wait_ge(mrow_moved, nb)
                    if f == 2:
                        pe.wait_ge(y_ready, SPANS * nb + 1)
                    for j in range(SPAN // KP):
                        kt = f * (SPAN // KP) + j
                        ins = pe.transpose(PS[:, f % 2, j * KP:(j + 1) * KP], XX[:, kt, :], ident[0:KP, 0:KP])
                    ins.then_inc(xxT_ps, 1)

                def score(nb, par, j):
                    g = nb + BATCH * call
                    if j == 0:
                        pe.wait_ge(kab_ready, g + 1)
                        pe.wait_ge(qs_ready, 2 * g + 2)
                        if call or not isinstance(nb, int) or nb >= 1:
                            pe.wait_ge(mrow_moved, g)
                    if j >= 2:
                        pe.wait_ge(sc_max, g * HQ_TILES * SPANS + j - 1)
                    r, s = j // SPANS, j % SPANS
                    pe.matmul(PS[:, j % 2, 0:SPAN], qA[:, par, r * 128:(r + 1) * 128],
                              kA[:, par, s * SPAN:(s + 1) * SPAN], start=True, stop=True).then_inc(sc_ps, 1)

                def max_rows(nb):
                    g = nb + BATCH * call
                    pe.wait_ge(negm_ready, 4 * g + 4)
                    for j in range(HQ_TILES):
                        ins = pe.matmul(PS[64:66, j // 4, (j % 4) * 128:(j % 4 + 1) * 128], mhl[:, j, :], ident[:, :],
                                        start=True, stop=True)
                    ins.then_inc(mrow_ps, 1)

                def score_t(b, par, kt):
                    g0 = KT * (b + BATCH * call)
                    if kt == 0:
                        pe.wait_ge(mrow_moved, b + BATCH * call + 1)
                    if call or not isinstance(b, int) or b or kt >= 2:
                        pe.wait_ge(pf_ready, g0 + kt - 1)
                    keys = slice(kt * KP, (kt + 1) * KP)
                    for j in range(2):
                        bank = PS[0:KP, 2 + 2 * (kt % 2) + j, 0:HALF]
                        pe.matmul(bank, kA[:, par, keys], qA[:, par, j * HALF:(j + 1) * HALF], start=True, stop=False)
                        ins = pe.matmul(bank, kB[:, par, keys], qB[:, par, j * HALF:(j + 1) * HALF],
                                        start=False, stop=True)
                    ins.then_inc(st_ps, 1)

                def weigh_high(b, par, kt, between=None):
                    g0 = KT * (b + BATCH * call)
                    if kt == 0:
                        pe.wait_ge(v_ready, b + BATCH * call + 1)
                        if call or not isinstance(b, int) or b:
                            pe.wait_ge(o_moved, b + BATCH * call)
                    pe.wait_ge(p_ready, g0 + kt + 1)
                    for i, w in enumerate((Wh, Wl)):
                        for j in range(2):
                            ins = pe.matmul(PS[:, 6 + j, 0:HALF], w[:, par, kt, :], Ph[:, kt % 2, j * HALF:(j + 1) * HALF],
                                            start=kt == 0 and i == 0, stop=False)
                    ins.then_inc(ph_used, 1)

                def weigh_low(b, par, kt):
                    g0 = KT * (b + BATCH * call)
                    pe.wait_ge(pl_ready, g0 + kt + 1)
                    for j in range(2):
                        ins = pe.matmul(PS[:, 6 + j, 0:HALF], Wh[:, par, kt, :], Pl[:, kt % 2, j * HALF:(j + 1) * HALF],
                                        start=False, stop=kt == KT - 1)
                    ins.then_inc(pl_used, 1)

                def step(b, par, has_next):
                    for kt in range(KT):
                        jobs = range((kt - 3) * SPANS, (kt - 2) * SPANS) if has_next and 3 <= kt < 10 else ()
                        if kt == 11 and has_next:
                            max_rows(b + 1)
                        if kt + 1 < KT:
                            score_t(b, par, kt + 1)
                        for j in jobs[0:1]:
                            score(b + 1, 1 - par, j)
                        if kt <= 1 and has_next and call == 0:
                            for f in ((0, 1), (2,))[kt]:
                                fill(b + 1, f)
                        if kt == 0 and (not isinstance(b, int) or b):
                            weigh_low(b - 1, 1 - par, KT - 1)
                        weigh_high(b, par, kt)
                        for j in jobs[1:2]:
                            score(b + 1, 1 - par, j)
                        if kt >= 1:
                            weigh_low(b, par, kt - 1)
                        for j in jobs[2:3]:
                            score(b + 1, 1 - par, j)
                    if has_next:
                        score_t(b + 1, 1 - par, 0)

                if call == 1:
                    pe.wait_ge(v_ready, BATCH + 1)
                pe.wait_ge(lin_moved, lin.n)
                if call == 0:
                    for f in range(SPANS):
                        fill(0, f)
                for j in range(HQ_TILES * SPANS):
                    score(0, 0, j)
                max_rows(0)
                score_t(0, 0, 0)
                static_and_loop(pe, step, BATCH - 1)
                weigh_low(BATCH - 1, 1, KT - 1)

            def outputs(call, nq, per):
                pe.wait_ge(u_ready, call + 1)
                for c in range(nq):
                    linear([(wvpad[:, h, :], qp[:, :, h, :]) for h in range(c * per, (c + 1) * per)], TOK)
                pe.wait_ge(lin_moved, lin.n)

            def moe(call, gate_w):
                w = we[:, :, :].rearrange("p b (j n) -> p b j n", j=3)
                loads = 3 - call
                before = 0 if call == 0 else 4 * 3 * 16

                pe.wait_ge(fm_ready, fm.up())
                project(lambda c, t: tok(xn, t), lambda c: gate_w[:, :], 1, EXPERTS)

                def up(e, par, has_next):
                    pe.wait_ge(expert_loaded[par], (e - par) * (loads * 8) + (before + loads * 16))
                    for c in range(FCH):
                        m = e * FCH + c
                        if isinstance(m, int) and m < 2:
                            pass
                        elif call == 0:
                            pe.wait_ge(mul_done, m - 1)
                        else:
                            pe.wait_ge(g_moved, m - 1 + EXPERTS * FCH)
                        mm = pe.matmul(PS[:, 2 + c % 2, 0:TOK], w[:, par, 0, c * 128:(c + 1) * 128], xn[:, :],
                                       start=True, stop=True)
                        if call == 0:
                            mm = pe.matmul(PS[:, 6 + c % 2, 0:TOK], w[:, par, 1, c * 128:(c + 1) * 128], xn[:, :],
                                           start=True, stop=True)
                        mm.then_inc(g_ps, 1)

                def down(e, par):
                    if call == 0:
                        pe.wait_ge(mul_done, (e + 1) * FCH)
                    else:
                        pe.wait_ge(g_moved, (e + 1 + EXPERTS) * FCH)
                    if not isinstance(e, int) or e >= 2:
                        pe.wait_ge(dn_added, e + EXPERTS * call + call + 1)
                    for t in range(TILES):
                        for c in range(FCH):
                            mm = pe.matmul(PS[0:TP, 4 + par, t * C:(t + 1) * C], tok(act[:, par, c, :], t),
                                           w[:, par, 2 - call, c * C:(c + 1) * C], start=c == 0, stop=c == FCH - 1)
                    mm.then_inc(dn_ps, 1)

                def step(e, par, has_next):
                    up(e, par, has_next)
                    if not isinstance(e, int) or e:
                        down(e - 1, 1 - par)
                    if call == 1 and isinstance(e, int) and e == 0:
                        pe.wait_ge(comb_ready, 2)
                        for t in range(TILES):
                            mm = pe.transpose(PS[0:EXPERTS, 7, t * TP:(t + 1) * TP], comb[:, :, t],
                                              ident[0:TP, 0:TP])
                        mm.then_inc(combT_ps, 1)
                        pe.wait_ge(combT_ready, 1)
                        project(lambda c, t: combT[:, t * TP:(t + 1) * TP], lambda c: b2[:, :], 1)

                static_and_loop(pe, step, EXPERTS - 1)
                down(EXPERTS - 1, 1)

            pe.wait_ge(consts_step, 18)
            to_fm(hat)
            pe.wait_ge(fm_ready, fm.up())
            pe.wait_ge(wA_loaded, 6 * 16)
            for c in range(4):
                linear([(w_q1[:, c * 128:(c + 1) * 128], xn[:, :])], TOK)
            for c in range(4):
                linear([(w_k1[:, c * 128:(c + 1) * 128], yn[:, :])], TOK)
            for p in range(TILES):
                linear([(tok(yn, p), w_v1)], 512, TP)
            self_attention(0, lambda c, p: tok(big1[:, c, :], p), 32)
            pe.wait_ge(oT_moved, TILES)
            mlp(w_a1)
            to_fm(hat)
            pe.wait_ge(wB_loaded, 8 * 16)
            queries(wq2, 4, 12 * 16, 4)
            cross(0)
            outputs(0, 4, 4)
            mlp(w_a2)
            to_fm(hat)
            pe.wait_ge(fm_ready, fm.up())
            project(lambda c, t: tok(xn, t), lambda c: attn_w[:, :], 1)
            to_fm(hat)
            moe(0, gate0)
            to_fm(hat)
            pe.wait_ge(wL1_loaded, 5 * 16)
            queries(w_qL1, 8, 18 * 16, 2)
            cross(1)
            outputs(1, 8, 2)
            project(lambda c, t: tok(big1[:, c, :], t), lambda c: w_oL1[:, c, :], 8)
            to_fm(ta)
            pe.wait_ge(fm_ready, fm.up())
            linear([(w_qkvL1[:, 0, :], xn[:, :])], TOK)
            linear([(w_qkvL1[:, 1, :], xn[:, :])], TOK)
            linear([(tok(xn, p), w_qkvL1[:, 2, :]) for p in range(TILES)], C, TP, offs=True)
            self_attention(1, lambda c, p: tok(big1[:, 0, :], p), 8)
            to_fm(tb)
            moe(1, gate1)


def kernel(**inputs):
    import numpy as np
    import concourse.bacc as bacc
    from concourse.bass_utils import run_bass_kernel_spmd

    a = {k: np.asarray(v) for k, v in inputs.items()}
    L0, F0, X1, F1 = "L0_xattn_", "L0_ffn_", "L1_xattn_", "L1_ffn_"
    heads_side = lambda w: w.transpose(1, 0, 2).reshape(w.shape[1], -1)
    chunk_cols = lambda v: v.reshape(-1, 128).T
    both = lambda v: np.concatenate([v, v]) if v.shape[0] == CTX else v
    ctx = a["ctx_512"]
    arrays = {
        "x": a["x"].reshape(TOK, C),
        "ctx": ctx,
        "ctxT": ctx.reshape(BATCH, KP, KT, CTX).transpose(0, 3, 2, 1).reshape(BATCH, CTX, KEYS),
        "rows": np.stack([a[n] for n in ROWS]),
        "cols": np.concatenate([np.stack([both(a[n]) for n in COLS], axis=1),
                                chunk_cols(a[L0 + "a1_li2_b"]), chunk_cols(a[L0 + "a2_li2_b"]),
                                chunk_cols(a[F1 + "b1"])], axis=1),
        "a1_wq": heads_side(a[L0 + "a1_wq"]), "a1_wk": heads_side(a[L0 + "a1_wk"]),
        "a1_wv": heads_side(a[L0 + "a1_wv"]),
        "a1_li1": a[L0 + "a1_li1_w"], "a1_li2": a[L0 + "a1_li2_w"], "a1_li3": a[L0 + "a1_li3_w"],
        "a2_wq": heads_side(a[L0 + "a2_wq"]),
        "a2_wk": a[L0 + "a2_wk"].transpose(0, 2, 1), "a2_wv": a[L0 + "a2_wv"],
        "a2_li1": a[L0 + "a2_li1_w"], "a2_li2": a[L0 + "a2_li2_w"], "a2_li3": a[L0 + "a2_li3_w"],
        "attn_w": a[F0 + "attn_w"].T, "gate0": a[F0 + "gate_w"].T,
        "gp": a[F0 + "gate_proj"].transpose(0, 2, 1), "up": a[F0 + "up_proj"].transpose(0, 2, 1),
        "dp": a[F0 + "down_proj"].transpose(0, 2, 1).reshape(EXPERTS, FCH, 128, C).transpose(0, 2, 1, 3)
        .reshape(EXPERTS, 128, FF),
        "L1_Wq": a[X1 + "Wq"], "L1_Wo": a[X1 + "Wo"],
        "L1_Wk": a[X1 + "Wk"].T.reshape(HEADS, 64, CTX),
        "L1_Wv": a[X1 + "Wv"].reshape(CTX, HEADS, 64).transpose(1, 0, 2),
        "L1f_Wq": heads_side(a[F1 + "Wq"]), "L1f_Wk": heads_side(a[F1 + "Wk"]), "L1f_Wv": heads_side(a[F1 + "Wv"]),
        "gate1": a[F1 + "gate_W"], "W1": a[F1 + "W1"], "b2": a[F1 + "b2"],
        "W2": a[F1 + "W2"].reshape(EXPERTS, FCH, 128, C).transpose(0, 2, 1, 3).reshape(EXPERTS, 128, FF),
    }
    arrays = {k: np.ascontiguousarray(v) for k, v in arrays.items()}

    nc = bacc.Bacc("TRN2", target_bir_lowering=False, num_devices=1)
    f32 = mybir.dt.float32
    d = {k: nc.dram_tensor("in_" + k, v.shape, f32, kind="ExternalInput").ap() for k, v in arrays.items()}
    out = nc.dram_tensor("out", (TOK, C), f32, kind="ExternalOutput").ap()
    build_program(nc, d, out)
    r = run_bass_kernel_spmd(nc, [{"in_" + k: v for k, v in arrays.items()}], core_ids=[0])
    return r.results[0]["out"].reshape(BATCH, SEQ, C)
```

```python
import concourse.bass as bass
import concourse.mybir as mybir
from contextlib import ExitStack

BATCH, SEQ, C = 8, 56, 128
KEYS, CTX = 1500, 64
HEADS = 16
TILES = 4
TP = BATCH * SEQ // TILES
TOK = BATCH * SEQ
KT = 12
KP = KEYS // KT
HQ = HEADS * SEQ
HQ_TILES = HQ // 128
HALF = HQ // 2
PAIRS = HEADS // 2
FF = 512
FCH = FF // 128
EXPERTS = 8
EPS = 1e-5
NEG = -1e30
SPAN = 500
SPANS = KEYS // SPAN

ROWS = ["L0_xattn_ln1_g", "L0_xattn_ln1_b", "L0_xattn_a1_li1_b", "L0_xattn_a1_li3_b",
        "L0_xattn_ln2_g", "L0_xattn_ln2_b", "L0_xattn_a2_li1_b", "L0_xattn_a2_li3_b",
        "L1_xattn_bo", "L1_ffn_ln1_g", "L1_ffn_ln1_b", "L1_ffn_ln2_g", "L1_ffn_ln2_b"]
COLS = ["L0_xattn_a1_lnx_g", "L0_xattn_a1_lnx_b", "L0_xattn_a1_lny_g", "L0_xattn_a1_lny_b",
        "L0_xattn_a1_ln3_g", "L0_xattn_a1_ln3_b",
        "L0_xattn_a2_lnx_g", "L0_xattn_a2_lnx_b", "L0_xattn_a2_lny_g", "L0_xattn_a2_lny_b",
        "L0_xattn_a2_ln3_g", "L0_xattn_a2_ln3_b",
        "L0_ffn_ln1_g", "L0_ffn_ln1_b", "L0_ffn_ln2_g", "L0_ffn_ln2_b"]
COL_A1_LI2 = len(COLS)
COL_A2_LI2 = COL_A1_LI2 + FCH
COL_B1 = COL_A2_LI2 + FCH
NCOLS = COL_B1 + EXPERTS * FCH


class Count:

    def __init__(self):
        self.n = 0

    def up(self, k=1):
        self.n += k
        return self.n


def build_program(nc, d, out):
    f32, f32r, i32 = mybir.dt.float32, mybir.dt.float32r, mybir.dt.int32
    ALU, ACT, AX = mybir.AluOpType, mybir.ActivationFunctionType, mybir.AxisListType

    with ExitStack() as ctx:
        def sb(name, shape, dt=f32):
            return ctx.enter_context(nc.sbuf_tensor(name, shape, dt))

        def sem(name):
            return ctx.enter_context(nc.semaphore(name))

        inverses = nc.dram_tensor("inverses", (HQ,), f32, kind="Internal").ap()
        PS = ctx.enter_context(nc.psum_tensor("PS", [128, 8, 512], f32))

        ident = sb("ident", [128, 128])
        mask_blocks = sb("mask_blocks", [TP, TP])
        mask_later = sb("mask_later", [TP, TP])
        mask_causal = sb("mask_causal", [TP, TP])
        heads4 = sb("heads4", [128, 4])
        heads16 = sb("heads16", [128, 16])
        rows = sb("rows", [TP, len(ROWS), C])
        cols = sb("cols", [128, NCOLS])

        x_in = sb("x_in", [TP, TILES, C])
        hat = sb("hat", [TP, TILES, C])
        ta = sb("ta", [TP, TILES, C])
        tb = sb("tb", [TP, TILES, C])
        tc_ = sb("tc_", [TP, TILES, C])
        stats = sb("stats", [TP, TILES, 6])
        mv = sb("mv", [TP, TILES, 2])
        rs = sb("rs", [TP, 4, TILES])
        xn = sb("xn", [128, TOK])
        yn = sb("yn", [128, TOK])
        wA = sb("wA", [128, 6 * 512])
        wq2 = sb("wq2", [128, 512])
        li2x = sb("li2x", [128, 3 * 512])
        wkpad = sb("wkpad", [128, PAIRS, 128])
        wvpad = sb("wvpad", [128, PAIRS, 128])
        attn_w = sb("attn_w", [128, C])
        gate0 = sb("gate0", [128, EXPERTS])
        gate1 = sb("gate1", [128, EXPERTS])
        b2 = sb("b2", [EXPERTS, C])
        lg = sb("lg", [TP, TILES, EXPERTS])
        top = sb("top", [TP, TILES, 8])
        gt = sb("gt", [TP, 4, TILES, EXPERTS])
        comb = sb("comb", [TP, EXPERTS, TILES])
        cw = sb("cw", [TP, 2, TILES])
        gs = sb("gs", [TP, TILES])
        combT = sb("combT", [EXPERTS, TOK])
        qp_area = sb("qp_area", [128, BATCH * KT * CTX])
        qp = qp_area[:, 0:BATCH * HALF].rearrange("p (b n) -> p b n", b=BATCH)
        cmean = sb("cmean", [KP, BATCH * KT])
        crstd = sb("crstd", [KP, BATCH * KT])
        cst = sb("cst", [KP, KT, 6])
        ctmp = sb("ctmp", [KP, 2, BATCH * KT])
        kA = sb("kA", [128, 2, KEYS], f32r)
        kB = sb("kB", [128, 2, KEYS], f32r)
        qA = sb("qA", [128, 2, HQ], f32r)
        qB = sb("qB", [128, 2, HQ], f32r)
        mx = sb("mx", [128, HQ_TILES, SPANS])
        negm = sb("negm", [128, HQ_TILES])
        mhr = sb("mhr", [128, HQ_TILES], f32r)
        mhl = sb("mhl", [128, HQ_TILES, 2])
        rsum = sb("rsum", [TP, 2, 16])
        rneg = sb("rneg", [TP, 2, 16])
        with ExitStack() as first:
            def sb1(name, shape, dt=f32):
                return first.enter_context(nc.sbuf_tensor(name, shape, dt))

            we = sb1("we", [128, 2, 3 * 512])
            big1 = sb1("big1", [128, 8, TOK])
            big2 = sb1("big2", [128, 4, TOK])
            arena = sb1("arena", [128, 9344])

        with ExitStack() as second:
            def sb2(name, shape, dt=f32):
                return second.enter_context(nc.sbuf_tensor(name, shape, dt))

            CT = sb2("CT", [KP, KT, CTX])
            ostage = sb2("ostage", [128, HQ])
            rden = sb2("rden", [64, HQ])
            dcol = sb2("dcol", [128, HQ_TILES])
            sb2("rest_of_we", [128, 512 - HQ_TILES])
            P = sb2("P", [KP, 2, HQ])
            Ph = sb2("Ph", [KP, 2, HQ], f32r)
            Pl = sb2("Pl", [KP, 2, HQ], f32r)
            XX = sb2("XX", [KP, KT, 128])
            Y = sb2("Y", [128, KEYS])
            Wh = sb2("Wh", [KP, 2, KT, 128], f32r)
            Wl = sb2("Wl", [KP, 2, KT, 128], f32r)

        sb("place_of_we", [128, 2, 3 * 512])
        wh = sb("wh", [128, 2, 2 * 512], f32r)
        wl = sb("wl", [128, 2, 2 * 512], f32r)
        act = sb("act", [128, 2, FCH, TOK])
        sg = sb("sg", [128, 2, TOK])
        xh, xl = qA[:, 0, 0:TOK], qA[:, 0, TOK:2 * TOK]

        def part(off, n):
            return arena[:, off:off + n]

        S = [m.rearrange("p (h k) -> p h k", h=16)[0:TP] for m in
             (part(0, 16 * TP), part(16 * TP, 16 * TP),
              we[:, :, :].rearrange("p b n -> p (b n)")[:, 0:16 * TP])]
        Kblk = part(3584, 16 * TP).rearrange("p (c h k) -> p c h k", c=4, h=4)
        PT = part(5376, 2 * 4 * TP).rearrange("p (b h q) -> p b h q", b=2, h=4)[0:TP]
        VT = part(6272, TILES * 512).rearrange("p (t n) -> p t n", t=TILES)[0:TP]
        OT = part(8320, 2 * 512).rearrange("p (b n) -> p b n", b=2)[0:TP]

        craw = qp_area[0:KP, :].rearrange("p (t c) -> p t c", c=CTX)
        qp_pairs = qp.rearrange("p b (j q) -> p b j q", j=PAIRS)

        w_q1, w_k1, w_v1 = wA[:, 0:512], wA[:, 512:1024], wA[:, 1024:1536]
        w_a1 = [wA[:, 1536:2048], wA[:, 2048:2560], wA[:, 2560:3072]]
        w_a2 = [li2x[:, 0:512], li2x[:, 512:1024], li2x[:, 1024:1536]]
        w_qL1 = wA[:, 0:1024]
        w_oL1 = wA[:, 1024:2048].rearrange("p (c n) -> p c n", c=8)
        w_qkvL1 = wA[:, 2048:2048 + 3 * C].rearrange("p (j n) -> p j n", j=3)

        x_loaded = sem("x_loaded")
        params_loaded = sem("params_loaded")
        wA_loaded = sem("wA_loaded")
        wB_loaded = sem("wB_loaded")
        craw_loaded = sem("craw_loaded")
        wL1_loaded = sem("wL1_loaded")
        pads_loaded = sem("pads_loaded")
        up_loaded = [sem("up_loaded_0"), sem("up_loaded_1")]
        down_loaded = [sem("down_loaded_0"), sem("down_loaded_1")]
        ct_loaded = sem("ct_loaded")
        dcol_loaded = sem("dcol_loaded")
        dcol_inverted = sem("dcol_inverted")
        inverses_stored = sem("inverses_stored")
        rden_loaded = sem("rden_loaded")
        y_loaded = sem("y_loaded")
        v_loaded = sem("v_loaded")
        out_stored = sem("out_stored")
        consts_step = sem("consts_step")
        dve_step = sem("dve_step")
        pads_zeroed = sem("pads_zeroed")
        stats_ready = sem("stats_ready")
        tm_ready = sem("tm_ready")
        fmT_ps = sem("fmT_ps")
        fm_ready = sem("fm_ready")
        lin_ps = sem("lin_ps")
        lin_moved = sem("lin_moved")
        proj_ps = sem("proj_ps")
        kblk_ready = sem("kblk_ready")
        s_ps = sem("s_ps")
        s_read = sem("s_read")
        maxima_ready = sem("maxima_ready")
        exp_done = sem("exp_done")
        masked = sem("masked")
        pt_ps = sem("pt_ps")
        pt_moved = sem("pt_moved")
        o_sa_ps = sem("o_sa_ps")
        o_sa_ready = sem("o_sa_ready")
        oT_ps = sem("oT_ps")
        oT_moved = sem("oT_moved")
        gate_in = sem("gate_in")
        gate_exp = sem("gate_exp")
        comb_ready = sem("comb_ready")
        combT_ps = sem("combT_ps")
        combT_ready = sem("combT_ready")
        g_ps = sem("g_ps")
        g_moved = sem("g_moved")
        u_ps = sem("u_ps")
        mul_done = sem("mul_done")
        x_split = sem("x_split")
        up_high = sem("up_high")
        up_split = sem("up_split")
        dn_ps = sem("dn_ps")
        dn_added = sem("dn_added")
        xx_ready = sem("xx_ready")
        xxT_ps = sem("xxT_ps")
        xx_half = sem("xx_half")
        centred = sem("centred")
        w_filled = sem("w_filled")
        vh_ready = sem("vh_ready")
        y_ready = sem("y_ready")
        k_high = sem("k_high")
        affine_done = sem("affine_done")
        last_inverted = sem("last_inverted")
        cw_ready = sem("cw_ready")
        ka_ready = sem("ka_ready")
        kb_ready = sem("kb_ready")
        v_ready = sem("v_ready")
        qs_ready = sem("qs_ready")
        sc_ps = sem("sc_ps")
        sc_max = sem("sc_max")
        negm_ready = sem("negm_ready")
        mrow_ps = sem("mrow_ps")
        mrow_moved = sem("mrow_moved")
        st_ps = sem("st_ps")
        p_ready = sem("p_ready")
        pf_ready = sem("pf_ready")
        pl_ready = sem("pl_ready")
        pl_last = sem("pl_last")
        ph_used = sem("ph_used")
        pl_used = sem("pl_used")
        o_moved = sem("o_moved")
        o_out = sem("o_out")
        u_ready = sem("u_ready")

        block = ctx.enter_context(nc.Block())

        CONSTS = 17
        LIN_PREP0 = 12 + 4
        LIN_U0 = LIN_PREP0 + 4 + PAIRS
        LIN_PREP1 = LIN_U0 + 4 + 4
        LIN_U1 = LIN_PREP1 + 8 + PAIRS

        def wait_low(engine, b, call, kt):
            if kt < 0:
                b, kt = b - 1, kt + KT
            last = isinstance(b, int) and b == BATCH - 1
            if last and kt % 2:
                engine.wait_ge(pl_last, call * (KT // 2) + kt // 2 + 1)
            else:
                before = b * KT + call * (BATCH * KT - KT // 2)
                engine.wait_ge(pl_ready, before + (kt // 2 if last else kt) + 1)

        def row(name):
            return rows[:, ROWS.index(name):ROWS.index(name) + 1, :].broadcast_to([TP, TILES, C])

        def col(name):
            return cols[:, COLS.index(name):COLS.index(name) + 1]

        def static_and_loop(engine, step, last):
            step(0, 0, True)
            with engine.Fori(0, (last - 1) // 2) as i:
                step(2 * i + 1, 1, True)
                step(2 * i + 2, 0, True)
            step(last, last % 2, False)

        @block.sync
        def _(sp):
            sp.dma_start(x_in[:, :, :], d["x"].rearrange("(t p) c -> p t c", p=TP)).then_inc(x_loaded, 16)
            sp.dma_start(rows[:, :, :], d["rows"].partition_broadcast(TP)).then_inc(params_loaded, 16)
            sp.dma_start(cols[:, :], d["cols"]).then_inc(params_loaded, 16)
            for dst, name in ((w_q1, "a1_wq"), (w_k1, "a1_wk"), (w_v1, "a1_wv"), (w_a1[1], "a1_li2")):
                sp.dma_start(dst, d[name]).then_inc(wA_loaded, 16)
            for dst, name in ((w_a1[0], "a1_li1"), (w_a1[2], "a1_li3")):
                sp.dma_start(dst.rearrange("p (c n) -> p c n", c=4),
                             d[name].rearrange("(c p) n -> p c n", p=128)).then_inc(wA_loaded, 16)
            sp.dma_start(craw, d["ctx"].rearrange("b (p k) c -> p b k c", p=KP)).then_inc(craw_loaded, 16)
            sp.dma_start(wq2[:, :], d["a2_wq"]).then_inc(wB_loaded, 16)
            sp.dma_start(w_a2[1], d["a2_li2"]).then_inc(wB_loaded, 16)
            for dst, name in ((w_a2[0], "a2_li1"), (w_a2[2], "a2_li3")):
                sp.dma_start(dst.rearrange("p (c n) -> p c n", c=4),
                             d[name].rearrange("(c p) n -> p c n", p=128)).then_inc(wB_loaded, 16)
            sp.dma_start(attn_w[:, :], d["attn_w"]).then_inc(wB_loaded, 16)
            sp.dma_start(gate0[:, :], d["gate0"]).then_inc(wB_loaded, 16)
            sp.dma_start(gate1[:, :], d["gate1"]).then_inc(wB_loaded, 16)
            sp.dma_start(b2[:, :], d["b2"]).then_inc(wB_loaded, 16)

            def load_pads(call, D, wk, wv):
                per = 128 // D
                sp.wait_ge(pads_zeroed, 2 * (call + 1))
                for r in range(per):
                    o = r % 2
                    pairs = slice(r // 2, PAIRS, per // 2)
                    sp.dma_start(wkpad[r * D:(r + 1) * D, pairs, o * CTX:(o + 1) * CTX],
                                 wk[r:HEADS:per].rearrange("g d c -> d g c")).then_inc(pads_loaded, 16)
                    sp.dma_start(wvpad[o * CTX:(o + 1) * CTX, pairs, r * D:(r + 1) * D],
                                 wv[r:HEADS:per].rearrange("g c d -> c g d")).then_inc(pads_loaded, 16)

            load_pads(0, 32, d["a2_wk"], d["a2_wv"])

            def load_ct(n):
                if not isinstance(n, int) or n:
                    sp.wait_ge(xx_ready, n)
                sp.dma_start(CT[:, :, :], d["ctx"][bass.ds(n, 1)].rearrange("b (p k) c -> p (b k) c", p=KP)) \
                    .then_inc(ct_loaded, 16)

            def spread_inverses(b, call):
                g = b + (BATCH - 1) * call
                sp.wait_ge(o_moved, 2 * (b + BATCH * call + 1))
                sp.dma_start(dcol[:, :], ostage[64:65, :].rearrange("a (p j) -> a p j", j=HQ_TILES)) \
                    .then_inc(dcol_loaded, 16)
                sp.wait_ge(dcol_inverted, g + 1)
                sp.dma_start(inverses.rearrange("(p j) -> p j", j=HQ_TILES), dcol[:, :]).then_inc(inverses_stored, 16)
                sp.wait_ge(inverses_stored, 16 * g + 16)
                sp.dma_start(rden[:, :], inverses.partition_broadcast(64)).then_inc(rden_loaded, 16)

            sp.wait_ge(pt_ps, 12)
            load_ct(0)
            sp.wait_ge(proj_ps, 2)
            sp.dma_start(w_qL1, d["L1_Wq"]).then_inc(wL1_loaded, 16)
            sp.dma_start(w_oL1, d["L1_Wo"].rearrange("(c p) n -> p c n", p=128)).then_inc(wL1_loaded, 16)
            for j, name in enumerate(("L1f_Wq", "L1f_Wk", "L1f_Wv")):
                sp.dma_start(w_qkvL1[:, j, :], d[name]).then_inc(wL1_loaded, 16)
            load_ct(1)
            load_ct(2)
            load_ct(3)
            spread_inverses(0, 0)
            with sp.Fori(4, BATCH) as i:
                load_ct(i)
                spread_inverses(i - 3, 0)
            for b in range(BATCH - 3, BATCH - 1):
                spread_inverses(b, 0)

            def load_weights(call, e, par, j0, j1, loaded):
                names = ("gp", "up", "dp") if call == 0 else ("W1", "W2")
                for j in range(j0, j1):
                    sp.dma_start(we[:, par, j * 512:(j + 1) * 512],
                                 d[names[j]][bass.ds(e, 1)].rearrange("a p n -> (a p) n")).then_inc(loaded[par], 16)

            def load_experts(call):
                first = 2 - call
                sp.wait_ge(u_ready, call + 1)
                for par in range(2):
                    load_weights(call, par, par, 0, first, up_loaded)
                    load_weights(call, par, par, first, first + 1, down_loaded)

                def next_up(e, par):
                    sp.wait_ge(up_split, e + (call * EXPERTS - 1))
                    load_weights(call, e, par, 0, first, up_loaded)

                def next_down(e, par):
                    sp.wait_ge(dn_ps, e + (call * EXPERTS - 1))
                    load_weights(call, e, par, first, first + 1, down_loaded)

                next_up(2, 0)
                with sp.Fori(0, EXPERTS // 2 - 2) as i:
                    for par in range(2):
                        next_up(2 * i + 3 + par, 1 - par)
                        next_down(2 * i + 2 + par, par)
                next_up(EXPERTS - 1, 1)
                next_down(EXPERTS - 2, 0)
                next_down(EXPERTS - 1, 1)

            load_experts(0)
            load_pads(1, 64, d["L1_Wk"], d["L1_Wv"])

            def load_kv(n):
                sp.wait_ge(ka_ready, n + BATCH)
                for j in range(2):
                    sp.dma_start(Y[j * CTX:(j + 1) * CTX, :], d["ctxT"][bass.ds(n, 1)].rearrange("a c k -> (a c) k")) \
                        .then_inc(y_loaded, 16)
                sp.wait_ge(v_ready, n + BATCH)
                sp.dma_start(XX[:, :, 0:CTX], d["ctx"][bass.ds(n, 1)].rearrange("b (p k) c -> p (b k) c", p=KP)) \
                    .then_inc(v_loaded, 16)

            sp.wait_ge(dn_ps, EXPERTS)
            load_kv(0)
            load_kv(1)
            with sp.Fori(2, BATCH) as i:
                load_kv(i)
                spread_inverses(i - 2, 1)
            spread_inverses(BATCH - 2, 1)
            sp.wait_ge(o_sa_ps, 2 * TILES)
            load_experts(1)
            sp.wait_ge(tm_ready, 10)
            sp.dma_start(out.rearrange("(t p) c -> p t c", p=TP), x_in[:, :, :]).then_inc(out_stored, 16)
            sp.wait_ge(out_stored, 16)

        @block.gpsimd
        def _(pool):
            n = Count()

            def seq(ins):
                ins.then_inc(consts_step, 1)
                pool.wait_ge(consts_step, n.up())

            def zero_pads(call):
                pool.memset(wkpad[:, :, :], 0.0).then_inc(pads_zeroed, 1)
                pool.wait_ge(pads_zeroed, 2 * call + 1)
                pool.memset(wvpad[:, :, :], 0.0).then_inc(pads_zeroed, 1)
                pool.wait_ge(pads_zeroed, 2 * call + 2)

            seq(pool.memset(ident[:, :], 0.0))
            seq(pool.affine_select(out=ident[:, :], in_=ident[:, :], compare_op=ALU.not_equal, fill=1.0,
                                   base=0, pattern=[[-1, 128]], channel_multiplier=1))
            seq(pool.memset(mask_blocks[:, :], 0.0))
            seq(pool.affine_select(out=mask_blocks[:, 0:SEQ], in_=mask_blocks[:, 0:SEQ], compare_op=ALU.is_ge,
                                   fill=NEG, base=SEQ - 1, pattern=[[0, SEQ]], channel_multiplier=-1))
            seq(pool.affine_select(out=mask_blocks[:, SEQ:TP], in_=mask_blocks[:, SEQ:TP], compare_op=ALU.is_ge,
                                   fill=NEG, base=-SEQ, pattern=[[0, SEQ]], channel_multiplier=1))
            seq(pool.memset(mask_later[:, :], 1.0))
            seq(pool.affine_select(out=mask_later[:, :], in_=mask_later[:, :], compare_op=ALU.is_gt, fill=0.0,
                                   base=0, pattern=[[1, TP]], channel_multiplier=-1))
            seq(pool.affine_select(out=mask_causal[:, :], in_=mask_blocks[:, :], compare_op=ALU.is_ge, fill=NEG,
                                   base=0, pattern=[[-1, TP]], channel_multiplier=1))
            for m, w, k in ((heads4, 32, 4), (heads16, 8, 16)):
                seq(pool.memset(m[:, :], 1.0))
                seq(pool.affine_select(out=m[:, :], in_=m[:, :], compare_op=ALU.is_ge, fill=0.0,
                                       base=0, pattern=[[-w, k]], channel_multiplier=1))
                seq(pool.affine_select(out=m[:, :], in_=m[:, :], compare_op=ALU.is_ge, fill=0.0,
                                       base=w - 1, pattern=[[w, k]], channel_multiplier=-1))
            zero_pads(0)
            seq(pool.memset(kB[64:128, :, :].bitcast(f32), 0.0))
            seq(pool.memset(kB[64:66, :, :].bitcast(f32), 1.0))
            seq(pool.memset(qB[64:128, :, :].bitcast(f32), 0.0))

            def self_attention(call, heads, chunk_of):
                pool.wait_ge(lin_moved, 8 if call == 0 else LIN_U1 + 8 + 2)
                for p in range(TILES):
                    for c in range(4):
                        if p >= 1:
                            pool.wait_ge(s_ps, 16 * call + 4 * (p - 1) + c + 1)
                        k = big2[:, chunk_of(c), p * TP:(p + 1) * TP].unsqueeze(1).broadcast_to([128, 4, TP])
                        m = heads[:, :] if call == 0 else heads[:, 4 * c:4 * c + 4]
                        pool.tensor_tensor(Kblk[:, c, :, :], k, m.unsqueeze(2).broadcast_to([128, 4, TP]), ALU.mult) \
                            .then_inc(kblk_ready, 1)
                    if call == 0 and p >= 2:
                        mask_pair(p - 2)
                if call == 0:
                    mask_pair(TILES - 2)
                    mask_pair(TILES - 1)

            def mask_pair(p):
                for h in (slice(0, 8), slice(8, 16)):
                    pool.wait_ge(exp_done, 4 * p + h.stop // 4)
                    pool.tensor_tensor(S[p % 3][:, h], S[p % 3][:, h],
                                       mask_later[:, :].unsqueeze(1).broadcast_to([TP, 8, TP]), ALU.mult) \
                        .then_inc(masked, 1)

            self_attention(0, heads4, lambda c: c)

            def low_part(b, call, kt):
                g0 = (b + BATCH * call) * KT
                pool.wait_ge(pf_ready, g0 + kt + 1)
                if call or not isinstance(b, int) or b or kt >= 2:
                    pool.wait_ge(pl_used, g0 + kt - 1)
                pool.tensor_tensor(Pl[:, kt % 2, :], P[:, kt % 2, :], Ph[:, kt % 2, :], ALU.subtract) \
                    .then_inc(pl_ready, 1)

            def cross(call):
                def step(b, par, has_next):
                    for kt in range(0, KT, 1 if has_next else 2):
                        low_part(b, call, kt)

                pool.memset(Wh[:, :, :, CTX:128].bitcast(f32), 1.0).then_inc(w_filled, 1)
                pool.wait_ge(w_filled, 2 * call + 1)
                pool.memset(Wl[:, :, :, CTX:128].bitcast(f32), 0.0).then_inc(w_filled, 1)
                pool.wait_ge(w_filled, 2 * call + 2)
                static_and_loop(pool, step, BATCH - 1)

            pool.wait_ge(oT_ps, TILES)
            cross(0)

            pool.wait_ge(lin_ps, LIN_U0 + 4)
            zero_pads(1)

            def moe(call):
                first = (2 - call) * 512

                def low_weights(e, par):
                    pool.wait_ge(up_high, e + EXPERTS * call + 1)
                    pool.tensor_tensor(wl[:, par, 0:first], we[:, par, 0:first], wh[:, par, 0:first].bitcast(f32),
                                       ALU.subtract).then_inc(up_split, 1)

                def step(e, par, has_next):
                    if has_next:
                        low_weights(e + 1, 1 - par)

                low_weights(0, 0)
                static_and_loop(pool, step, EXPERTS - 1)

            moe(0)

            pool.wait_ge(dn_ps, EXPERTS)
            cross(1)

            self_attention(1, heads16, lambda c: 0)
            moe(1)

        @block.scalar
        def _(sc):
            fmT, lin, pts = Count(), Count(), Count()

            def move_fm(outs):
                sc.wait_ge(fmT_ps, fmT.up())
                for dst, g, b in outs:
                    if g is None:
                        ins = sc.activation(dst, PS[:, 7, 0:TOK], ACT.Identity)
                    else:
                        ins = sc.activation(dst, PS[:, 7, 0:TOK], ACT.Identity, bias=col(b), scale=col(g))
                ins.then_inc(fm_ready, 1)

            def move_lin(dst, n, func=ACT.Identity, bias=0.0, parts=128, view=None):
                sc.wait_ge(lin_ps, lin.up())
                src = PS[0:parts, (lin.n - 1) % 7, 0:n]
                sc.activation(dst, view(src) if view else src, func, bias=bias).then_inc(lin_moved, 1)

            def self_attention(call):
                def exp(p, c):
                    if c == 0:
                        sc.wait_ge(maxima_ready, TILES * call + p + 1)
                        if p >= 2:
                            sc.wait_ge(o_sa_ready, TILES * call + p - 1)
                    for h in range(4 * c, 4 * c + 4):
                        ins = sc.activation(S[p % 3][:, h, :], S[p % 3][:, h, :], ACT.Exp,
                                            bias=rneg[:, p % 2, h:h + 1], accum_out=rsum[:, p % 2, h:h + 1])
                    ins.then_inc(exp_done, 1)

                def values(p):
                    for c in range(4):
                        sc.wait_ge(pt_ps, pts.up())
                        sc.activation(PT[:, c % 2], PS[0:TP, 4 + c % 2, 0:4 * TP].rearrange("p (h q) -> p h q", h=4),
                                      ACT.Identity).then_inc(pt_moved, 1)
                        if p + 1 < TILES:
                            exp(p + 1, c)
                    if call == 0:
                        sc.wait_ge(oT_ps, p + 1)
                        sc.activation(big1[:, 0:4, p * TP:(p + 1) * TP],
                                      PS[:, 7, 0:4 * TP].rearrange("p (c q) -> p c q", c=4), ACT.Identity) \
                            .then_inc(oT_moved, 1)

                for c in range(4):
                    exp(0, c)
                for p in range(TILES):
                    values(p)

            def mlp(pre, c0):
                move_fm([(xn[:, :], pre + "ln3_g", pre + "ln3_b")])
                for c in range(FCH):
                    move_lin(big2[:, c, :], TOK, ACT.Gelu, cols[:, c0 + c:c0 + c + 1])

            def queries(nq):
                for c in range(nq):
                    move_lin(big1[:, c, :], TOK)
                for j in range(PAIRS):
                    move_lin(qp_pairs[:, :, j, :], TOK, view=lambda s: s.rearrange("p (b q) -> p b q", b=BATCH))

            def fills(nb, which=range(SPANS)):
                for f in which:
                    sc.wait_ge(xxT_ps, SPANS * nb + f + 1)
                    sc.activation(Y[:, f * SPAN:(f + 1) * SPAN], PS[:, f % 2, 0:SPAN], ACT.Identity,
                                  bias=col("L0_xattn_a2_lny_b"), scale=col("L0_xattn_a2_lny_g")) \
                        .then_inc(y_ready, 1)

            def double(nb):
                sc.wait_ge(xx_half, nb + 1)
                sc.activation(XX[:, :, CTX:128], XX[:, :, 0:CTX], ACT.Identity).then_inc(xx_ready, 1)

            def values_high(nb, par, call):
                g = nb + BATCH * call
                if not isinstance(nb, int) or nb >= 2 or call:
                    sc.wait_ge(pl_used, KT * (g - 1))
                if call:
                    sc.wait_ge(v_loaded, 16 * nb + 16)
                else:
                    sc.wait_ge(xx_half, nb + 1)
                sc.activation(Wh[:, par, :, 0:CTX], XX[:, :, 0:CTX], ACT.Identity).then_inc(vh_ready, 1)

            def cross(call, scale):
                def step(b, par, has_next, has_third=False):
                    g0 = (b + BATCH * call) * KT
                    for kt in range(KT):
                        sc.wait_ge(st_ps, g0 + kt + 1)
                        if call or not isinstance(b, int) or b or kt >= 2:
                            wait_low(sc, b, call, kt - 2)
                            sc.wait_ge(ph_used, g0 + kt - 1)
                        bank = 2 + 2 * (kt % 2)
                        for dst, signal in ((Ph, p_ready), (P, pf_ready)):
                            sc.activation(dst[:, kt % 2, :].rearrange("p (j n) -> p j n", j=2),
                                          PS[0:KP, bank:bank + 2, 0:HALF], ACT.Exp, scale=scale).then_inc(signal, 1)
                        if kt == 0 and has_next and call == 0:
                            sc.wait_ge(ka_ready, b + 1)
                            fills(b + 1, (0, 1))
                        if kt == 1 and has_next and call == 0:
                            fills(b + 1, (2,))
                        if kt == 2 and has_next:
                            values_high(b + 1, 1 - par, call)
                        if kt == 9 and has_third and call == 0:
                            double(b + 2)

                if call == 0:
                    double(1)
                    step(0, 0, True, True)
                    with sc.Fori(0, BATCH // 2 - 2) as i:
                        step(2 * i + 1, 1, True, True)
                        step(2 * i + 2, 0, True, True)
                    for b in range(BATCH - 3, BATCH):
                        step(b, b % 2, b + 1 < BATCH, b + 2 < BATCH)
                else:
                    static_and_loop(sc, step, BATCH - 1)

            sc.wait_ge(params_loaded, 32)
            move_fm([(xn[:, :], "L0_xattn_a1_lnx_g", "L0_xattn_a1_lnx_b"),
                     (yn[:, :], "L0_xattn_a1_lny_g", "L0_xattn_a1_lny_b")])
            for c in range(4):
                move_lin(big1[:, c, :], TOK)
            for c in range(4):
                move_lin(big2[:, c, :], TOK)
            for p in range(TILES):
                move_lin(VT[:, p, :], 512, parts=TP)
            self_attention(0)
            double(0)
            sc.wait_ge(w_filled, 2)
            values_high(0, 0, 0)
            mlp("L0_xattn_a1_", COL_A1_LI2)

            move_fm([(xn[:, :], "L0_xattn_a2_lnx_g", "L0_xattn_a2_lnx_b")])
            fills(0)
            sc.wait_ge(stats_ready, 1)
            queries(4)
            cross(0, 32 ** -0.5)
            for c in range(4):
                move_lin(big1[:, c, :], TOK)
            mlp("L0_xattn_a2_", COL_A2_LI2)

            def gate(call):
                sc.wait_ge(gate_in, call + 1)
                sc.activation(gt[:, 0], gt[:, 0], ACT.Exp).then_inc(gate_exp, 1)

            move_fm([(xn[:, :], "L0_ffn_ln1_g", "L0_ffn_ln1_b")])
            move_fm([(xh, "L0_ffn_ln2_g", "L0_ffn_ln2_b"), (xn[:, :], "L0_ffn_ln2_g", "L0_ffn_ln2_b")])
            gate(0)

            def silu(e, _par, _has_next):
                for c in range(FCH):
                    m = e * FCH + c
                    sc.wait_ge(g_ps, m + 1)
                    if not isinstance(e, int) or m >= 2:
                        sc.wait_ge(mul_done, m - 1)
                    sc.activation(sg[:, c % 2, :], PS[:, 2 + c % 2, 0:TOK], ACT.Silu).then_inc(g_moved, 1)

            static_and_loop(sc, silu, EXPERTS - 1)

            move_fm([(xn[:, :], None, None)])
            sc.wait_ge(w_filled, 4)
            values_high(0, 0, 1)
            queries(8)
            cross(1, 64 ** -0.5)
            for c in range(8):
                move_lin(big1[:, c, :], TOK)

            move_fm([(xn[:, :], None, None)])
            move_lin(big1[:, 0, :], TOK)
            move_lin(big2[:, 0, :], TOK)
            move_lin(VT[:, :, 0:C], 512, parts=TP, view=lambda s: s.rearrange("p (t n) -> p t n", t=TILES))
            self_attention(1)

            move_fm([(xh, None, None), (xn[:, :], None, None)])
            gate(1)

            def relu(e, par, _has_next):
                for c in range(FCH):
                    m = e * FCH + c
                    sc.wait_ge(g_ps, m + 1 + EXPERTS * FCH)
                    if not isinstance(e, int) or e >= 2:
                        sc.wait_ge(dn_ps, e - 1 + EXPERTS)
                    sc.activation(act[:, par, c, :], PS[:, 2 + c % 2, 0:TOK], ACT.Relu,
                                  bias=cols[:, bass.ds(COL_B1 + m, 1)]).then_inc(g_moved, 1)

            static_and_loop(sc, relu, EXPERTS - 1)

        @block.vector
        def _(v):
            n, proj = Count(), Count()

            def seq(ins):
                ins.then_inc(dve_step, 1)
                v.wait_ge(dve_step, n.up())

            def rsqrt(y, var, tmp):
                seq(v.tensor_scalar(y.bitcast(i32), var.bitcast(i32), -0.5, 1597463007.0, ALU.mult, ALU.add))
                for _ in range(3):
                    seq(v.tensor_tensor(tmp, y, y, ALU.mult))
                    seq(v.scalar_tensor_tensor(tmp, tmp, -0.5, var, ALU.mult, ALU.mult))
                    seq(v.scalar_tensor_tensor(y, tmp, 1.5, y, ALU.add, ALU.mult))

            def layernorm(src, dst):
                for t in range(TILES):
                    ins = v.bn_stats(stats[:, t, :], src[:, t, :])
                seq(ins)
                for t in range(TILES):
                    ins = v.bn_aggr(mv[:, t, :], stats[:, t, :])
                seq(ins)
                seq(v.tensor_scalar(rs[:, 0, :], mv[:, :, 1], EPS, None, ALU.add))
                rsqrt(rs[:, 1, :], rs[:, 0, :], rs[:, 2, :])
                for t in range(TILES):
                    ins = v.tensor_scalar(dst[:, t, :], src[:, t, :], mv[:, t, 0:1], rs[:, 1, t:t + 1],
                                          ALU.subtract, ALU.mult)
                seq(ins)

            def layernorm_twice(src, dst, once=None):
                for t in range(TILES):
                    ins = v.bn_stats(stats[:, t, :], src[:, t, :])
                seq(ins)
                for t in range(TILES):
                    ins = v.bn_aggr(mv[:, t, :], stats[:, t, :])
                seq(ins)
                seq(v.tensor_scalar(rs[:, 0, :], mv[:, :, 1], EPS, None, ALU.add))
                rsqrt(rs[:, 1, :], rs[:, 0, :], rs[:, 2, :])
                seq(v.tensor_tensor(rs[:, 2, :], rs[:, 1, :], rs[:, 1, :], ALU.mult))
                seq(v.tensor_tensor(rs[:, 0, :], rs[:, 2, :], mv[:, :, 1], ALU.mult))
                seq(v.tensor_scalar(rs[:, 0, :], rs[:, 0, :], EPS, None, ALU.add))
                rsqrt(rs[:, 3, :], rs[:, 0, :], rs[:, 2, :])
                seq(v.tensor_tensor(rs[:, 3, :], rs[:, 3, :], rs[:, 1, :], ALU.mult))
                for t in range(TILES):
                    ins = v.tensor_scalar(dst[:, t, :], src[:, t, :], mv[:, t, 0:1], rs[:, 3, t:t + 1],
                                          ALU.subtract, ALU.mult)
                seq(ins)
                if once is not None:
                    ready()
                    for t in range(TILES):
                        ins = v.tensor_scalar(once[:, t, :], src[:, t, :], mv[:, t, 0:1], rs[:, 1, t:t + 1],
                                              ALU.subtract, ALU.mult)
                    seq(ins)

            def tt(dst, a, b, op):
                seq(v.tensor_tensor(dst, a, b, op))

            def affine(dst, src, g, b):
                tt(dst, src, row(g), ALU.mult)
                tt(dst, dst, row(b), ALU.add)

            def proj_in():
                v.wait_ge(proj_ps, proj.up())
                return PS[0:TP, 0, :].rearrange("p (t c) -> p t c", t=TILES)

            def ready():
                v.engine_nop().then_inc(tm_ready, 1)

            def self_attention(call, scale, mask, D, between=lambda p: None):
                def shift(p):
                    if p >= 3:
                        v.wait_ge(pt_ps, 16 * call + 4 * (p - 2))
                    for c in range(4):
                        v.wait_ge(s_ps, 16 * call + 4 * p + c + 1)
                        ins = v.scalar_tensor_tensor(
                            S[p % 3][:, 4 * c:4 * c + 4, :],
                            PS[0:TP, c, 0:4 * TP].rearrange("p (h k) -> p h k", h=4), scale,
                            mask[:, :].unsqueeze(1).broadcast_to([TP, 4, TP]), ALU.mult, ALU.add)
                        ins.then_inc(s_read, 1)
                    v.wait_ge(s_read, 16 * call + 4 * p + 4)
                    if p >= 2:
                        v.wait_ge(exp_done, 4 * (TILES * call + p - 1))
                    v.tensor_reduce(rneg[:, p % 2, :], S[p % 3], AX.X, ALU.max, negate=True).then_inc(maxima_ready, 1)

                def sums(p):
                    v.wait_ge(exp_done, 4 * (TILES * call + p + 1))
                    seq(v.reciprocal(rsum[:, p % 2, :], rsum[:, p % 2, :]))

                def output(p):
                    v.wait_ge(o_sa_ps, TILES * call + p + 1)
                    if call == 0 and p >= 2:
                        v.wait_ge(oT_ps, p - 1)
                    dst = OT[:, p % 2, :] if call == 0 else tb[:, p, :]
                    v.tensor_tensor(dst.rearrange("p (h e) -> p h e", e=D),
                                    PS[0:TP, 6, 0:16 * D].rearrange("p (h e) -> p h e", e=D),
                                    rsum[:, p % 2, :].unsqueeze(2).broadcast_to([TP, 16, D]),
                                    ALU.mult).then_inc(o_sa_ready, 1)

                shift(0)
                shift(1)
                for p in range(TILES):
                    if p + 1 < TILES:
                        between(p)
                    sums(p)
                    if p + 2 < TILES:
                        shift(p + 2)
                    output(p)

            def mlp(b3, skip):
                tt(tb[:, :, :], proj_in(), tb[:, :, :], ALU.add)
                layernorm(tb, hat)
                ready()
                tt(tc_[:, :, :], tb[:, :, :], row(b3), ALU.add)
                tt(tc_[:, :, :], tc_[:, :, :], skip[:, :, :], ALU.add)
                tt(tc_[:, :, :], proj_in(), tc_[:, :, :], ALU.add)

            def normalise(nb, parts=(0, 1)):
                if 0 in parts:
                    v.wait_ge(ct_loaded, 16 * nb + 16)
                    mean = cmean[:, bass.ds(nb * KT, KT)].unsqueeze(2).broadcast_to([KP, KT, CTX])
                    v.tensor_tensor(CT[:, :, :], CT[:, :, :], mean, ALU.subtract).then_inc(centred, 1)
                if 1 in parts:
                    v.wait_ge(centred, nb + 1)
                    if not isinstance(nb, int) or nb > 0:
                        v.wait_ge(xxT_ps, SPANS * nb)
                        v.wait_ge(v_ready, nb)
                    rstd = crstd[:, bass.ds(nb * KT, KT)].unsqueeze(2).broadcast_to([KP, KT, CTX])
                    v.tensor_tensor(XX[:, :, 0:CTX], CT[:, :, :], rstd, ALU.mult).then_inc(xx_half, 1)

            def cross(call):
                def affine_out(b):
                    v.wait_ge(o_out, b + 1)
                    o = qp[:, bass.ds(b, 1)].rearrange("p a n -> p (a n)")
                    v.tensor_scalar(o, o, col("L0_xattn_a2_lny_g"), col("L0_xattn_a2_lny_b"),
                                    ALU.mult, ALU.add).then_inc(affine_done, 1)

                def split_queries(nb, par, out_b=None):
                    if call or not isinstance(nb, int) or nb >= 2:
                        v.wait_ge(st_ps, KT * (nb + BATCH * call - 1))
                    q = qp[:, bass.ds(nb, 1)].rearrange("p a n -> p (a n)")
                    heads = [(q[o * 64:(o + 1) * 64], slice(o * HALF, (o + 1) * HALF)) for o in range(2)]
                    for rows_ in (slice(0, 64), slice(64, 128)):
                        for src, columns in heads:
                            ins = v.tensor_copy(qA[rows_, par, columns], src)
                    ins.then_inc(qs_ready, 1)
                    if out_b is not None:
                        move_output(out_b)
                    v.wait_ge(qs_ready, 2 * (nb + BATCH * call) + 1)
                    for o, (src, columns) in enumerate(heads):
                        ins = v.tensor_tensor(qB[0:64, par, columns], src, qA[o * 64:(o + 1) * 64, par, columns],
                                              ALU.subtract)
                    ins.then_inc(qs_ready, 1)

                def split_keys(nb, par):
                    g = nb + BATCH * call
                    for i, keys in enumerate((slice(0, 2 * SPAN), slice(2 * SPAN, KEYS))):
                        if call == 0:
                            v.wait_ge(y_ready, SPANS * nb + 2 + i)
                        elif i == 0:
                            v.wait_ge(y_loaded, 32 * nb + 32)
                        v.tensor_copy(kA[:, par, keys], Y[:, keys]).then_inc(k_high, 1)
                        v.wait_ge(k_high, 2 * g + 1 + i)
                        ins = v.tensor_tensor(kA[64:128, par, keys], Y[64:128, keys], kA[64:128, par, keys],
                                              ALU.subtract)
                    ins.then_inc(ka_ready, 1)
                    v.tensor_copy(kB[0:64, par, :], kA[0:64, par, :]).then_inc(kb_ready, 1)

                def values_low(nb, par):
                    v.wait_ge(vh_ready, nb + BATCH * call + 1)
                    v.tensor_tensor(Wl[:, par, :, 0:CTX], XX[:, :, 0:CTX], Wh[:, par, :, 0:CTX], ALU.subtract) \
                        .then_inc(v_ready, 1)

                def move_output(b):
                    g = b + BATCH * call
                    v.wait_ge(pl_used, KT * (g + 1))
                    if call or not isinstance(b, int) or b:
                        v.wait_ge(o_out, g)
                    for j in range(2):
                        v.tensor_copy(ostage[:, j * HALF:(j + 1) * HALF], PS[:, 6 + j, 0:HALF]).then_inc(o_moved, 1)

                def invert(b):
                    v.wait_ge(dcol_loaded, 16 * (b + (BATCH - 1) * call) + 16)
                    v.reciprocal(dcol[:, :], dcol[:, :]).then_inc(dcol_inverted, 1)

                def divide(b):
                    if not (isinstance(b, int) and b == BATCH - 1):
                        v.wait_ge(rden_loaded, 16 * (b + (BATCH - 1) * call) + 16)
                    for o in range(2):
                        columns = slice(o * HALF, (o + 1) * HALF)
                        ins = v.tensor_tensor(qp[o * 64:(o + 1) * 64, bass.ds(b, 1)].rearrange("p a n -> p (a n)"),
                                              ostage[0:64, columns], rden[:, columns], ALU.mult)
                    ins.then_inc(o_out, 1)

                def maxima(nb, par, out_b=None, third=None):
                    g = nb + BATCH * call
                    for j in range(HQ_TILES * SPANS):
                        v.wait_ge(sc_ps, g * HQ_TILES * SPANS + j + 1)
                        v.tensor_reduce(mx[:, j // SPANS, j % SPANS:j % SPANS + 1], PS[:, j % 2, 0:SPAN],
                                        AX.X, ALU.max).then_inc(sc_max, 1)
                        if out_b is not None and j == 3:
                            invert(out_b)
                        if out_b is not None and j == 15:
                            divide(out_b)
                        if out_b is not None and j == 18 and call == 0:
                            affine_out(out_b)
                        if third is not None and j in (8, 12):
                            normalise(third, (j // 4 - 2,))
                    maxima_rows(nb, par)

                def first_maxima():
                    for r in range(HQ_TILES):
                        v.wait_ge(sc_ps, (BATCH * call * HQ_TILES + r + 1) * SPANS)
                        bank = SPANS * (r % 2)
                        v.tensor_reduce(mx[:, r, 0:1], PS[:, bank:bank + SPANS, 0:SPAN], AX.XY, ALU.max) \
                            .then_inc(sc_max, SPANS)
                    maxima_rows(0, 0, 1)

                def maxima_rows(nb, par, parts=SPANS):
                    g = nb + BATCH * call
                    v.wait_ge(sc_max, (g + 1) * HQ_TILES * SPANS)
                    v.tensor_reduce(negm[:, :], mx[:, :, 0:parts], AX.X, ALU.max, negate=True).then_inc(negm_ready, 1)
                    v.wait_ge(negm_ready, 4 * g + 1)
                    v.tensor_copy(mhr[:, :], negm[:, :]).then_inc(negm_ready, 1)
                    v.wait_ge(negm_ready, 4 * g + 2)
                    v.tensor_copy(mhl[:, :, 0], mhr[:, :].bitcast(f32)).then_inc(negm_ready, 1)
                    v.tensor_tensor(mhl[:, :, 1], negm[:, :], mhr[:, :].bitcast(f32), ALU.subtract) \
                        .then_inc(negm_ready, 1)
                    v.wait_ge(mrow_ps, g + 1)
                    v.tensor_copy(qB[64:66, par, 0:512], PS[64:66, 0, 0:512])
                    v.tensor_copy(qB[64:66, par, 512:HQ], PS[64:66, 1, 0:HQ - 512]).then_inc(mrow_moved, 1)

                def step(b, par, has_next, has_third=False):
                    out_b = b - 1 if not isinstance(b, int) or b else None
                    if has_next:
                        split_queries(b + 1, 1 - par, out_b)
                    elif out_b is not None:
                        move_output(out_b)
                    if has_next:
                        split_keys(b + 1, 1 - par)
                        values_low(b + 1, 1 - par)
                        maxima(b + 1, 1 - par, out_b, b + 2 if has_third else None)
                    else:
                        for kt in range(1, KT, 2):
                            g0 = (b + BATCH * call) * KT
                            v.wait_ge(pf_ready, g0 + kt + 1)
                            v.wait_ge(pl_used, g0 + kt - 1)
                            v.tensor_tensor(Pl[:, kt % 2, :], P[:, kt % 2, :], Ph[:, kt % 2, :], ALU.subtract) \
                                .then_inc(pl_last, 1)
                            if kt == 3:
                                invert(out_b)
                            if kt == 7:
                                divide(out_b)
                                if call == 0:
                                    affine_out(out_b)

                split_keys(0, 0)
                values_low(0, 0)
                if call == 0:
                    normalise(1)
                v.wait_ge(lin_moved, (LIN_U0, LIN_U1)[call])
                split_queries(0, 0)
                if call == 0:
                    first_maxima()
                    step(0, 0, True, True)
                    with v.Fori(0, BATCH // 2 - 2) as i:
                        step(2 * i + 1, 1, True, True)
                        step(2 * i + 2, 0, True, True)
                    for b in range(BATCH - 3, BATCH):
                        step(b, b % 2, b + 1 < BATCH, b + 2 < BATCH)
                else:
                    first_maxima()
                    static_and_loop(v, step, BATCH - 1)
                move_output(BATCH - 1)
                v.wait_ge(o_moved, 2 * BATCH * (call + 1))
                v.reciprocal(rden[:, :], ostage[64:128, :]).then_inc(last_inverted, 1)
                v.wait_ge(last_inverted, call + 1)
                divide(BATCH - 1)
                v.wait_ge(o_out, BATCH * (call + 1))
                if call == 0:
                    affine_out(BATCH - 1)
                    v.wait_ge(affine_done, BATCH)

            def gate(call):
                v.wait_ge(proj_ps, proj.up())
                seq(v.tensor_copy(lg[:, :, :], PS[0:TP, 0, 0:TILES * EXPERTS].rearrange("p (t e) -> p t e", t=TILES)))
                for t in range(TILES):
                    ins = v.max(top[:, t, :], lg[:, t, :])
                seq(ins)
                bc = lambda a: a.broadcast_to([TP, TILES, EXPERTS])
                v.tensor_tensor(gt[:, 0], lg[:, :, :], bc(top[:, :, 0:1]), ALU.subtract).then_inc(gate_in, 1)
                tt(gt[:, 1], lg[:, :, :], bc(top[:, :, 1:2]), ALU.is_gt)
                tt(gt[:, 2], lg[:, :, :], bc(top[:, :, 1:2]), ALU.is_equal)
                seq(v.tensor_reduce(gs[:, :], gt[:, 1], AX.X, ALU.add))
                tt(gt[:, 3, :, 0], gt[:, 2, :, 0], gs[:, :], ALU.add)
                for e in range(1, EXPERTS):
                    tt(gt[:, 3, :, e], gt[:, 3, :, e - 1], gt[:, 2, :, e], ALU.add)
                seq(v.scalar_tensor_tensor(gt[:, 2], gt[:, 3], 2.0, gt[:, 2], ALU.is_le, ALU.mult))
                tt(gt[:, 1], gt[:, 1], gt[:, 2], ALU.add)
                v.wait_ge(gate_exp, call + 1)
                tt(gt[:, 1], gt[:, 1], gt[:, 0], ALU.mult)
                seq(v.tensor_reduce(gs[:, :], gt[:, 1], AX.X, ALU.add))
                seq(v.reciprocal(gs[:, :], gs[:, :]))
                seq(v.tensor_tensor(comb[:, :, :].rearrange("p e t -> p t e"), gt[:, 1],
                                    gs[:, :].unsqueeze(2).broadcast_to([TP, TILES, EXPERTS]), ALU.mult))
                v.engine_nop().then_inc(comb_ready, 1)

            def split_tokens(call):
                v.wait_ge(fm_ready, (6, 9)[call])
                v.tensor_tensor(xl, xn[:, :], xh.bitcast(f32), ALU.subtract).then_inc(x_split, 1)

            def high_weights(e, par, call):
                layers = 2 - call
                v.wait_ge(up_loaded[par], (e - par) * (layers * 8) + (call * EXPERTS * 16 + layers * 16))
                if not isinstance(e, int) or e >= 2:
                    v.wait_ge(g_ps if call else u_ps, (e - 1) * FCH + EXPERTS * FCH * call)
                v.tensor_copy(wh[:, par, 0:layers * 512], we[:, par, 0:layers * 512]).then_inc(up_high, 1)

            def add_expert(e, par, call):
                g = e + EXPERTS * call
                v.tensor_copy(cw[:, par, :], comb[:, bass.ds(e, 1), :].rearrange("p a t -> p (a t)")) \
                    .then_inc(cw_ready, 1)
                v.wait_ge(cw_ready, g + 1)
                v.wait_ge(dn_ps, g + 1)
                v.wait_ge(dn_added, g + call + 1)
                for t in range(TILES):
                    ins = v.scalar_tensor_tensor(tc_[:, t, :], PS[0:TP, 4 + par, t * C:(t + 1) * C],
                                                 cw[:, par, t:t + 1], tc_[:, t, :], ALU.mult, ALU.add)
                ins.then_inc(dn_added, 1)


            v.wait_ge(x_loaded, 16)
            layernorm_twice(x_in, hat)
            v.wait_ge(params_loaded, 32)
            affine(ta[:, :, :], hat[:, :, :], "L0_xattn_ln1_g", "L0_xattn_ln1_b")
            layernorm(ta, hat)
            ready()
            tt(tb[:, :, :], ta[:, :, :], row("L0_xattn_a1_li1_b"), ALU.add)

            def context_stats(b):
                for k in range(KT):
                    ins = v.bn_stats(cst[:, k, :], craw[:, b * KT + k, :])
                seq(ins)
                w = slice(b * KT, (b + 1) * KT)
                tt(cmean[:, w], cst[:, :, 1], cst[:, :, 4], ALU.add)
                tt(ctmp[:, 0, w], cst[:, :, 1], cst[:, :, 4], ALU.subtract)
                tt(ctmp[:, 1, w], cst[:, :, 2], cst[:, :, 5], ALU.add)

            def context_rstd():
                seq(v.tensor_scalar(cmean[:, :], cmean[:, :], 0.5, None, ALU.mult))
                seq(v.tensor_scalar(ctmp[:, 0, :], ctmp[:, 0, :], 0.5, None, ALU.mult))
                tt(ctmp[:, 0, :], ctmp[:, 0, :], ctmp[:, 0, :], ALU.mult)
                seq(v.scalar_tensor_tensor(ctmp[:, 0, :], ctmp[:, 1, :], 1.0 / CTX, ctmp[:, 0, :], ALU.mult, ALU.add))
                seq(v.tensor_scalar(ctmp[:, 0, :], ctmp[:, 0, :], EPS, None, ALU.add))
                rsqrt(crstd[:, :], ctmp[:, 0, :], ctmp[:, 1, :])
                v.engine_nop().then_inc(stats_ready, 1)

            v.wait_ge(craw_loaded, 16)
            for b in range(5):
                context_stats(b)
            self_attention(0, 32 ** -0.5, mask_blocks, 32, between=lambda p: context_stats(5 + p))
            context_rstd()
            v.wait_ge(oT_ps, TILES)
            normalise(0)
            mlp("L0_xattn_a1_li3_b", ta)
            layernorm(tc_, hat)
            affine(ta[:, :, :], hat[:, :, :], "L0_xattn_ln2_g", "L0_xattn_ln2_b")
            layernorm(ta, hat)
            ready()
            tt(tb[:, :, :], ta[:, :, :], row("L0_xattn_a2_li1_b"), ALU.add)
            cross(0)
            v.engine_nop().then_inc(u_ready, 1)
            mlp("L0_xattn_a2_li3_b", ta)
            tt(x_in[:, :, :], x_in[:, :, :], tc_[:, :, :], ALU.add)
            layernorm_twice(x_in, hat, ta)
            high_weights(0, 0, 0)
            tt(tb[:, :, :], proj_in(), ta[:, :, :], ALU.add)
            layernorm(tb, hat)
            ready()
            v.tensor_tensor(tc_[:, :, :], x_in[:, :, :], tb[:, :, :], ALU.add).then_inc(dn_added, 1)
            split_tokens(0)
            gate(0)

            def expert0(e, par, has_next):
                for c in range(FCH):
                    v.wait_ge(g_moved, e * FCH + c + 1)
                    v.wait_ge(u_ps, e * FCH + c + 1)
                    v.tensor_tensor(act[:, par, c, :], sg[:, c % 2, :], PS[:, 6 + c % 2, 0:TOK], ALU.mult) \
                        .then_inc(mul_done, 1)
                    if has_next and c == 1:
                        high_weights(e + 1, 1 - par, 0)
                if not isinstance(e, int) or e:
                    add_expert(e - 1, 1 - par, 0)

            static_and_loop(v, expert0, EXPERTS - 1)
            add_expert(EXPERTS - 1, 1, 0)
            v.wait_ge(dn_added, EXPERTS + 1)
            layernorm(tc_, hat)
            ready()
            tt(x_in[:, :, :], tc_[:, :, :], row("L1_xattn_bo"), ALU.add)
            cross(1)
            v.engine_nop().then_inc(u_ready, 1)
            tt(x_in[:, :, :], proj_in(), x_in[:, :, :], ALU.add)
            layernorm(x_in, ta)
            ready()
            self_attention(1, 128 ** -0.5, mask_causal, 8)
            v.wait_ge(o_sa_ready, 2 * TILES)
            layernorm(tb, hat)
            affine(tb[:, :, :], hat[:, :, :], "L1_ffn_ln1_g", "L1_ffn_ln1_b")
            tt(tb[:, :, :], tb[:, :, :], ta[:, :, :], ALU.add)
            ready()
            tt(x_in[:, :, :], x_in[:, :, :], tb[:, :, :], ALU.add)
            high_weights(0, 0, 1)
            split_tokens(1)
            gate(1)
            v.wait_ge(combT_ps, 1)
            seq(v.tensor_copy(combT[:, :], PS[0:EXPERTS, 7, 0:TOK]))
            v.engine_nop().then_inc(combT_ready, 1)
            v.tensor_copy(tc_[:, :, :], proj_in()).then_inc(dn_added, 1)

            def expert1(e, par, has_next):
                if has_next:
                    high_weights(e + 1, 1 - par, 1)
                if not isinstance(e, int) or e:
                    add_expert(e - 1, 1 - par, 1)

            static_and_loop(v, expert1, EXPERTS - 1)
            add_expert(EXPERTS - 1, 1, 1)
            v.wait_ge(dn_added, 2 * EXPERTS + 2)
            layernorm(tc_, hat)
            affine(hat[:, :, :], hat[:, :, :], "L1_ffn_ln2_g", "L1_ffn_ln2_b")
            tt(x_in[:, :, :], x_in[:, :, :], hat[:, :, :], ALU.add)
            ready()

        @block.tensor
        def _(pe):
            tm, fm, lin = Count(), Count(), Count()

            WARM_MLP = (24, 24)
            WARM_QUERIES = (52, 30)
            WARM_MOE = (38, 5)
            WARM_L1 = (20, 20)

            def keep_warm(n):
                for _ in range(n):
                    pe.matmul(PS[:, 3, 0:64], ident[:, :], ident[:, 0:64], start=True, stop=True)

            def to_fm(src, idle=0):
                keep_warm(idle)
                pe.wait_ge(tm_ready, tm.up())
                for t in range(TILES):
                    ins = pe.transpose(PS[:, 7, t * TP:(t + 1) * TP], src[:, t, :], ident[0:TP, 0:TP])
                ins.then_inc(fmT_ps, 1)

            def linear(products, nout, parts=128, offs=None):
                j = lin.n
                if j >= 7:
                    pe.wait_ge(lin_moved, j - 6)
                for i, (l, r) in enumerate(products):
                    if offs is None:
                        ins = pe.matmul(PS[0:parts, j % 7, 0:nout], l, r,
                                        start=i == 0, stop=i == len(products) - 1)
                    else:
                        ins = pe.matmul(PS[0:parts, j % 7, i * nout:(i + 1) * nout], l, r, start=True, stop=True)
                lin.up()
                ins.then_inc(lin_ps, 1)

            def project(lhs, w, chunks, width=C):
                for t in range(TILES):
                    for c in range(chunks):
                        ins = pe.matmul(PS[0:TP, 0, t * width:(t + 1) * width], lhs(c, t), w(c),
                                        start=c == 0, stop=c == chunks - 1)
                ins.then_inc(proj_ps, 1)

            def tok(tile, t):
                return tile[:, t * TP:(t + 1) * TP]

            def self_attention(call, q, D):
                last = lin.n
                pe.wait_ge(lin_moved, last)

                def scores(p):
                    for c in range(4):
                        pe.wait_ge(kblk_ready, 16 * call + 4 * p + c + 1)
                        if p >= 1:
                            pe.wait_ge(s_read, 16 * call + 4 * (p - 1) + c + 1)
                        pe.matmul(PS[0:TP, c, 0:4 * TP], q(c, p), Kblk[:, c, :, :].rearrange("p h k -> p (h k)"),
                                  start=True, stop=True).then_inc(s_ps, 1)

                def values(p):
                    if p >= 1:
                        pe.wait_ge(o_sa_ready, TILES * call + p)

                    def transposes(c):
                        if call == 0 and c % 2 == 0:
                            pe.wait_ge(masked, 2 * p + c // 2 + 1)
                        elif call == 1:
                            pe.wait_ge(exp_done, 4 * (TILES + p) + c + 1)
                        if p * 4 + c >= 2:
                            pe.wait_ge(pt_moved, 16 * call + 4 * p + c - 1)
                        for h in range(4):
                            ins = pe.transpose(PS[0:TP, 4 + c % 2, h * TP:(h + 1) * TP], S[p % 3][:, 4 * c + h, :],
                                               ident[0:TP, 0:TP])
                        ins.then_inc(pt_ps, 1)

                    def weigh(c):
                        pe.wait_ge(pt_moved, 16 * call + 4 * p + c + 1)
                        for h in range(4):
                            hh = 4 * c + h
                            ins = pe.matmul(PS[0:TP, 6, hh * D:(hh + 1) * D], PT[:, c % 2, h, :],
                                            VT[:, p, hh * D:(hh + 1) * D], start=True, stop=True)
                        return ins

                    transposes(0)
                    for c in range(4):
                        if c + 1 < 4:
                            transposes(c + 1)
                        ins = weigh(c)
                    ins.then_inc(o_sa_ps, 1)

                def out_t(p):
                    pe.wait_ge(o_sa_ready, p + 1)
                    if p >= 1:
                        pe.wait_ge(oT_moved, p)
                    for c in range(4):
                        ins = pe.transpose(PS[:, 7, c * TP:(c + 1) * TP], OT[:, p % 2, c * 128:(c + 1) * 128],
                                           ident[0:TP, 0:TP])
                    ins.then_inc(oT_ps, 1)

                for p in range(3):
                    scores(p)
                for p in range(TILES):
                    values(p)
                    if p + 3 < TILES:
                        scores(p + 3)
                    if call == 0:
                        out_t(p)

            def mlp(w, idle):
                project(lambda c, t: tok(big1[:, c, :], t), lambda c: w[0][:, c * C:(c + 1) * C], 4)
                to_fm(hat, idle)
                pe.wait_ge(fm_ready, fm.up())
                for c in range(FCH):
                    linear([(w[1][:, c * 128:(c + 1) * 128], xn[:, :])], TOK)
                pe.wait_ge(lin_moved, lin.n)
                project(lambda c, t: tok(big2[:, c, :], t), lambda c: w[2][:, c * C:(c + 1) * C], FCH)

            def queries(wq, nq, loaded, per):
                pe.wait_ge(fm_ready, fm.up())
                for c in range(nq):
                    linear([(wq[:, c * 128:(c + 1) * 128], xn[:, :])], TOK)
                pe.wait_ge(pads_loaded, loaded)
                pe.wait_ge(lin_moved, lin.n)
                for j in range(PAIRS):
                    linear([(wkpad[:, j, :], big1[:, 2 * j // per, :])], TOK)

            def fill(nb, f):
                if f == 0:
                    pe.wait_ge(xx_ready, nb + 1)
                if f == 0 and (not isinstance(nb, int) or nb >= 1):
                    pe.wait_ge(mrow_moved, nb)
                if f == 2:
                    pe.wait_ge(y_ready, SPANS * nb + 1)
                for j in range(SPAN // KP):
                    kt = f * (SPAN // KP) + j
                    ins = pe.transpose(PS[:, f % 2, j * KP:(j + 1) * KP], XX[:, kt, :], ident[0:KP, 0:KP])
                ins.then_inc(xxT_ps, 1)

            def cross(call):
                def first_scores():
                    pe.wait_ge(ka_ready, BATCH * call + 1)
                    pe.wait_ge(qs_ready, 2 * BATCH * call + 1)
                    for r in range(HQ_TILES):
                        if r >= 2:
                            pe.wait_ge(sc_max, (BATCH * call * HQ_TILES + r - 1) * SPANS)
                        for s in range(SPANS):
                            pe.matmul(PS[:, SPANS * (r % 2) + s, 0:SPAN], qA[:, 0, r * 128:(r + 1) * 128],
                                      kA[:, 0, s * SPAN:(s + 1) * SPAN], start=True, stop=True).then_inc(sc_ps, 1)

                def score(nb, par, j):
                    g = nb + BATCH * call
                    if j == 0:
                        pe.wait_ge(ka_ready, g + 1)
                        pe.wait_ge(qs_ready, 2 * g + 1)
                        if call or not isinstance(nb, int) or nb >= 1:
                            pe.wait_ge(mrow_moved, g)
                    if j >= 2:
                        pe.wait_ge(sc_max, g * HQ_TILES * SPANS + j - 1)
                    r, s = j // SPANS, j % SPANS
                    pe.matmul(PS[:, j % 2, 0:SPAN], qA[:, par, r * 128:(r + 1) * 128],
                              kA[:, par, s * SPAN:(s + 1) * SPAN], start=True, stop=True).then_inc(sc_ps, 1)

                def max_rows(nb):
                    g = nb + BATCH * call
                    pe.wait_ge(negm_ready, 4 * g + 4)
                    for j in range(HQ_TILES):
                        ins = pe.matmul(PS[64:66, j // 4, (j % 4) * 128:(j % 4 + 1) * 128], mhl[:, j, :], ident[:, :],
                                        start=True, stop=True)
                    ins.then_inc(mrow_ps, 1)

                def score_t(b, par, kt):
                    g0 = KT * (b + BATCH * call)
                    if call or not isinstance(b, int) or b or kt >= 2:
                        pe.wait_ge(pf_ready, g0 + kt - 1)
                    keys = slice(kt * KP, (kt + 1) * KP)
                    for k, q in ((kA, qA), (kB, qB)):
                        if k is kB and kt == 0:
                            pe.wait_ge(qs_ready, 2 * (b + BATCH * call) + 2)
                            pe.wait_ge(kb_ready, b + BATCH * call + 1)
                            pe.wait_ge(mrow_moved, b + BATCH * call + 1)
                        for j in range(2):
                            ins = pe.matmul(PS[0:KP, 2 + 2 * (kt % 2) + j, 0:HALF], k[:, par, keys],
                                            q[:, par, j * HALF:(j + 1) * HALF], start=k is kA, stop=k is kB)
                    ins.then_inc(st_ps, 1)

                def weigh_high(b, par, kt):
                    g0 = KT * (b + BATCH * call)
                    if kt == 0:
                        pe.wait_ge(v_ready, b + BATCH * call + 1)
                    pe.wait_ge(p_ready, g0 + kt + 1)
                    for j in range(2):
                        if kt == 0 and (call or not isinstance(b, int) or b):
                            pe.wait_ge(o_moved, 2 * (b + BATCH * call) - 1 + j)
                        for i, w in enumerate((Wh, Wl)):
                            ins = pe.matmul(PS[:, 6 + j, 0:HALF], w[:, par, kt, :],
                                            Ph[:, kt % 2, j * HALF:(j + 1) * HALF],
                                            start=kt == 0 and i == 0, stop=False)
                    ins.then_inc(ph_used, 1)

                def weigh_low(b, par, kt):
                    g0 = KT * (b + BATCH * call)
                    wait_low(pe, b, call, kt)
                    for j in range(2):
                        ins = pe.matmul(PS[:, 6 + j, 0:HALF], Wh[:, par, kt, :], Pl[:, kt % 2, j * HALF:(j + 1) * HALF],
                                        start=False, stop=kt == KT - 1)
                    ins.then_inc(pl_used, 1)

                first_job = (0, 0, 0, 0, 3, 6, 9, 12, 15, 18, 21, 21, 21) if call == 0 else \
                            (0, 0, 0, 2, 4, 7, 10, 13, 16, 19, 21, 21, 21)

                def step(b, par, has_next):
                    for kt in range(KT):
                        jobs = range(first_job[kt], first_job[kt + 1]) if has_next else ()
                        if kt + 1 < KT:
                            score_t(b, par, kt + 1)
                        if kt == 0 and (not isinstance(b, int) or b):
                            weigh_low(b - 1, 1 - par, KT - 1)
                        for j in jobs[0:1]:
                            score(b + 1, 1 - par, j)
                        if kt <= 1 and has_next and call == 0:
                            for f in ((0, 1), (2,))[kt]:
                                fill(b + 1, f)
                        if kt == 11 and has_next:
                            max_rows(b + 1)
                        weigh_high(b, par, kt)
                        for j in jobs[1:2]:
                            score(b + 1, 1 - par, j)
                        if kt >= 1:
                            weigh_low(b, par, kt - 1)
                        for j in jobs[2:3]:
                            score(b + 1, 1 - par, j)
                    if has_next:
                        score_t(b + 1, 1 - par, 0)

                if call == 1:
                    pe.wait_ge(v_ready, BATCH + 1)
                pe.wait_ge(lin_moved, lin.n)
                first_scores()
                max_rows(0)
                score_t(0, 0, 0)
                static_and_loop(pe, step, BATCH - 1)
                weigh_low(BATCH - 1, 1, KT - 1)

            def outputs(call, nq, per):
                pe.wait_ge(u_ready, call + 1)
                for c in range(nq):
                    pairs = range(c * per // 2, (c + 1) * per // 2)
                    linear([(wvpad[:, j, :], qp_pairs[:, :, j, :]) for j in pairs], TOK)
                pe.wait_ge(lin_moved, lin.n)

            def moe(call, gate_w):
                h, l = (w[:, :, :].rearrange("p b (j n) -> p b j n", j=2) for w in (wh, wl))

                pe.wait_ge(fm_ready, fm.up())
                project(lambda c, t: tok(xn, t), lambda c: gate_w[:, :], 1, EXPERTS)
                pe.wait_ge(x_split, call + 1)

                def up(e, par):
                    pe.wait_ge(up_split, e + EXPERTS * call + 1)
                    for c in range(FCH):
                        m = e * FCH + c
                        for j in range(2 - call):
                            if not isinstance(m, int) or m >= 2:
                                if j == 0:
                                    pe.wait_ge(g_moved, m - 1 + EXPERTS * FCH * call)
                                else:
                                    pe.wait_ge(mul_done, m - 1)
                            for i, (w, x) in enumerate(((h, xh), (l, xh), (h, xl))):
                                mm = pe.matmul(PS[:, 2 + 4 * j + c % 2, 0:TOK], w[:, par, j, c * 128:(c + 1) * 128], x,
                                               start=i == 0, stop=i == 2)
                            mm.then_inc((g_ps, u_ps)[j], 1)

                def down(e, par):
                    pe.wait_ge(down_loaded[par], (e - par) * 8 + (call * EXPERTS * 8 + 16))
                    if call == 0:
                        pe.wait_ge(mul_done, (e + 1) * FCH)
                    else:
                        pe.wait_ge(g_moved, (e + 1 + EXPERTS) * FCH)
                    if not isinstance(e, int) or e >= 2:
                        pe.wait_ge(dn_added, e + EXPERTS * call + call + 1)
                    for t in range(TILES):
                        for c in range(FCH):
                            mm = pe.matmul(PS[0:TP, 4 + par, t * C:(t + 1) * C], tok(act[:, par, c, :], t),
                                           we[:, par, (2 - call) * 512 + c * C:(2 - call) * 512 + (c + 1) * C],
                                           start=c == 0, stop=c == FCH - 1)
                    mm.then_inc(dn_ps, 1)

                def step(e, par, has_next):
                    up(e, par)
                    if not isinstance(e, int) or e:
                        down(e - 1, 1 - par)
                    if call == 1 and isinstance(e, int) and e == 0:
                        pe.wait_ge(comb_ready, 2)
                        for t in range(TILES):
                            mm = pe.transpose(PS[0:EXPERTS, 7, t * TP:(t + 1) * TP], comb[:, :, t],
                                              ident[0:TP, 0:TP])
                        mm.then_inc(combT_ps, 1)
                        pe.wait_ge(combT_ready, 1)
                        project(lambda c, t: combT[:, t * TP:(t + 1) * TP], lambda c: b2[:, :], 1)

                static_and_loop(pe, step, EXPERTS - 1)
                down(EXPERTS - 1, 1)

            pe.wait_ge(consts_step, CONSTS)
            to_fm(hat, 0)
            pe.wait_ge(fm_ready, fm.up())
            pe.wait_ge(wA_loaded, 6 * 16)
            for c in range(4):
                linear([(w_q1[:, c * 128:(c + 1) * 128], xn[:, :])], TOK)
            for c in range(4):
                linear([(w_k1[:, c * 128:(c + 1) * 128], yn[:, :])], TOK)
            for p in range(TILES):
                linear([(tok(yn, p), w_v1)], 512, TP)
            self_attention(0, lambda c, p: tok(big1[:, c, :], p), 32)
            pe.wait_ge(oT_moved, TILES)
            mlp(w_a1, WARM_MLP[0])
            to_fm(hat, WARM_QUERIES[0])
            pe.wait_ge(lin_moved, lin.n)
            for f in range(SPANS):
                fill(0, f)
            pe.wait_ge(y_ready, SPANS)
            pe.wait_ge(wB_loaded, 8 * 16)
            queries(wq2, 4, 8 * 16, 4)
            cross(0)
            outputs(0, 4, 4)
            mlp(w_a2, WARM_MLP[1])
            to_fm(hat, WARM_MOE[0])
            pe.wait_ge(fm_ready, fm.up())
            project(lambda c, t: tok(xn, t), lambda c: attn_w[:, :], 1)
            to_fm(hat, WARM_MOE[1])
            moe(0, gate0)
            to_fm(hat, WARM_QUERIES[1])
            pe.wait_ge(wL1_loaded, 5 * 16)
            queries(w_qL1, 8, 12 * 16, 2)
            cross(1)
            outputs(1, 8, 2)
            project(lambda c, t: tok(big1[:, c, :], t), lambda c: w_oL1[:, c, :], 8)
            to_fm(ta, WARM_L1[0])
            pe.wait_ge(fm_ready, fm.up())
            linear([(w_qkvL1[:, 0, :], xn[:, :])], TOK)
            linear([(w_qkvL1[:, 1, :], xn[:, :])], TOK)
            linear([(tok(xn, p), w_qkvL1[:, 2, :]) for p in range(TILES)], C, TP, offs=True)
            self_attention(1, lambda c, p: tok(big1[:, 0, :], p), 8)
            to_fm(tb, WARM_L1[1])
            moe(1, gate1)


def kernel(**inputs):
    import numpy as np
    import concourse.bacc as bacc
    from concourse.bass_utils import run_bass_kernel_spmd

    a = {k: np.asarray(v) for k, v in inputs.items()}
    L0, F0, X1, F1 = "L0_xattn_", "L0_ffn_", "L1_xattn_", "L1_ffn_"
    heads_side = lambda w: w.transpose(1, 0, 2).reshape(w.shape[1], -1)
    chunk_cols = lambda v: v.reshape(-1, 128).T
    both = lambda v: np.concatenate([v, v]) if v.shape[0] == CTX else v
    ctx = a["ctx_512"]
    arrays = {
        "x": a["x"].reshape(TOK, C),
        "ctx": ctx,
        "ctxT": ctx.reshape(BATCH, KP, KT, CTX).transpose(0, 3, 2, 1).reshape(BATCH, CTX, KEYS),
        "rows": np.stack([a[n] for n in ROWS]),
        "cols": np.concatenate([np.stack([both(a[n]) for n in COLS], axis=1),
                                chunk_cols(a[L0 + "a1_li2_b"]), chunk_cols(a[L0 + "a2_li2_b"]),
                                chunk_cols(a[F1 + "b1"])], axis=1),
        "a1_wq": heads_side(a[L0 + "a1_wq"]), "a1_wk": heads_side(a[L0 + "a1_wk"]),
        "a1_wv": heads_side(a[L0 + "a1_wv"]),
        "a1_li1": a[L0 + "a1_li1_w"], "a1_li2": a[L0 + "a1_li2_w"], "a1_li3": a[L0 + "a1_li3_w"],
        "a2_wq": heads_side(a[L0 + "a2_wq"]),
        "a2_wk": a[L0 + "a2_wk"].transpose(0, 2, 1), "a2_wv": a[L0 + "a2_wv"],
        "a2_li1": a[L0 + "a2_li1_w"], "a2_li2": a[L0 + "a2_li2_w"], "a2_li3": a[L0 + "a2_li3_w"],
        "attn_w": a[F0 + "attn_w"].T, "gate0": a[F0 + "gate_w"].T,
        "gp": a[F0 + "gate_proj"].transpose(0, 2, 1), "up": a[F0 + "up_proj"].transpose(0, 2, 1),
        "dp": a[F0 + "down_proj"].transpose(0, 2, 1).reshape(EXPERTS, FCH, 128, C).transpose(0, 2, 1, 3)
        .reshape(EXPERTS, 128, FF),
        "L1_Wq": a[X1 + "Wq"], "L1_Wo": a[X1 + "Wo"],
        "L1_Wk": a[X1 + "Wk"].T.reshape(HEADS, 64, CTX),
        "L1_Wv": a[X1 + "Wv"].reshape(CTX, HEADS, 64).transpose(1, 0, 2),
        "L1f_Wq": heads_side(a[F1 + "Wq"]), "L1f_Wk": heads_side(a[F1 + "Wk"]), "L1f_Wv": heads_side(a[F1 + "Wv"]),
        "gate1": a[F1 + "gate_W"], "W1": a[F1 + "W1"], "b2": a[F1 + "b2"],
        "W2": a[F1 + "W2"].reshape(EXPERTS, FCH, 128, C).transpose(0, 2, 1, 3).reshape(EXPERTS, 128, FF),
    }
    arrays = {k: np.ascontiguousarray(v) for k, v in arrays.items()}

    nc = bacc.Bacc("TRN2", target_bir_lowering=False, num_devices=1)
    f32 = mybir.dt.float32
    d = {k: nc.dram_tensor("in_" + k, v.shape, f32, kind="ExternalInput").ap() for k, v in arrays.items()}
    out = nc.dram_tensor("out", (TOK, C), f32, kind="ExternalOutput").ap()
    build_program(nc, d, out)
    r = run_bass_kernel_spmd(nc, [{"in_" + k: v for k, v in arrays.items()}], core_ids=[0])
    return r.results[0]["out"].reshape(BATCH, SEQ, C)
```
